# Optimizing a Trainium2 kernel written in Bass

```python
import numpy as np
import jax
import jax.numpy as jnp

def _softmax(x, axis=-1):
    return jax.nn.softmax(x, axis=axis)

def _gelu(x):
    return jax.nn.gelu(x, approximate=True)

def _silu(x):
    return jax.nn.silu(x)

def _sigmoid(x):
    return jax.nn.sigmoid(x)

def _layernorm(x, axis=-1, eps=1e-05):
    m = jnp.mean(x, axis=axis, keepdims=True)
    v = jnp.var(x, axis=axis, keepdims=True)
    return (x - m) / jnp.sqrt(v + eps)

def _scatter_add(tgt, idx, src, axis=0):
    return tgt.at[idx].add(src)

def _segment_sum(src, seg, n):
    return jax.ops.segment_sum(src, seg, n)
kernel_name = 'mk_gnn_preln_d2_gnn_r8_8e4a7e'

def setup_inputs(seed: int=0):
    np.random.seed(seed)
    _w = jnp.asarray

    def _rec_inputs():
        import jax
        import jax.numpy as jnp
        _gk = jax.random.key(seed)
        x = -0.0002117 + 1 * jax.random.normal(jax.random.fold_in(_gk, 1), (3125, 1024), jnp.float32)
        src = jax.random.randint(jax.random.fold_in(_gk, 2), (50000,), 0, 3125, jnp.int32)
        dst = jax.random.randint(jax.random.fold_in(_gk, 3), (50000,), 0, 3125, jnp.int32)
        _o = jnp.argsort(dst, stable=True)
        src = src[_o]
        dst = dst[_o]
        return (x, src, dst)
    x, src, dst = _rec_inputs()

    def _L0_gnn_setup():
        import jax, jax.numpy as jnp
        import numpy as np
        N = 3125
        E = 50000
        H = 4
        C = 256
        D_IN = 1024
        NEG_SLOPE = 0.2
        key = jax.random.key(seed)
        k1, k2, k3, k4, k5, k6 = jax.random.split(key, 6)
        x = jax.random.normal(k1, (N, D_IN), dtype=jnp.float32)
        edge_index = jax.random.randint(k2, (2, E), 0, N, dtype=jnp.int64)
        scale = 1.0 / np.sqrt(D_IN)
        W = jax.random.normal(k3, (D_IN, H * C), dtype=jnp.float32) * scale
        att_src = jax.random.normal(k4, (H, C), dtype=jnp.float32) * 0.1
        att_dst = jax.random.normal(k5, (H, C), dtype=jnp.float32) * 0.1
        bias = jax.random.normal(k6, (H * C,), dtype=jnp.float32) * 0.01
        return {'x': x, 'edge_index': edge_index, 'W': W, 'att_src': att_src, 'att_dst': att_dst, 'bias': bias}
    _L0_gnn_all = _L0_gnn_setup()
    _L0_gnn_in = {k: v for k, v in _L0_gnn_all.items() if k in ('W', 'att_src', 'att_dst', 'bias')}
    del _L0_gnn_all

    def _L1_gnn_setup():
        import jax, jax.numpy as jnp
        import numpy as np
        NEG_SLOPE = 0.1
        EPS = 1e-05
        key = jax.random.key(seed)
        k1, k2, k3, k4, k5 = jax.random.split(key, 5)
        N, E, DIN, DOUT = (1250, 20000, 1024, 1024)
        x = jax.random.normal(k1, (N, DIN), dtype=jnp.float32)
        W = jax.random.normal(k2, (DIN, DOUT), dtype=jnp.float32) * 0.02
        a = jax.random.normal(k3, (1, 2 * DOUT), dtype=jnp.float32) * 0.02
        src = jax.random.randint(k4, (E,), 0, N, dtype=jnp.int64)
        dst = jax.random.randint(k5, (E,), 0, N, dtype=jnp.int64)
        return {'x': x, 'W': W, 'a': a, 'src': src, 'dst': dst}
    _L1_gnn_all = _L1_gnn_setup()
    _L1_gnn_in = {k: v for k, v in _L1_gnn_all.items() if k in ('W', 'a')}
    del _L1_gnn_all
    return {'x': x, 'src': src, 'dst': dst, 'L0_gnn_W': _L0_gnn_in['W'], 'L0_gnn_att_src': _L0_gnn_in['att_src'], 'L0_gnn_att_dst': _L0_gnn_in['att_dst'], 'L0_gnn_bias': _L0_gnn_in['bias'], 'L1_gnn_W': _L1_gnn_in['W'], 'L1_gnn_a': _L1_gnn_in['a']}

def reference(x, src, dst, L0_gnn_W, L0_gnn_att_src, L0_gnn_att_dst, L0_gnn_bias, L1_gnn_W, L1_gnn_a):
    import jax
    import jax.numpy as jnp

    def _L0_gnn_ref(x, edge_index, W, att_src, att_dst, bias):
        import jax, jax.numpy as jnp
        import numpy as np
        N = 3125
        E = 50000
        H = 4
        C = 256
        D_IN = 1024
        NEG_SLOPE = 0.2
        xp = (x @ W).reshape(N, H, C)
        a_src = jnp.einsum('nhc,hc->nh', xp, att_src)
        a_dst = jnp.einsum('nhc,hc->nh', xp, att_dst)
        loops = jnp.arange(N, dtype=edge_index.dtype)
        src = jnp.concatenate([edge_index[0], loops])
        dst = jnp.concatenate([edge_index[1], loops])
        e = jax.nn.leaky_relu(a_src[src] + a_dst[dst], NEG_SLOPE)
        m = jax.ops.segment_max(e, dst, num_segments=N)
        ee = jnp.exp(e - m[dst])
        z = jax.ops.segment_sum(ee, dst, num_segments=N)
        alpha = ee / z[dst]
        msgs = xp[src] * alpha[:, :, None]
        out = jax.ops.segment_sum(msgs, dst, num_segments=N)
        out = out.reshape(N, H * C) + bias
        return jax.nn.relu(out)

    def _L1_gnn_ref(x, W, a, src, dst):
        import jax, jax.numpy as jnp
        import numpy as np
        NEG_SLOPE = 0.1
        EPS = 1e-05
        N = x.shape[0]
        d = W.shape[1]
        h = x @ W
        a_l, a_r = (a[0, :d], a[0, d:])
        al = h @ a_l
        ar = h @ a_r
        e = jnp.exp(-jax.nn.leaky_relu(al[src] + ar[dst], negative_slope=NEG_SLOPE))
        rowsum = jax.ops.segment_sum(e, src, num_segments=N)
        h_prime = jax.ops.segment_sum(e[:, None] * h[dst], src, num_segments=N)
        h_prime = h_prime / (rowsum[:, None] + EPS)
        return jax.nn.elu(h_prime)
    edge_index = jnp.stack([src, dst])
    h = jnp.maximum(_layernorm(x, axis=-1), 0.0)
    x = x + _L0_gnn_ref(h, edge_index, L0_gnn_W, L0_gnn_att_src, L0_gnn_att_dst, L0_gnn_bias)
    h = jnp.maximum(_layernorm(x, axis=-1), 0.0)
    x = x + _L1_gnn_ref(h, L1_gnn_W, L1_gnn_a, src, dst)
    return x

_drawn_inputs = setup_inputs


def setup_inputs(seed=0):
    import zlib

    import numpy as np

    out = dict(_drawn_inputs(seed))
    spreads = {}
    factors = {'L0_gnn_bias': 7.729, 'L1_gnn_a': 4.539}
    for name, (base, spread) in spreads.items():
        noise = np.random.default_rng([zlib.crc32(name.encode()), seed]).standard_normal(out[name].shape)
        drawn = base * np.exp(spread * noise) if base else spread * noise
        out[name] = jnp.asarray(drawn.astype(out[name].dtype))
    for name, factor in factors.items():
        out[name] = (out[name] * factor).astype(out[name].dtype)
    return out
```

```python
from contextlib import ExitStack

import concourse.bass as bass
from concourse import mybir

F32 = mybir.dt.float32
BF16 = mybir.dt.bfloat16
F16 = mybir.dt.float16
U32 = mybir.dt.uint32
I32 = mybir.dt.int32
ALU = mybir.AluOpType
ACT = mybir.ActivationFunctionType
AX_X = mybir.AxisListType.X

P = 128
N = 3125
D = 1024
H = 4
C = D // H
E = 50000
SLOPE0 = 0.2
SLOPE1 = 0.1
LN_EPS = 1e-5
SUM_EPS = 1e-5
NEG = -1.0e30

TILES = -(-N // P)
NP = TILES * P
TAIL = N - (TILES - 1) * P
KC = D // P
HALF = 512
CX = C + 1

GT = 5
G = TILES // GT
GW = GT * P

EP = 125
ER = E // EP
HALO = 49
EX = HALO + ER + HALO
OOB = float(1 << 25)
EB = 20
EARLY = 4
CMP = (HALO - 1) // (2 * EARLY)

assert TILES == G * GT and EP * ER == E and ER % (2 * EB) == 0 and CMP * 2 * EARLY == HALO - 1 and CMP % 2 == 0


def rows(table, tile, size=P):
    return table[bass.ds(tile * P, size), :]


def hold(eng, passed, sem, value):
    eng.wait_ge(sem, value)
    eng.sem_inc(passed, 1)


def build(nc, x, src, dst, w0, att_src, att_dst, bias, w1, a1, out):
    counts = nc.dram_tensor("counts", [NP * NP, 1], F32, kind="Internal").ap()
    table = nc.dram_tensor("edge_table", [NP * NP, 1], F32, kind="Internal").ap()
    table2 = table.rearrange("(d s) o -> d (s o)", s=NP)
    arow_d = nc.dram_tensor("a_src_rows", [H * TILES, P], F32, kind="Internal").ap()
    trow_d = nc.dram_tensor("dst_term_rows", [G * 2 * H * GT, P], F32, kind="Internal").ap()
    agg_d = nc.dram_tensor("attention_sums", [H, NP, CX], F32, kind="Internal").ap()
    x1_d = nc.dram_tensor("x1", [NP, D], F32, kind="Internal").ap()
    alrow_d = nc.dram_tensor("al_rows", [TILES, P], F32, kind="Internal").ap()
    ctx = ExitStack()
    with ctx:
        ident = ctx.enter_context(nc.sbuf_tensor("ident", [P, P], F32))
        crowded = ctx.enter_context(nc.sbuf_tensor("crowded", [P, 1], I32))
        with ExitStack() as both:
            xp = both.enter_context(nc.sbuf_tensor("xp", [P, TILES, H, CX], F32))
            a_src = both.enter_context(nc.sbuf_tensor("a_src", [P, TILES * H], F32))
            a_dst = both.enter_context(nc.sbuf_tensor("a_dst", [P, TILES * H], F32))
            with ExitStack() as edges:
                key = edges.enter_context(nc.sbuf_tensor("key", [P, EX], F32))
                phase1(nc, x, src, dst, w0, att_src, att_dst, table, table2, arow_d,
                       ident, xp, a_src, a_dst, key, crowded)
                any_edges(nc, table, counts, ident, key, crowded)
            phase2(nc, table2, arow_d, trow_d, agg_d, ident, xp, a_src, a_dst)
        with ExitStack() as both:
            h2 = both.enter_context(nc.sbuf_tensor("h2", [P, TILES * D], F32))
            al = both.enter_context(nc.sbuf_tensor("al", [P, TILES], F32))
            ar = both.enter_context(nc.sbuf_tensor("ar", [P, TILES], F32))
            phase3(nc, x, bias, w1, a1, agg_d, x1_d, alrow_d, ident, h2, al, ar)
            phase4(nc, table2, alrow_d, x1_d, ident, h2, ar, out)


def phase1(nc, x, src, dst, w0, att_src, att_dst, table, table2, arow_d,
           ident, xp, a_src, a_dst, key, crowded):
    ctx = ExitStack()
    with ctx:
        def sb(name, shape, dt=F32):
            return ctx.enter_context(nc.sbuf_tensor(name, shape, dt))

        def sem(name):
            return ctx.enter_context(nc.semaphore(name))

        w_sb = sb("w0_sb", [P, KC, D])
        att_bc = sb("att_bc", [P, 2, D])
        xt = [sb(f"xt{k}", [P, D]) for k in range(2)]
        ht = [sb(f"ht{k}", [P, D]) for k in range(2)]
        hT = [sb(f"hT{k}", [P, KC, P]) for k in range(2)]
        stats = sb("stats", [P, 2, 6])
        mv = sb("mv", [P, 2])
        std = sb("std", [P, 1])
        rstd = sb("rstd", [P, 1])
        nbias = sb("nbias", [P, 1])
        prod = sb("prod", [P, C])
        asd = [sb(f"asd{k}", [P, 2, H]) for k in range(2)]
        a_hm = sb("a_hm", [P, H * TILES])
        a_rows = sb("a_rows", [H * TILES, P])
        neg = sb("neg", [P, 1, GW])
        e_src = sb("e_src", [P, EX], I32)
        e_dst = sb("e_dst", [P, EX], I32)
        equal = [sb(f"equal{k}", [P, HALO + ER], BF16) for k in range(2)]
        later = sb("later", [P, ER], BF16)
        before = sb("before", [P, ER], BF16)
        back = sb("back", [P, 2, ER])
        bad = sb("bad", [P, 1])
        bad_all = sb("bad_all", [P, 1])
        lnc = sb("lnc", [P, ER])
        skip = sb("skip", [P, ER])
        idx = sb("idx", [P, ER], U32)
        idx_st = [sb(f"idx_st{k}", [P, EB], U32) for k in range(2)]
        lnc_st = [sb(f"lnc_st{k}", [P, EB]) for k in range(2)]
        eps = sb("eps", [P, 1])

        tp = ctx.enter_context(nc.psum_tensor("tp", [P, KC * P], F32))
        mm = [ctx.enter_context(nc.psum_tensor(f"mm{k}", [P, D], F32)) for k in range(2)]

        edges_in = sem("edges_in")
        weights_in = sem("weights_in")
        x_in = [sem(f"x_in{k}") for k in range(2)]
        neg_set = sem("neg_set")
        ones_set = sem("ones_set")
        table_clear = sem("table_clear")
        consts = sem("consts")
        stats_done = sem("stats_done")
        aggr_done = sem("aggr_done")
        std_done = sem("std_done")
        rstd_done = sem("rstd_done")
        norm_done = sem("norm_done")
        h_done = sem("h_done")
        h_used = sem("h_used")
        hT_done = sem("hT_done")
        mm_done = sem("mm_done")
        xp_copied = sem("xp_copied")
        scored = sem("scored")
        scores_kept = sem("scores_kept")
        a_hm_done = sem("a_hm_done")
        a_T_done = sem("a_T_done")
        a_rows_done = sem("a_rows_done")
        a_rows_out = sem("a_rows_out")
        pads_set = sem("pads_set")
        key_done = sem("key_done")
        compared = sem("compared")
        tallied = sem("tallied")
        edge_math = sem("edge_math")
        bad_set = sem("bad_set")
        bad_done = sem("bad_done")
        bad_summed = sem("bad_summed")
        ln_in = sem("ln_in")
        ln_done = sem("ln_done")
        idx_done = sem("idx_done")
        staged = sem("staged")
        lnc_out = [sem(f"lnc_out{k}") for k in range(2)]
        passed = sem("passed_phase1")
        block = ctx.enter_context(nc.Block())

        @block.sync
        def _(sp):
            sp.sem_inc(h_done, 2)
            sp.wait_ge(pads_set, 2)
            for e_sb, e_in in ((e_dst, dst), (e_src, src)):
                near = e_in.rearrange("(p t) -> p t", t=ER)
                sp.dma_start(e_sb[0:EP, HALO:HALO + ER], near).then_inc(edges_in, 16)
                sp.dma_start(e_sb[1:EP, 0:HALO], near[0:EP - 1, ER - HALO:ER]).then_inc(edges_in, 16)
                sp.dma_start(e_sb[0:EP - 1, HALO + ER:EX], near[1:EP, 0:HALO]).then_inc(edges_in, 16)
            sp.dma_start(w_sb[:, :, :], w0.rearrange("(k p) n -> p k n", p=P)).then_inc(weights_in, 16)
            for k, att in enumerate((att_src, att_dst)):
                sp.dma_start(att_bc[:, k, :],
                             att.rearrange("h c -> (h c)").rearrange("(o n) -> o n", o=1).to_broadcast([P, D]))\
                    .then_inc(weights_in, 16)
            def load(i, k, size=P):
                hold(sp, passed, h_done, i + 1)
                sp.dma_start(xt[k][0:size, :], rows(x, i, size)).then_inc(x_in[k], 16)

            with sp.Fori(0, TILES // 2) as r:
                i = r * 2
                for k in range(2):
                    load(i + k, k)
            load(TILES - 1, 0, TAIL)
            sp.wait_ge(a_rows_done, 1)
            sp.dma_start(arow_d, a_rows[:, :]).then_inc(a_rows_out, 16)
            sp.wait_ge(a_rows_out, 16)

        @block.gpsimd
        def _(pool):
            pool.memset(neg[:, :, :], NEG).then_inc(neg_set, 1)
            pool.memset(ident[:, :], 0.0).then_inc(consts, 1)
            pool.wait_ge(consts, 1)
            pool.affine_select(out=ident[:, :], in_=ident[:, :], compare_op=ALU.not_equal, fill=1.0,
                               base=0, pattern=[[-1, P]], channel_multiplier=1).then_inc(consts, 1)
            pool.wait_ge(bad_done, 1)
            pool.partition_all_reduce(bad_all[:, :], bad[:, :], P, bass.bass_isa.ReduceOp.add)\
                .then_inc(bad_summed, 1)

            pool.wait_ge(table_clear, 16 * TILES)
            pool.wait_ge(idx_done, 1)
            pool.wait_ge(ln_done, 2)

            def write_counts(b, k):
                cols = bass.ds(b * EB, EB)
                pool.tensor_copy(idx_st[k][:, :], idx[:, cols]).then_inc(staged, 1)
                pool.tensor_copy(lnc_st[k][:, :], lnc[:, cols]).then_inc(staged, 1)
                hold(pool, passed, staged, 2 * b + 2)
                for j in range(EB):
                    pool.indirect_dma_start(
                        out=table, out_offset=bass.IndirectOffsetOnAxis(ap=idx_st[k][:, j:j + 1], axis=0),
                        in_=lnc_st[k][:, j:j + 1], in_offset=None,
                        bounds_check=NP * NP - 1, oob_is_err=False).then_inc(lnc_out[k], 16)

            blocks = ER // EB
            for k in range(2):
                write_counts(k, k)
            with pool.Fori(1, blocks // 2) as r:
                b = r * 2
                for k in range(2):
                    hold(pool, passed, lnc_out[k], b * (8 * EB))
                    write_counts(b + k, k)
            for k in range(2):
                pool.wait_ge(lnc_out[k], ER * 8)

        @block.scalar
        def _(act):
            def normalise(i, k):
                act.wait_ge(aggr_done, i + 1)
                act.activation(std[:, :], mv[:, 1:2], ACT.Sqrt, bias=eps[:, :]).then_inc(std_done, 1)
                act.wait_ge(norm_done, i + 1)
                act.wait_ge(h_used, i + 1)
                act.activation(ht[k][:, :], xt[k][:, :], ACT.Relu, bias=nbias[:, :], scale=rstd[:, :])\
                    .then_inc(h_done, 1)

            def keep_transposed(i, k):
                act.wait_ge(h_used, i + 3)
                act.wait_ge(mm_done, i + 1)
                act.activation(hT[k][:, :, :].rearrange("p k n -> p (k n)"), tp[:, :], ACT.Copy)\
                    .then_inc(hT_done, 1)

            def keep_xp(i, k):
                act.wait_ge(scores_kept, 2 * i + 2)
                act.activation(xp[:, i, :, 0:C], mm[k][:, :].rearrange("p (h c) -> p h c", h=H), ACT.Copy)\
                    .then_inc(xp_copied, 1)

            act.sem_inc(h_used, 2)
            act.sem_inc(mm_done, 2)
            act.wait_ge(neg_set, 1)
            with act.Fori(0, TILES) as i:
                act.dma_start(rows(table2, i).rearrange("p (g w) -> p g w", w=GW),
                              neg[:, :, :].to_broadcast([P, G, GW])).then_inc(table_clear, 16)
            act.wait_ge(ones_set, 2)
            normalise(0, 0)
            normalise(1, 1)
            keep_transposed(0, 0)

            def pair(i):
                for k in range(2):
                    keep_transposed(i + k + 1, 1 - k)
                    normalise(i + k + 2, k)
                    keep_xp(i + k, k)

            with act.Fori(0, EARLY) as r:
                pair(r * 2)
            act.wait_ge(ln_in, 1)
            act.activation(lnc[:, :], lnc[:, :], ACT.Ln).then_inc(ln_done, 1)
            with act.Fori(EARLY, TILES // 2 - 1) as r:
                pair(r * 2)
            keep_transposed(TILES - 2, 1)
            normalise(TILES - 1, 0)
            keep_xp(TILES - 3, 0)
            keep_transposed(TILES - 1, 0)
            keep_xp(TILES - 2, 1)
            keep_xp(TILES - 1, 0)
            act.wait_ge(a_T_done, 1)
            act.activation(a_rows[:, :], tp[0:H * TILES, 0:P], ACT.Copy).then_inc(a_rows_done, 1)

        @block.vector
        def _(dve):
            dve.memset(e_dst[:, :], -1).then_inc(pads_set, 1)
            dve.memset(e_src[:, :], -1).then_inc(pads_set, 1)
            dve.memset(later[:, :], 0.0).then_inc(tallied, 1)
            dve.memset(before[:, :], 0.0).then_inc(tallied, 1)
            dve.memset(xp[:, :, :, C:CX], 1.0).then_inc(ones_set, 1)
            dve.memset(eps[:, :], LN_EPS).then_inc(ones_set, 1)
            def statistics(i, k, rounds):
                dve.wait_ge(x_in[k], rounds * 16)
                for j in range(2):
                    dve.bn_stats(stats[:, j, :], xt[k][:, j * HALF:(j + 1) * HALF]).then_inc(stats_done, 1)
                hold(dve, passed, stats_done, 2 * i + 2)
                dve.bn_aggr(mv[:, :], stats[:, :, :].rearrange("p a b -> p (a b)")).then_inc(aggr_done, 1)
                dve.wait_ge(std_done, i + 1)
                dve.reciprocal(rstd[:, :], std[:, :]).then_inc(rstd_done, 1)
                dve.wait_ge(rstd_done, i + 1)
                dve.scalar_tensor_tensor(out=nbias[:, :], in0=mv[:, 0:1], scalar=-1.0, in1=rstd[:, :],
                                         op0=ALU.mult, op1=ALU.mult).then_inc(norm_done, 1)
                dve.wait_ge(h_done, i + 3)

            def score(i, k):
                dve.wait_ge(mm_done, i + 3)
                for h in range(H):
                    for j in range(2):
                        dve.tensor_tensor_reduce(out=prod[:, :], in0=mm[k][:, h * C:(h + 1) * C],
                                                 in1=att_bc[:, j, h * C:(h + 1) * C], scale=1.0, scalar=0.0,
                                                 op0=ALU.mult, op1=ALU.add, accum_out=asd[k][:, j, h:h + 1])\
                            .then_inc(scored, 1)
                        dve.wait_ge(scored, i * (2 * H) + 2 * h + j + 1)
                dve.tensor_copy(a_src[:, bass.ds(i * H, H)], asd[k][:, 0, :]).then_inc(scores_kept, 1)
                dve.tensor_copy(a_dst[:, bass.ds(i * H, H)], asd[k][:, 1, :]).then_inc(scores_kept, 1)

            mine = slice(HALO, HALO + ER)

            def compare(k, slot):
                dve.tensor_tensor(equal[slot][:, :], key[:, 0:HALO + ER], key[:, bass.ds(k, HALO + ER)],
                                  ALU.is_equal).then_inc(compared, 1)

            def tally(k, slot):
                dve.wait_ge(compared, k)
                dve.wait_ge(tallied, k * 2)
                dve.tensor_tensor(later[:, :], later[:, :], equal[slot][:, mine], ALU.add).then_inc(tallied, 1)
                dve.tensor_tensor(before[:, :], before[:, :], equal[slot][:, bass.ds(k * -1 + HALO, ER)],
                                  ALU.add).then_inc(tallied, 1)

            def some_comparisons(k):
                for j in range(CMP):
                    dve.wait_ge(tallied, (k + j) * 2)
                    compare(k + j + 1, 1 - j % 2)
                    tally(k + j, j % 2)

            def index_edges():
                dve.tensor_tensor(back[:, 0, :], e_dst[:, mine], e_dst[:, HALO - 1:HALO + ER - 1],
                                  ALU.subtract).then_inc(edge_math, 1)
                dve.tensor_tensor(back[:, 1, :], e_dst[:, mine], e_dst[:, 0:ER],
                                  ALU.subtract).then_inc(edge_math, 1)
                dve.wait_ge(edge_math, 2)
                dve.tensor_scalar(back[:, 0, :], back[:, 0, :], 0.0, None, ALU.is_lt).then_inc(edge_math, 1)
                dve.tensor_scalar(back[:, 1, :], back[:, 1, :], 1.0, None, ALU.is_lt).then_inc(edge_math, 1)
                dve.wait_ge(edge_math, 4)
                dve.tensor_reduce(bad[0:EP, :], back[0:EP, :, :].rearrange("p a b -> p (a b)"), AX_X, ALU.max)\
                    .then_inc(bad_done, 1)
                dve.wait_ge(bad_done, 1)
                dve.wait_ge(tallied, 2 * HALO)
                dve.tensor_scalar(lnc[:, :], later[:, :], 1.0, None, ALU.add).then_inc(ln_in, 1)
                dve.tensor_scalar(back[:, 0, :], key[:, mine], 0.0, None, ALU.is_lt).then_inc(edge_math, 1)
                dve.wait_ge(edge_math, 5)
                dve.tensor_tensor(back[:, 0, :], back[:, 0, :], before[:, :], ALU.add).then_inc(edge_math, 1)
                dve.wait_ge(bad_summed, 1)
                dve.wait_ge(edge_math, 6)
                dve.tensor_scalar(back[:, 0, :], back[:, 0, :], bad_all[:, :], None, ALU.add)\
                    .then_inc(edge_math, 1)
                dve.tensor_copy(crowded[:, :], bad_all[:, :]).then_inc(edge_math, 1)
                dve.wait_ge(edge_math, 8)
                dve.tensor_scalar(skip[:, :], back[:, 0, :], 0.0, OOB, ALU.is_gt, ALU.mult)\
                    .then_inc(edge_math, 1)
                dve.wait_ge(edge_math, 9)
                dve.tensor_tensor(idx[:, :], skip[:, :], key[:, mine], ALU.add).then_inc(idx_done, 1)
                dve.wait_ge(ln_done, 1)
                dve.scalar_tensor_tensor(out=lnc[:, :], in0=later[:, :], scalar=0.5, in1=lnc[:, :],
                                         op0=ALU.is_gt, op1=ALU.mult).then_inc(ln_done, 1)

            dve.memset(bad[:, :], 0.0).then_inc(bad_set, 1)
            dve.wait_ge(bad_set, 1)
            dve.wait_ge(weights_in, 48)
            statistics(0, 0, 1)
            statistics(1, 1, 1)
            dve.wait_ge(edges_in, 96)
            dve.scalar_tensor_tensor(out=key[:, :], in0=e_dst[:, :], scalar=float(NP), in1=e_src[:, :],
                                     op0=ALU.mult, op1=ALU.add).then_inc(key_done, 1)
            dve.wait_ge(key_done, 1)
            compare(1, 0)
            with dve.Fori(0, EARLY) as r:
                for k in range(2):
                    statistics(r * 2 + k + 2, k, r + 2)
                    some_comparisons((r * 2 + k) * CMP + 1)
                    score(r * 2 + k, k)
            index_edges()
            with dve.Fori(EARLY, TILES // 2 - 1) as r:
                for k in range(2):
                    statistics(r * 2 + k + 2, k, r + 2)
                    score(r * 2 + k, k)
            statistics(TILES - 1, 0, TILES // 2 + 1)
            score(TILES - 3, 0)
            score(TILES - 2, 1)
            score(TILES - 1, 0)
            dve.wait_ge(scores_kept, 2 * TILES)
            dve.tensor_copy(a_hm[:, :].rearrange("p (h t) -> p h t", h=H),
                            a_src[:, :].rearrange("p (t h) -> p h t", h=H)).then_inc(a_hm_done, 1)

        @block.tensor
        def _(pe):
            def transpose_h(i, k):
                pe.wait_ge(h_done, i + 3)
                pe.wait_ge(hT_done, i)
                for c in range(KC):
                    last = pe.transpose(tp[:, c * P:(c + 1) * P], ht[k][:, c * P:(c + 1) * P], ident[:, :])
                last.then_inc(h_used, 1)

            def project(i, k):
                pe.wait_ge(hT_done, i + 1)
                pe.wait_ge(xp_copied, i + 1)
                for c in range(KC):
                    for f in range(2):
                        last = pe.matmul(mm[k][:, f * HALF:(f + 1) * HALF], hT[k][:, c, :],
                                         w_sb[:, c, f * HALF:(f + 1) * HALF], start=c == 0, stop=c == KC - 1)
                last.then_inc(mm_done, 1)

            pe.sem_inc(xp_copied, 2)
            pe.wait_ge(consts, 2)
            pe.wait_ge(weights_in, 48)
            transpose_h(0, 0)
            with pe.Fori(0, TILES // 2) as r:
                i = r * 2
                for k in range(2):
                    transpose_h(i + k + 1, 1 - k)
                    project(i + k, k)
            project(TILES - 1, 0)
            pe.wait_ge(a_hm_done, 1)
            pe.wait_ge(hT_done, TILES)
            pe.transpose(tp[0:H * TILES, 0:P], a_hm[:, :], ident[:, :]).then_inc(a_T_done, 1)


def any_edges(nc, table, counts, ident, key, crowded):
    with ExitStack() as ctx:
        flag = nc.values_load(crowded[0:1, 0:1], min_val=0, max_val=P)
        ctx.enter_context(nc.If(flag > 0))
        ctx.enter_context(ExitStack())

        def sb(name, shape, dt=F32):
            return ctx.enter_context(nc.sbuf_tensor(name, shape, dt))

        def sem(name):
            return ctx.enter_context(nc.semaphore(name))

        zeros = sb("zeros", [P, NP])
        below = sb("below", [P, P])
        col = sb("col", [P, 1])
        spread = sb("spread", [P, P])
        same = sb("same", [P, P])
        same_low = sb("same_low", [P, P])
        times = sb("times", [P, 1])
        first = sb("first", [P, 1])
        skip1 = sb("skip1", [P, 1])
        idx1 = sb("idx1", [P, 1], U32)
        seen = sb("seen", [P, 1])
        ln_seen = sb("ln_seen", [P, 1])
        turned = ctx.enter_context(nc.psum_tensor("turned", [P, P], F32))
        set_up = sem("set_up")
        zeroed = sem("zeroed")
        col_math = sem("col_math")
        turned_done = sem("turned_done")
        idx_ready = sem("idx_ready")
        seen_clear = sem("seen_clear")
        seen_in = sem("seen_in")
        seen_done = sem("seen_done")
        ln_seen_done = sem("ln_seen_done")
        written = sem("written")
        col_written = sem("col_written")
        passed = sem("passed_any_edges")
        block = ctx.enter_context(nc.Block())

        @block.sync
        def _(sp):
            sp.wait_ge(set_up, 1)
            with sp.Fori(0, TILES) as i:
                sp.dma_start(rows(counts.rearrange("(d s) o -> d (s o)", s=NP), i), zeros[:, :])\
                    .then_inc(zeroed, 16)

        @block.gpsimd
        def _(pool):
            pool.memset(zeros[:, :], 0.0).then_inc(set_up, 1)
            pool.memset(below[:, :], 1.0).then_inc(set_up, 1)
            pool.wait_ge(set_up, 2)
            pool.affine_select(out=below[:, :], in_=below[:, :], compare_op=ALU.is_gt, fill=0.0,
                               base=0, pattern=[[-1, P]], channel_multiplier=1).then_inc(set_up, 1)
            pool.sem_inc(col_written, 1)
            pool.wait_ge(zeroed, 16 * TILES)

            with pool.Fori(0, ER) as c:
                pool.memset(seen[:, :], 0.0).then_inc(seen_clear, 1)
                hold(pool, passed, seen_clear, c + 1)
                hold(pool, passed, idx_ready, c + 1)
                pool.indirect_dma_start(out=seen[:, :], out_offset=None, in_=counts,
                                        in_offset=bass.IndirectOffsetOnAxis(ap=idx1[:, :], axis=0),
                                        bounds_check=NP * NP - 1, oob_is_err=False).then_inc(seen_in, 16)
                hold(pool, passed, ln_seen_done, c + 1)
                for to, value in ((counts, seen), (table, ln_seen)):
                    pool.indirect_dma_start(out=to, out_offset=bass.IndirectOffsetOnAxis(ap=idx1[:, :], axis=0),
                                            in_=value[:, :], in_offset=None,
                                            bounds_check=NP * NP - 1, oob_is_err=False).then_inc(written, 16)
                hold(pool, passed, written, (c + 1) * 32)
                pool.sem_inc(col_written, 1)

        @block.scalar
        def _(act):
            with act.Fori(0, ER) as c:
                act.wait_ge(seen_done, c + 1)
                act.activation(ln_seen[:, :], seen[:, :], ACT.Ln).then_inc(ln_seen_done, 1)

        @block.tensor
        def _(pe):
            with pe.Fori(0, ER) as c:
                pe.wait_ge(col_math, c * 7 + 2)
                pe.transpose(turned[:, :], spread[:, :], ident[:, :]).then_inc(turned_done, 1)

        @block.vector
        def _(dve):
            dve.wait_ge(set_up, 3)
            with dve.Fori(0, ER) as c:
                def step(n, ins):
                    ins.then_inc(col_math, 1)
                    dve.wait_ge(col_math, c * 7 + n)

                step(1, dve.tensor_copy(col[:, :], key[:, bass.ds(c + HALO, 1)]))
                step(2, dve.tensor_copy(spread[:, :], col[:, :].to_broadcast([P, P])))
                dve.wait_ge(turned_done, c + 1)
                step(3, dve.tensor_scalar(same[:, :], turned[:, :], col[:, :], None, ALU.is_equal))
                step(4, dve.tensor_tensor(same_low[:, :], same[:, :], below[:, :], ALU.mult))
                step(5, dve.tensor_reduce(times[:, :], same[:, :], AX_X, ALU.add))
                step(6, dve.tensor_reduce(first[:, :], same_low[:, :], AX_X, ALU.max))
                dve.wait_ge(col_written, c + 1)
                step(7, dve.scalar_tensor_tensor(out=skip1[:, :], in0=col[:, :], scalar=0.0, in1=first[:, :],
                                                 op0=ALU.is_lt, op1=ALU.max))
                dve.scalar_tensor_tensor(out=idx1[:, :], in0=skip1[:, :], scalar=OOB, in1=col[:, :],
                                         op0=ALU.mult, op1=ALU.add).then_inc(idx_ready, 1)
                dve.wait_ge(seen_in, (c + 1) * 16)
                dve.tensor_tensor(seen[:, :], seen[:, :], times[:, :], ALU.add).then_inc(seen_done, 1)


def phase2(nc, table2, arow_d, trow_d, agg_d, ident, xp, a_src, a_dst):
    CW = 400
    CH = NP // CW
    ITEMS = CH * GT
    STEPS = H * TILES
    VS = 4
    SPAN = 93
    FINISH, TURN, COPY = SPAN, SPAN + 1, SPAN + 2
    TM = 11
    assert CH * CW == NP and ITEMS % 2 == 0 and STEPS % VS == 0 and COPY < STEPS - 1
    due = {}
    for item in range(ITEMS):
        due.setdefault(item * SPAN // ITEMS, []).append(item)
    arow_v = arow_d.rearrange("(h t) p -> h (t p)", h=H)
    ctx = ExitStack()
    with ctx:
        def sb(name, shape, dt=F32):
            return ctx.enter_context(nc.sbuf_tensor(name, shape, dt))

        def sem(name):
            return ctx.enter_context(nc.semaphore(name))

        steep = sb("steep", [P, TILES * H])
        flat = sb("flat", [P, TILES * H])
        e_self = sb("e_self", [P, TILES * H])
        L = sb("L", [P, TILES, GW])
        t12 = [sb(f"t12_{k}", [P, 2, GW]) for k in range(2)]
        v = [sb(f"v{k}", [P, GW]) for k in range(VS)]
        blk = [sb(f"blk{k}", [P, GT, P]) for k in range(2)]
        bc = sb("bc", [P, H, CW])
        nat = [sb(f"nat{k}", [P, CW]) for k in range(2)]
        stage = sb("stage", [P, GT, CX])
        mpart = sb("mpart", [P, GT, H, CH])
        mx = sb("mx", [P, GT * H])
        ms = sb("ms", [P, GT * H])
        t1 = sb("t1", [P, GT * H])
        t2 = sb("t2", [P, GT * H])
        le = sb("le", [P, GT * H])
        trow = sb("trow", [P, 2, H, GT])
        trow_t = sb("trow_t", [2 * H * GT, P])
        junk_sb = sb("junk_sb", [P, CW], BF16)
        acc = [ctx.enter_context(nc.psum_tensor(f"acc{k}", [P, HALF], F32)) for k in range(GT)]
        lt = ctx.enter_context(nc.psum_tensor("lt", [P, 2 * HALF], F32))
        spare = ctx.enter_context(nc.psum_tensor("spare", [P, HALF], F32))
        junk = [spare[:, 0:CW], junk_sb[:, :]]

        scaled = sem("scaled")
        bc_in = sem("bc_in")
        nat_in = [sem(f"nat_in{k}") for k in range(2)]
        maxed = sem("maxed")
        t_math = sem("t_math")
        t_turned = sem("t_turned")
        t_copied = sem("t_copied")
        t_out = sem("t_out")
        self_done = sem("self_done")
        t12_in = [sem(f"t12_in{k}") for k in range(2)]
        blk_in = [sem(f"blk_in{k}") for k in range(2)]
        L_turned = sem("L_turned")
        L_filled = sem("L_filled")
        raw_done = sem("raw_done")
        masked = sem("masked")
        w_ready = sem("w_ready")
        v_used = sem("v_used")
        acc_done = sem("acc_done")
        acc_free = sem("acc_free")
        agg_out = sem("agg_out")
        passed = sem("passed_phase2")
        block = ctx.enter_context(nc.Block())

        @block.sync
        def _(sp):
            def load_item(g, item):
                c, dt = divmod(item, GT)
                if dt == 0:
                    hold(sp, passed, maxed, (g * ITEMS + item) * H + H)
                    sp.dma_start(bc[:, :, :], arow_v[:, c * CW:(c + 1) * CW].rearrange("(o h) c -> o h c", o=1)
                                 .to_broadcast([P, H, CW])).then_inc(bc_in, 16)
                hold(sp, passed, maxed, (g * ITEMS + item) * H)
                sp.dma_start(nat[item % 2][:, :], table2[bass.ds(g * GW + dt * P, P), c * CW:(c + 1) * CW])\
                    .then_inc(nat_in[item % 2], 16)

            def store_sums(g, h):
                unit = g * H + h
                hold(sp, passed, acc_free, unit * GT + 2 * GT)
                sp.dma_start(agg_d[h, bass.ds(g * GW, GW), :].rearrange("(t p) c -> p t c", p=P),
                             stage[:, :, :]).then_inc(agg_out, 16)

            def group(g, ahead):
                for n in range(STEPS):
                    if ahead:
                        for item in due.get(n, ()):
                            load_item(g + 1, item)
                    if n % TILES == 8 and n > TILES:
                        store_sums(g, n // TILES - 1)
                store_sums(g, H - 1)

            sp.sem_inc(agg_out, 16)
            sp.sem_inc(maxed, H)
            for item in range(ITEMS):
                load_item(0, item)
            with sp.Fori(0, G - 1) as g:
                group(g, True)
            group(G - 1, False)
            sp.wait_ge(agg_out, 16 * G * H + 16)

        @block.gpsimd
        def _(pool):
            def load_block(g, s):
                hold(pool, passed, L_turned, g * TILES + s + 1)
                pool.dma_start(blk[s % 2][:, :, :],
                               table2[bass.ds(g * GW, GW), s * P:(s + 1) * P].rearrange("(t p) c -> p t c", p=P))\
                    .then_inc(blk_in[s % 2], 16)

            def load_terms(g, h, first=False):
                if not first:
                    hold(pool, passed, raw_done, g * STEPS + (h - 1) * TILES + 1)
                rows_g = trow_d[bass.ds(g * (2 * H * GT), 2 * H * GT), :]
                pool.dma_start(t12[h % 2][:, :, :],
                               rows_g.rearrange("(k h t) p -> h k (t p)", k=2, h=H)[h:h + 1, :, :]
                               .to_broadcast([P, 2, GW])).then_inc(t12_in[h % 2], 16)

            def store_terms(g):
                hold(pool, passed, t_copied, g + 1)
                pool.dma_start(trow_d[bass.ds(g * (2 * H * GT), 2 * H * GT), :], trow_t[:, :]).then_inc(t_out, 16)
                hold(pool, passed, t_out, g * 16 + 16)

            def prepare(g, first=False):
                for s in range(TILES):
                    load_block(g, s)
                store_terms(g)
                load_terms(g, 0, first)

            pool.sem_inc(L_turned, 2)
            prepare(0, first=True)
            with pool.Fori(0, G - 1) as g:
                for h in range(1, H):
                    load_terms(g, h)
                prepare(g + 1)
            for h in range(1, H):
                load_terms(G - 1, h)

        @block.scalar
        def _(act):
            def weigh(g, n):
                h, s = divmod(n, TILES)
                act.wait_ge(masked, g * STEPS + n + 1)
                act.activation(v[n % VS][:, :], v[n % VS][:, :], ACT.Exp,
                               bias=flat[:, s * H + h:s * H + h + 1]).then_inc(w_ready, 1)

            def fill(g, s):
                act.wait_ge(L_turned, g * TILES + s + 3)
                act.activation(L[:, s, :], lt[:, 0:GW], ACT.Copy).then_inc(L_filled, 1)

            def copy_terms(g):
                act.wait_ge(t_turned, g + 1)
                act.wait_ge(t_out, g * 16)
                act.activation(trow_t[:, :], spare[0:2 * H * GT, 0:P], ACT.Copy).then_inc(t_copied, 1)
                act.activation(e_self[:, bass.ds(g * (GT * H), GT * H)], le[:, :], ACT.Exp).then_inc(self_done, 1)

            def group(g, ahead):
                for n in range(STEPS):
                    weigh(g, n)
                    if ahead and n >= STEPS - TILES + 2:
                        fill(g + 1, n - (STEPS - TILES + 2))
                    if ahead and n == COPY:
                        copy_terms(g + 1)
                if ahead:
                    fill(g + 1, TILES - 2)
                    fill(g + 1, TILES - 1)

            for s in range(TILES):
                fill(0, s)
            copy_terms(0)
            act.wait_ge(scaled, 2)
            with act.Fori(0, G - 1) as g:
                group(g, True)
            group(G - 1, False)

        @block.tensor
        def _(pe):
            def turn(g, s):
                ahead = g * 13 + s // 2 if s % 2 == 0 else g * 12 + s // 2
                pe.wait_ge(blk_in[s % 2], ahead * 16 + 16)
                pe.wait_ge(L_filled, g * TILES + s)
                for dt in range(GT):
                    last = pe.transpose(lt[:, dt * P:(dt + 1) * P], blk[s % 2][:, dt, :], ident[:, :])
                last.then_inc(L_turned, 1)

            def turn_terms(g):
                hold(pe, passed, t_math, g * TM + TM)
                pe.transpose(spare[0:2 * H * GT, 0:P], trow[:, :, :, :].rearrange("p k h t -> p (k h t)"),
                             ident[:, :]).then_inc(t_turned, 1)

            def add_up(g, n):
                h, s = divmod(n, TILES)
                pe.wait_ge(w_ready, g * STEPS + n + 1)
                for dt in range(GT):
                    if s == 0:
                        pe.wait_ge(acc_free, (g * H + h) * GT + dt + 1)
                    one = pe.matmul(acc[dt][:, 0:CX], v[n % VS][:, dt * P:(dt + 1) * P], xp[:, s, h, :],
                                    start=s == 0, stop=s == TILES - 1)
                    if dt == GT - 1:
                        one.then_inc(v_used, 1)
                    elif s == TILES - 1:
                        one.then_inc(acc_done, 1)

            def group(g, ahead):
                for n in range(STEPS):
                    add_up(g, n)
                    if ahead and n >= STEPS - TILES:
                        turn(g + 1, n - (STEPS - TILES))
                    if ahead and n == TURN:
                        turn_terms(g + 1)

            pe.sem_inc(acc_free, GT)
            for s in range(TILES):
                turn(0, s)
            turn_terms(0)
            with pe.Fori(0, G - 1) as g:
                group(g, True)
            group(G - 1, False)

        @block.vector
        def _(dve):
            def look(g, item):
                c, dt = divmod(item, GT)
                dve.wait_ge(nat_in[item % 2], (g * (ITEMS // 2) + item // 2 + 1) * 16)
                if dt == 0:
                    dve.wait_ge(bc_in, (g * CH + c + 1) * 16)
                if item == 0:
                    dve.wait_ge(t_copied, g)
                    dve.wait_ge(t_math, g * TM)
                for h in range(H):
                    hold(dve, passed, maxed, (g * ITEMS + item) * H + h + H - 1)
                    dve.tensor_tensor_reduce(out=junk[h % 2], in0=nat[item % 2][:, :], in1=bc[:, h, :],
                                             scale=1.0, scalar=NEG, op0=ALU.add, op1=ALU.max,
                                             accum_out=mpart[:, dt, h, c:c + 1]).then_inc(maxed, 1)

            def finish_terms(g):
                mine = bass.ds(g * (GT * H), GT * H)
                done = [0]

                def then(ins):
                    ins.then_inc(t_math, 1)
                    done[0] += 1
                    dve.wait_ge(t_math, g * TM + done[0])

                dve.wait_ge(maxed, (g + 1) * (ITEMS * H) + H)
                dve.wait_ge(t_turned, g)
                dve.wait_ge(self_done, g)
                then(dve.tensor_reduce(mx[:, :], mpart[:, :, :, :].rearrange("p t h c -> p (t h) c"), AX_X, ALU.max))
                then(dve.tensor_tensor(mx[:, :], mx[:, :], a_src[:, mine], ALU.max))
                then(dve.tensor_tensor(mx[:, :], mx[:, :], a_dst[:, mine], ALU.add))
                then(dve.scalar_tensor_tensor(out=ms[:, :], in0=mx[:, :], scalar=SLOPE0, in1=mx[:, :],
                                              op0=ALU.mult, op1=ALU.max))
                then(dve.tensor_tensor(t1[:, :], a_dst[:, mine], ms[:, :], ALU.subtract))
                then(dve.scalar_tensor_tensor(out=t2[:, :], in0=a_dst[:, mine], scalar=SLOPE0, in1=ms[:, :],
                                              op0=ALU.mult, op1=ALU.subtract))
                then(dve.tensor_tensor(le[:, :], t1[:, :], steep[:, mine], ALU.add))
                then(dve.tensor_tensor(le[:, :], le[:, :], t2[:, :], ALU.max))
                then(dve.tensor_tensor(le[:, :], le[:, :], flat[:, mine], ALU.add))
                for k, t in enumerate((t1, t2)):
                    then(dve.tensor_copy(trow[:, k, :, :], t[:, :].rearrange("p (t h) -> p h t", h=H)))

            def score(g, n):
                h, s = divmod(n, TILES)
                dve.wait_ge(v_used, g * STEPS + n + 1)
                if s == 0:
                    dve.wait_ge(t12_in[h % 2], (g * (H // 2) + h // 2 + 1) * 16)
                dve.scalar_tensor_tensor(out=v[n % VS][:, :], in0=t12[h % 2][:, 0, :],
                                         scalar=steep[:, s * H + h:s * H + h + 1], in1=t12[h % 2][:, 1, :],
                                         op0=ALU.add, op1=ALU.max).then_inc(raw_done, 1)

            def mask(g, n):
                h, s = divmod(n, TILES)
                dve.wait_ge(raw_done, g * STEPS + n + 2)
                if h == 0:
                    dve.wait_ge(L_filled, g * TILES + s + 1)
                dve.tensor_tensor(v[n % VS][:, :], v[n % VS][:, :], L[:, s, :], ALU.add).then_inc(masked, 1)

            def keep_sums(g, h):
                unit = g * H + h
                dve.wait_ge(agg_out, unit * 16 + 16)
                dve.wait_ge(self_done, g + 1)
                for dt in range(GT):
                    if dt < GT - 1:
                        dve.wait_ge(acc_done, unit * (GT - 1) + dt + 1)
                    else:
                        dve.wait_ge(v_used, unit * TILES + TILES + VS)
                    dve.scalar_tensor_tensor(out=stage[:, dt, :], in0=xp[:, g * GT + dt, h, :],
                                             scalar=e_self[:, bass.ds(g * (GT * H) + dt * H + h, 1)],
                                             in1=acc[dt][:, 0:CX], op0=ALU.mult, op1=ALU.add).then_inc(acc_free, 1)

            def group(g, ahead):
                score(g, 0)
                for n in range(STEPS):
                    if n < STEPS - 1:
                        score(g, n + 1)
                    mask(g, n)
                    if n % TILES == 2 and n > TILES:
                        keep_sums(g, n // TILES - 1)
                    if ahead:
                        for item in due.get(n, ()):
                            look(g + 1, item)
                        if n == FINISH:
                            finish_terms(g + 1)
                keep_sums(g, H - 1)

            dve.sem_inc(v_used, VS)
            dve.sem_inc(raw_done, 1)
            dve.tensor_scalar(steep[:, :], a_src[:, :], 1.0 - SLOPE0, None, ALU.mult).then_inc(scaled, 1)
            dve.tensor_scalar(flat[:, :], a_src[:, :], SLOPE0, None, ALU.mult).then_inc(scaled, 1)
            dve.wait_ge(scaled, 2)
            for item in range(ITEMS):
                look(0, item)
            finish_terms(0)
            with dve.Fori(0, G - 1) as g:
                group(g, True)
            group(G - 1, False)


def phase3(nc, x, bias, w1, a1, agg_d, x1_d, alrow_d, ident, h2, al, ar):
    ctx = ExitStack()
    with ctx:
        def sb(name, shape, dt=F32):
            return ctx.enter_context(nc.sbuf_tensor(name, shape, dt))

        def sem(name):
            return ctx.enter_context(nc.semaphore(name))

        w_sb = sb("w1_sb", [P, KC, D])
        bias_bc = sb("bias_bc", [P, D])
        a_bc = sb("a_bc", [P, 2, D])
        xt = [sb(f"x1t{k}", [P, D]) for k in range(2)]
        sums = [sb(f"sums{k}", [P, H, CX]) for k in range(2)]
        y = sb("y", [P, D])
        ht = [sb(f"h1t{k}", [P, D]) for k in range(2)]
        hT = [sb(f"h1T{k}", [P, KC, P]) for k in range(2)]
        rz = sb("rz", [P, H])
        stats = sb("stats1", [P, 2, 6])
        mv = sb("mv1", [P, 2])
        std = sb("std1", [P, 1])
        rstd = sb("rstd1", [P, 1])
        nbias = sb("nbias1", [P, 1])
        prod = sb("prod1", [P, D])
        alr = [sb(f"alr{k}", [P, 2]) for k in range(2)]
        al_rows = sb("al_rows_sb", [TILES, P])
        eps = sb("eps1", [P, 1])
        tp = ctx.enter_context(nc.psum_tensor("tp1", [P, KC * P], F32))
        mm = [ctx.enter_context(nc.psum_tensor(f"mmb{k}", [P, D], F32)) for k in range(2)]

        weights_in = sem("w1_in")
        x_in = [sem(f"xb_in{k}") for k in range(2)]
        x1_done = sem("x1_done")
        x1_out = [sem(f"x1_out{k}") for k in range(2)]
        eps_set = sem("eps_set")
        rz_done = sem("rz_done")
        y_done = sem("y_done")
        stats_done = sem("stats1_done")
        aggr_done = sem("aggr1_done")
        std_done = sem("std1_done")
        rstd_done = sem("rstd1_done")
        norm_done = sem("norm1_done")
        h_done = sem("h1_done")
        h_used = sem("h1_used")
        hT_done = sem("hT1_done")
        mm_done = sem("mm1_done")
        h2_copied = sem("h2_copied")
        scored = sem("scored1")
        scores_kept = sem("scores1_kept")
        al_turned = sem("al_turned")
        al_copied = sem("al_copied")
        al_out = sem("al_out")
        passed = sem("passed_phase3")
        block = ctx.enter_context(nc.Block())

        @block.sync
        def _(sp):
            def load(i, k, rounds, size=P):
                hold(sp, passed, h_done, i + 1)
                hold(sp, passed, x1_out[k], rounds * 16)
                sp.dma_start(xt[k][0:size, :], rows(x, i, size)).then_inc(x_in[k], 16)
                sp.dma_start(sums[k][:, :, :], agg_d[:, bass.ds(i * P, P), :].rearrange("h p c -> p h c"))\
                    .then_inc(x_in[k], 16)

            def store(i, k):
                hold(sp, passed, x1_done, i + 1)
                sp.dma_start(rows(x1_d, i), xt[k][:, :]).then_inc(x1_out[k], 16)

            sp.sem_inc(h_done, 2)
            load(0, 0, 0)
            sp.dma_start(bias_bc[:, :], bias.rearrange("(o n) -> o n", o=1).to_broadcast([P, D]))\
                .then_inc(weights_in, 16)
            sp.dma_start(a_bc[:, :, :].rearrange("p k n -> p (k n)"), a1.to_broadcast([P, 2 * D]))\
                .then_inc(weights_in, 16)
            sp.dma_start(w_sb[:, :, :], w1.rearrange("(k p) n -> p k n", p=P)).then_inc(weights_in, 16)
            load(1, 1, 0)
            with sp.Fori(0, TILES // 2 - 1) as r:
                for k in range(2):
                    store(r * 2 + k, k)
                    load(r * 2 + k + 2, k, r + 1)
            store(TILES - 3, 0)
            load(TILES - 1, 0, TILES // 2, TAIL)
            store(TILES - 2, 1)
            store(TILES - 1, 0)
            for k in range(2):
                sp.wait_ge(x1_out[k], 16 * (TILES // 2 + 1 - k))
            sp.wait_ge(al_copied, 1)
            sp.dma_start(alrow_d, al_rows[:, :]).then_inc(al_out, 16)
            sp.wait_ge(al_out, 16)

        @block.scalar
        def _(act):
            def normalise(i, k):
                act.wait_ge(aggr_done, i + 1)
                act.activation(std[:, :], mv[:, 1:2], ACT.Sqrt, bias=eps[:, :]).then_inc(std_done, 1)
                act.wait_ge(norm_done, i + 1)
                act.wait_ge(h_used, i + 1)
                act.activation(ht[k][:, :], xt[k][:, :], ACT.Relu, bias=nbias[:, :], scale=rstd[:, :])\
                    .then_inc(h_done, 1)

            def keep_transposed(i, k):
                act.wait_ge(h_used, i + 3)
                act.wait_ge(mm_done, i + 1)
                act.activation(hT[k][:, :, :].rearrange("p k n -> p (k n)"), tp[:, :], ACT.Copy)\
                    .then_inc(hT_done, 1)

            def keep_h2(i, k):
                act.wait_ge(scores_kept, 2 * i + 2)
                act.activation(h2[:, bass.ds(i * D, D)], mm[k][:, :], ACT.Copy).then_inc(h2_copied, 1)

            act.sem_inc(h_used, 2)
            act.sem_inc(mm_done, 2)
            act.wait_ge(eps_set, 1)
            normalise(0, 0)
            normalise(1, 1)
            keep_transposed(0, 0)
            with act.Fori(0, TILES // 2 - 1) as r:
                i = r * 2
                for k in range(2):
                    keep_transposed(i + k + 1, 1 - k)
                    normalise(i + k + 2, k)
                    keep_h2(i + k, k)
            keep_transposed(TILES - 2, 1)
            normalise(TILES - 1, 0)
            keep_h2(TILES - 3, 0)
            keep_transposed(TILES - 1, 0)
            keep_h2(TILES - 2, 1)
            keep_h2(TILES - 1, 0)
            act.wait_ge(al_turned, 1)
            act.activation(al_rows[:, :], tp[0:TILES, 0:P], ACT.Copy).then_inc(al_copied, 1)

        @block.vector
        def _(dve):
            def finish_layer(i, k, rounds):
                dve.wait_ge(x_in[k], rounds * 32)
                dve.wait_ge(y_done, i * H)
                dve.reciprocal(rz[:, :], sums[k][:, :, C:CX].rearrange("p h c -> p (h c)")).then_inc(rz_done, 1)
                dve.wait_ge(rz_done, i + 1)
                dve.wait_ge(x1_done, i)
                for h in range(H):
                    dve.scalar_tensor_tensor(out=y[:, h * C:(h + 1) * C], in0=sums[k][:, h, 0:C],
                                             scalar=rz[:, h:h + 1], in1=bias_bc[:, h * C:(h + 1) * C],
                                             op0=ALU.mult, op1=ALU.add).then_inc(y_done, 1)
                dve.wait_ge(y_done, i * H + H)
                dve.scalar_tensor_tensor(out=xt[k][:, :], in0=y[:, :], scalar=0.0, in1=xt[k][:, :],
                                         op0=ALU.max, op1=ALU.add).then_inc(x1_done, 1)
                dve.wait_ge(x1_done, i + 1)

            def statistics(i, k):
                for j in range(2):
                    dve.bn_stats(stats[:, j, :], xt[k][:, j * HALF:(j + 1) * HALF]).then_inc(stats_done, 1)
                hold(dve, passed, stats_done, 2 * i + 2)
                dve.bn_aggr(mv[:, :], stats[:, :, :].rearrange("p a b -> p (a b)")).then_inc(aggr_done, 1)
                dve.wait_ge(std_done, i + 1)
                dve.reciprocal(rstd[:, :], std[:, :]).then_inc(rstd_done, 1)
                dve.wait_ge(rstd_done, i + 1)
                dve.scalar_tensor_tensor(out=nbias[:, :], in0=mv[:, 0:1], scalar=-1.0, in1=rstd[:, :],
                                         op0=ALU.mult, op1=ALU.mult).then_inc(norm_done, 1)
                dve.wait_ge(h_done, i + 3)

            def score(i, k):
                dve.wait_ge(mm_done, i + 3)
                for j in range(2):
                    dve.wait_ge(scored, i * 2 + j)
                    dve.tensor_tensor_reduce(out=prod[:, :], in0=mm[k][:, :], in1=a_bc[:, j, :], scale=1.0,
                                             scalar=0.0, op0=ALU.mult, op1=ALU.add,
                                             accum_out=alr[k][:, j:j + 1]).then_inc(scored, 1)
                dve.wait_ge(scored, i * 2 + 2)
                dve.tensor_copy(al[:, bass.ds(i, 1)], alr[k][:, 0:1]).then_inc(scores_kept, 1)
                dve.tensor_copy(ar[:, bass.ds(i, 1)], alr[k][:, 1:2]).then_inc(scores_kept, 1)
                dve.wait_ge(scores_kept, 2 * i + 2)

            dve.memset(eps[:, :], LN_EPS).then_inc(eps_set, 1)
            dve.wait_ge(weights_in, 48)
            for k in range(2):
                finish_layer(k, k, 1)
                statistics(k, k)
            with dve.Fori(0, TILES // 2 - 1) as r:
                for k in range(2):
                    finish_layer(r * 2 + k + 2, k, r + 2)
                    statistics(r * 2 + k + 2, k)
                    score(r * 2 + k, k)
            finish_layer(TILES - 1, 0, TILES // 2 + 1)
            statistics(TILES - 1, 0)
            score(TILES - 3, 0)
            score(TILES - 2, 1)
            score(TILES - 1, 0)

        @block.tensor
        def _(pe):
            def transpose_h(i, k):
                pe.wait_ge(h_done, i + 3)
                pe.wait_ge(hT_done, i)
                for c in range(KC):
                    last = pe.transpose(tp[:, c * P:(c + 1) * P], ht[k][:, c * P:(c + 1) * P], ident[:, :])
                last.then_inc(h_used, 1)

            def project(i, k):
                pe.wait_ge(hT_done, i + 1)
                pe.wait_ge(h2_copied, i + 1)
                for c in range(KC):
                    for f in range(2):
                        last = pe.matmul(mm[k][:, f * HALF:(f + 1) * HALF], hT[k][:, c, :],
                                         w_sb[:, c, f * HALF:(f + 1) * HALF], start=c == 0, stop=c == KC - 1)
                last.then_inc(mm_done, 1)

            pe.sem_inc(h2_copied, 2)
            pe.wait_ge(weights_in, 48)
            transpose_h(0, 0)
            with pe.Fori(0, TILES // 2) as r:
                i = r * 2
                for k in range(2):
                    transpose_h(i + k + 1, 1 - k)
                    project(i + k, k)
            project(TILES - 1, 0)
            pe.wait_ge(scores_kept, 2 * TILES)
            pe.wait_ge(hT_done, TILES)
            pe.transpose(tp[0:TILES, 0:P], al[:, :], ident[:, :]).then_inc(al_turned, 1)


def phase4(nc, table2, alrow_d, x1_d, ident, h2, ar, out):
    STEPS = 2 * TILES
    WS = 5
    KEEP, FINISH = 2, 4
    assert STEPS % WS == 0 and STEPS % 2 == 0
    ctx = ExitStack()
    with ctx:
        def sb(name, shape, dt=F32):
            return ctx.enter_context(nc.sbuf_tensor(name, shape, dt))

        def sem(name):
            return ctx.enter_context(nc.semaphore(name))

        al_bc = sb("al_bc", [P, NP])
        neg_al = sb("neg_al", [P, NP])
        neg_flat = sb("neg_flat", [P, NP])
        steep_ar = sb("steep_ar", [P, TILES])
        flat_ar = sb("flat_ar", [P, TILES])
        w = [sb(f"w{k}", [P, GW]) for k in range(WS)]
        raw = [sb(f"raw{k}", [P, GW]) for k in range(2)]
        w_sum = sb("w_sum", [P, GW])
        ones = sb("ones", [P, 1])
        rs = sb("rs", [P, GT])
        total = sb("total", [P, GT])
        y = sb("yo", [P, GT, HALF])
        m = sb("mo", [P, GT, HALF])
        x1t = sb("x1o", [P, GT, HALF])
        acc = [ctx.enter_context(nc.psum_tensor(f"accb{k}", [P, HALF], F32)) for k in range(GT)]
        rs_ps = ctx.enter_context(nc.psum_tensor("rs_ps", [P, HALF], F32))

        al_in = sem("al_in")
        consts = sem("consts4")
        L_in = [sem(f"L_in{k}") for k in range(WS)]
        raw_done = sem("raw4_done")
        masked = sem("masked4")
        w_ready = sem("w4_ready")
        w_summed = sem("w_summed")
        w_used = sem("w_used")
        acc_done = sem("acc4_done")
        acc_free = sem("acc4_free")
        total_done = sem("total_done")
        rs_math = sem("rs_math")
        m_done = sem("m_done")
        e_done = sem("e_done")
        x1_in = sem("x1_in")
        elu_done = sem("elu_done")
        y_done = sem("yo_done")
        y_out = sem("y_out")
        passed = sem("passed_phase4")
        block = ctx.enter_context(nc.Block())

        @block.sync
        def _(sp):
            def load_L(g, n):
                dt = n % TILES
                hold(sp, passed, w_used, g * STEPS + n + 1)
                if WS <= n < TILES + WS:
                    hold(sp, passed, w_summed, g * TILES + n - WS + 1)
                sp.dma_start(w[n % WS][:, :], table2[dt * P:(dt + 1) * P, bass.ds(g * GW, GW)])\
                    .then_inc(L_in[n % WS], 16)

            def load_x1(g, f):
                hold(sp, passed, y_done, g * 2 + f)
                sp.dma_start(x1t[:, :, :], x1_d[bass.ds(g * GW, GW), f * HALF:(f + 1) * HALF]
                             .rearrange("(t p) c -> p t c", p=P)).then_inc(x1_in, 16)

            def store(g, f, last=False):
                hold(sp, passed, y_done, g * 2 + f + 1)
                cols = slice(f * HALF, (f + 1) * HALF)
                whole = GT - 1 if last else GT
                sp.dma_start(out[bass.ds(g * GW, whole * P), cols].rearrange("(t p) c -> p t c", p=P),
                             y[:, 0:whole, :]).then_inc(y_out, 16)
                if last:
                    sp.dma_start(out[N - TAIL:N, cols], y[0:TAIL, GT - 1, :]).then_inc(y_out, 16)

            def group(g, first=False, last=False):
                for n in range(STEPS):
                    load_L(g, n)
                    if n == TILES // 2 and not first:
                        store(g - 1, 1)
                    if n == TILES + TILES // 2:
                        store(g, 0, last)
                    if n == TILES // 2 + 1:
                        load_x1(g, 0)
                    if n == TILES + TILES // 2 + 1:
                        load_x1(g, 1)

            sp.sem_inc(w_used, WS)
            sp.dma_start(al_bc[:, :], alrow_d.rearrange("t p -> (t p)").rearrange("(o n) -> o n", o=1)
                         .to_broadcast([P, NP])).then_inc(al_in, 16)
            group(0, first=True)
            with sp.Fori(1, G - 1) as g:
                group(g)
            group(G - 1, last=True)
            store(G - 1, 1, last=True)
            sp.wait_ge(y_out, 16 * (2 * G + 2))

        @block.scalar
        def _(act):
            def weigh(g, n):
                dt = n % TILES
                act.wait_ge(masked, g * STEPS + n + 3)
                act.activation(w[n % WS][:, :], w[n % WS][:, :], ACT.Exp, bias=flat_ar[:, dt:dt + 1])\
                    .then_inc(w_ready, 1)

            def exp_m(unit):
                act.wait_ge(m_done, unit + 1)
                act.activation(m[:, :, :], m[:, :, :], ACT.Exp).then_inc(e_done, 1)

            def group(g, first=False):
                for n in range(STEPS):
                    weigh(g, n)
                    if n == FINISH and not first:
                        exp_m(g * 2 - 1)
                    if n == TILES + FINISH:
                        exp_m(g * 2)

            act.wait_ge(consts, 5)
            group(0, first=True)
            with act.Fori(1, G) as g:
                group(g)
            exp_m(2 * G - 1)

        @block.vector
        def _(dve):
            def score(g, n):
                dt = n % TILES
                cols = bass.ds(g * GW, GW)
                dve.wait_ge(masked, g * STEPS + n + 1)
                dve.scalar_tensor_tensor(out=raw[n % 2][:, :], in0=neg_al[:, cols], scalar=steep_ar[:, dt:dt + 1],
                                         in1=neg_flat[:, cols], op0=ALU.add, op1=ALU.min).then_inc(raw_done, 1)

            def mask(g, n):
                dve.wait_ge(raw_done, g * STEPS + n + 1)
                dve.wait_ge(L_in[n % WS], (g * (STEPS // WS) + n // WS + 1) * 16)
                dve.tensor_tensor(w[n % WS][:, :], w[n % WS][:, :], raw[n % 2][:, :], ALU.add).then_inc(masked, 1)

            def sum_weights(g, n):
                dve.wait_ge(w_ready, g * STEPS + n + 1)
                if n == 0:
                    dve.wait_ge(total_done, g)
                    dve.tensor_copy(w_sum[:, :], w[0][:, :]).then_inc(w_summed, 1)
                else:
                    dve.wait_ge(w_summed, g * TILES + n)
                    dve.tensor_tensor(w_sum[:, :], w_sum[:, :], w[n % WS][:, :], ALU.add).then_inc(w_summed, 1)

            def invert_total(g):
                dve.wait_ge(total_done, g + 1)
                dve.wait_ge(acc_free, g * 2 * GT + GT)
                dve.tensor_scalar(total[:, :], rs_ps[:, 0:GT], SUM_EPS, None, ALU.add).then_inc(rs_math, 1)
                dve.wait_ge(rs_math, g * 2 + 2)
                dve.reciprocal(rs[:, :], total[:, :]).then_inc(rs_math, 1)
                dve.wait_ge(rs_math, g * 2 + 3)

            def keep(unit):
                dve.wait_ge(y_done, unit)
                for st in range(GT):
                    if st < GT - 1:
                        dve.wait_ge(acc_done, unit * (GT - 1) + st + 1)
                    else:
                        dve.wait_ge(w_used, unit * TILES + TILES + WS)
                    if st == 0:
                        dve.wait_ge(y_out, unit * 16)
                    dve.tensor_scalar(y[:, st, :], acc[st][:, :], rs[:, st:st + 1], None, ALU.mult)\
                        .then_inc(acc_free, 1)
                dve.wait_ge(acc_free, unit * GT + 2 * GT)
                dve.tensor_scalar(m[:, :, :], y[:, :, :], 0.0, None, ALU.min).then_inc(m_done, 1)

            def finish(unit):
                dve.wait_ge(e_done, unit + 1)
                dve.scalar_tensor_tensor(out=y[:, :, :], in0=y[:, :, :], scalar=0.0, in1=m[:, :, :],
                                         op0=ALU.max, op1=ALU.add).then_inc(elu_done, 1)
                dve.wait_ge(elu_done, unit + 1)
                dve.wait_ge(x1_in, unit * 16 + 16)
                dve.scalar_tensor_tensor(out=y[:, :, :], in0=y[:, :, :], scalar=-1.0, in1=x1t[:, :, :],
                                         op0=ALU.add, op1=ALU.add).then_inc(y_done, 1)

            def group(g, first=False):
                score(g, 0)
                for n in range(STEPS):
                    if n < STEPS - 1:
                        score(g, n + 1)
                    mask(g, n)
                    if 1 <= n <= TILES:
                        sum_weights(g, n - 1)
                    if not first and n == KEEP:
                        keep(g * 2 - 1)
                    if not first and n == FINISH:
                        finish(g * 2 - 1)
                    if n == TILES + KEEP:
                        invert_total(g)
                        keep(g * 2)
                    if n == TILES + FINISH:
                        finish(g * 2)

            dve.sem_inc(masked, 2)
            dve.sem_inc(rs_math, 1)
            dve.memset(ones[:, :], 1.0).then_inc(consts, 1)
            dve.tensor_scalar(steep_ar[:, :], ar[:, :], SLOPE1 - 1.0, None, ALU.mult).then_inc(consts, 1)
            dve.tensor_scalar(flat_ar[:, :], ar[:, :], -SLOPE1, None, ALU.mult).then_inc(consts, 1)
            dve.wait_ge(al_in, 16)
            dve.tensor_scalar(neg_al[:, :], al_bc[:, :], -1.0, None, ALU.mult).then_inc(consts, 1)
            dve.tensor_scalar(neg_flat[:, :], al_bc[:, :], -SLOPE1, None, ALU.mult).then_inc(consts, 1)
            dve.wait_ge(consts, 5)
            group(0, first=True)
            with dve.Fori(1, G) as g:
                group(g)
            keep(2 * G - 1)
            finish(2 * G - 1)

        @block.tensor
        def _(pe):
            def add_up(g, n):
                f, dt = divmod(n, TILES)
                pe.wait_ge(w_ready, g * STEPS + n + 1)
                for st in range(GT):
                    if dt == 0:
                        pe.wait_ge(acc_free, (g * 2 + f) * GT + st + 1)
                    one = pe.matmul(acc[st][:, :], w[n % WS][:, st * P:(st + 1) * P],
                                    h2[:, dt * D + f * HALF:dt * D + (f + 1) * HALF],
                                    start=dt == 0, stop=dt == TILES - 1)
                    if st == GT - 1:
                        one.then_inc(w_used, 1)
                    elif dt == TILES - 1:
                        one.then_inc(acc_done, 1)

            def sum_total(g):
                pe.wait_ge(w_summed, g * TILES + TILES)
                pe.wait_ge(rs_math, g * 2 + 1)
                for st in range(GT):
                    one = pe.matmul(rs_ps[:, st:st + 1], w_sum[:, st * P:(st + 1) * P], ones[:, :],
                                    start=True, stop=True)
                one.then_inc(total_done, 1)

            def group(g):
                for n in range(STEPS):
                    add_up(g, n)
                    if n == TILES - 1:
                        sum_total(g)

            pe.sem_inc(acc_free, GT)
            pe.wait_ge(consts, 5)
            with pe.Fori(0, G) as g:
                group(g)


_INS = ["x", "src", "dst", "L0_gnn_W", "L0_gnn_att_src", "L0_gnn_att_dst", "L0_gnn_bias",
        "L1_gnn_W", "L1_gnn_a"]


def kernel(**inputs):
    import numpy as _np
    import concourse.bacc as _bacc
    from concourse import mybir as _mybir
    from concourse.bass_utils import run_bass_kernel_spmd as _run

    nc = _bacc.Bacc("TRN2", target_bir_lowering=False, num_devices=1)
    arrays, args = {}, []
    for name in _INS:
        a = _np.ascontiguousarray(inputs[name])
        arrays[f"in_{name}_dram"] = a
        args.append(nc.dram_tensor(f"in_{name}_dram", a.shape, _mybir.dt.from_np(a.dtype), kind="ExternalInput").ap())
    out = nc.dram_tensor("out_0_dram", (N, D), _mybir.dt.float32, kind="ExternalOutput").ap()
    build(nc, *args, out)
    r = _run(nc, [arrays], core_ids=[0])
    return r.results[0]["out_0_dram"]
```

```python
from contextlib import ExitStack

import concourse.bass as bass
from concourse import mybir

F32 = mybir.dt.float32
F32R = mybir.dt.float32r
BF16 = mybir.dt.bfloat16
F16 = mybir.dt.float16
U32 = mybir.dt.uint32
I32 = mybir.dt.int32
ALU = mybir.AluOpType
ACT = mybir.ActivationFunctionType
AX_X = mybir.AxisListType.X

P = 128
N = 3125
D = 1024
H = 4
C = D // H
E = 50000
SLOPE0 = 0.2
SLOPE1 = 0.1
LN_EPS = 1e-5
SUM_EPS = 1e-5
NEG = -1.0e30

TILES = -(-N // P)
NP = TILES * P
TAIL = N - (TILES - 1) * P
KC = D // P
HALF = 512
CX = C + 1

GT = 5
G = TILES // GT
GW = GT * P

EP = 125
ER = E // EP
HALO = 49
EX = HALO + ER + HALO
OOB = float(1 << 25)
EB = 20
FIRST = 6

assert TILES == G * GT and EP * ER == E and ER % (2 * EB) == 0 and HALO % 2 == 1


def rows(table, tile, size=P):
    return table[bass.ds(tile * P, size), :]


def hold(eng, passed, sem, value):
    eng.wait_ge(sem, value)
    eng.sem_inc(passed, 1)


def build(nc, x, src, dst, w0, att_src, att_dst, bias, w1, a1, out):
    counts = nc.dram_tensor("counts", [NP * NP, 1], F32, kind="Internal").ap()
    table = nc.dram_tensor("edge_table", [NP * NP, 1], F32, kind="Internal").ap()
    table2 = table.rearrange("(d s) o -> d (s o)", s=NP)
    arow_d = nc.dram_tensor("a_src_rows", [H * TILES, P], F32, kind="Internal").ap()
    trow_d = nc.dram_tensor("dst_term_rows", [G * 2 * H * GT, P], F32, kind="Internal").ap()
    agg_d = nc.dram_tensor("attention_sums", [H, NP, CX], F32, kind="Internal").ap()
    x1_d = nc.dram_tensor("x1", [NP, D], F32, kind="Internal").ap()
    alrow_d = nc.dram_tensor("al_rows", [TILES, P], F32, kind="Internal").ap()
    low_d = nc.dram_tensor("h2_low", [NP, D], F32R, kind="Internal").ap()
    ctx = ExitStack()
    with ctx:
        ident = ctx.enter_context(nc.sbuf_tensor("ident", [P, P], F32))
        crowded = ctx.enter_context(nc.sbuf_tensor("crowded", [P, 1], I32))
        with ExitStack() as both:
            xp = both.enter_context(nc.sbuf_tensor("xp", [P, TILES, H, CX], F32))
            a_src = both.enter_context(nc.sbuf_tensor("a_src", [P, TILES * H], F32))
            a_dst = both.enter_context(nc.sbuf_tensor("a_dst", [P, TILES * H], F32))
            with ExitStack() as edges:
                key = edges.enter_context(nc.sbuf_tensor("key", [P, EX], F32))
                phase1(nc, x, src, dst, w0, att_src, att_dst, table, table2, arow_d,
                       ident, xp, a_src, a_dst, key, crowded)
                any_edges(nc, table, counts, ident, key, crowded)
            phase2(nc, table2, arow_d, trow_d, agg_d, ident, xp, a_src, a_dst)
        with ExitStack() as both:
            h2 = both.enter_context(nc.sbuf_tensor("h2", [P, TILES * D], F32R))
            al = both.enter_context(nc.sbuf_tensor("al", [P, TILES], F32))
            ar = both.enter_context(nc.sbuf_tensor("ar", [P, TILES], F32))
            phase3(nc, x, bias, w1, a1, agg_d, x1_d, alrow_d, low_d, ident, h2, al, ar)
            phase4(nc, table2, alrow_d, x1_d, low_d, ident, h2, ar, out)


def phase1(nc, x, src, dst, w0, att_src, att_dst, table, table2, arow_d,
           ident, xp, a_src, a_dst, key, crowded):
    ctx = ExitStack()
    with ctx:
        def sb(name, shape, dt=F32):
            return ctx.enter_context(nc.sbuf_tensor(name, shape, dt))

        def sem(name):
            return ctx.enter_context(nc.semaphore(name))

        w_sb = sb("w0_sb", [P, KC, D])
        att_bc = sb("att_bc", [P, 2, D])
        xt = [sb(f"xt{k}", [P, D]) for k in range(2)]
        ht = [sb(f"ht{k}", [P, D]) for k in range(2)]
        hT = [sb(f"hT{k}", [P, KC, P]) for k in range(2)]
        stats = sb("stats", [P, 2, 6])
        mv = sb("mv", [P, 2])
        std = sb("std", [P, 1])
        rstd = sb("rstd", [P, 1])
        nbias = sb("nbias", [P, 1])
        prod = sb("prod", [P, C])
        asd = [sb(f"asd{k}", [P, 2, H]) for k in range(2)]
        a_hm = sb("a_hm", [P, H * TILES])
        a_rows = sb("a_rows", [H * TILES, P])
        neg = sb("neg", [P, 1, GW])
        e_src = sb("e_src", [P, EX], I32)
        e_dst = sb("e_dst", [P, EX], I32)
        equal = [sb(f"equal{k}", [P, HALO + ER], BF16) for k in range(2)]
        later = sb("later", [P, ER], BF16)
        before = sb("before", [P, ER], BF16)
        back = sb("back", [P, 2, ER])
        bad = sb("bad", [P, 1])
        bad_all = sb("bad_all", [P, 1])
        lnc = sb("lnc", [P, ER])
        skip = sb("skip", [P, ER])
        idx = sb("idx", [P, ER], U32)
        idx_st = [sb(f"idx_st{k}", [P, EB], U32) for k in range(2)]
        lnc_st = [sb(f"lnc_st{k}", [P, EB]) for k in range(2)]
        eps = sb("eps", [P, 1])

        tp = ctx.enter_context(nc.psum_tensor("tp", [P, KC * P], F32))
        mm = [ctx.enter_context(nc.psum_tensor(f"mm{k}", [P, D], F32)) for k in range(2)]

        edges_in = sem("edges_in")
        weights_in = sem("weights_in")
        x_in = [sem(f"x_in{k}") for k in range(2)]
        neg_set = sem("neg_set")
        ones_set = sem("ones_set")
        table_clear = sem("table_clear")
        consts = sem("consts")
        stats_done = sem("stats_done")
        aggr_done = sem("aggr_done")
        std_done = sem("std_done")
        rstd_done = sem("rstd_done")
        norm_done = sem("norm_done")
        h_done = sem("h_done")
        h_used = sem("h_used")
        hT_done = sem("hT_done")
        mm_done = sem("mm_done")
        xp_copied = sem("xp_copied")
        scored = sem("scored")
        scores_kept = sem("scores_kept")
        a_hm_done = sem("a_hm_done")
        a_T_done = sem("a_T_done")
        a_rows_done = sem("a_rows_done")
        a_rows_out = sem("a_rows_out")
        pads_set = sem("pads_set")
        key_done = sem("key_done")
        compared = sem("compared")
        tallied = sem("tallied")
        edge_math = sem("edge_math")
        bad_set = sem("bad_set")
        bad_done = sem("bad_done")
        bad_summed = sem("bad_summed")
        ln_in = sem("ln_in")
        ln_done = sem("ln_done")
        idx_done = sem("idx_done")
        staged = sem("staged")
        lnc_out = [sem(f"lnc_out{k}") for k in range(2)]
        passed = sem("passed_phase1")
        block = ctx.enter_context(nc.Block())

        @block.sync
        def _(sp):
            sp.sem_inc(h_done, 2)
            sp.wait_ge(pads_set, 2)
            for e_sb, e_in in ((e_dst, dst), (e_src, src)):
                near = e_in.rearrange("(p t) -> p t", t=ER)
                sp.dma_start(e_sb[0:EP, HALO:HALO + ER], near).then_inc(edges_in, 16)
                sp.dma_start(e_sb[1:EP, 0:HALO], near[0:EP - 1, ER - HALO:ER]).then_inc(edges_in, 16)
                sp.dma_start(e_sb[0:EP - 1, HALO + ER:EX], near[1:EP, 0:HALO]).then_inc(edges_in, 16)
            def load(i, k, size=P):
                hold(sp, passed, h_done, i + 1)
                sp.dma_start(xt[k][0:size, :], rows(x, i, size)).then_inc(x_in[k], 16)

            for k in range(2):
                load(k, k)
            sp.dma_start(w_sb[:, :, :], w0.rearrange("(k p) n -> p k n", p=P)).then_inc(weights_in, 16)
            for k, att in enumerate((att_src, att_dst)):
                sp.dma_start(att_bc[:, k, :],
                             att.rearrange("h c -> (h c)").rearrange("(o n) -> o n", o=1).to_broadcast([P, D]))\
                    .then_inc(weights_in, 16)
            with sp.Fori(1, TILES // 2) as r:
                i = r * 2
                for k in range(2):
                    load(i + k, k)
            load(TILES - 1, 0, TAIL)
            sp.wait_ge(a_rows_done, 1)
            sp.dma_start(arow_d, a_rows[:, :]).then_inc(a_rows_out, 16)
            sp.wait_ge(a_rows_out, 16)

        @block.gpsimd
        def _(pool):
            pool.memset(neg[:, :, :], NEG).then_inc(neg_set, 1)
            pool.memset(ident[:, :], 0.0).then_inc(consts, 1)
            pool.wait_ge(consts, 1)
            pool.affine_select(out=ident[:, :], in_=ident[:, :], compare_op=ALU.not_equal, fill=1.0,
                               base=0, pattern=[[-1, P]], channel_multiplier=1).then_inc(consts, 1)
            pool.wait_ge(bad_done, 1)
            pool.partition_all_reduce(bad_all[:, :], bad[:, :], P, bass.bass_isa.ReduceOp.add)\
                .then_inc(bad_summed, 1)

            pool.wait_ge(table_clear, 16 * TILES)
            pool.wait_ge(idx_done, 1)
            pool.wait_ge(ln_done, 2)

            def write_counts(b, k):
                cols = bass.ds(b * EB, EB)
                pool.tensor_copy(idx_st[k][:, :], idx[:, cols]).then_inc(staged, 1)
                pool.tensor_copy(lnc_st[k][:, :], lnc[:, cols]).then_inc(staged, 1)
                hold(pool, passed, staged, 2 * b + 2)
                for j in range(EB):
                    pool.indirect_dma_start(
                        out=table, out_offset=bass.IndirectOffsetOnAxis(ap=idx_st[k][:, j:j + 1], axis=0),
                        in_=lnc_st[k][:, j:j + 1], in_offset=None,
                        bounds_check=NP * NP - 1, oob_is_err=False).then_inc(lnc_out[k], 16)

            blocks = ER // EB
            for k in range(2):
                write_counts(k, k)
            with pool.Fori(1, blocks // 2) as r:
                b = r * 2
                for k in range(2):
                    hold(pool, passed, lnc_out[k], b * (8 * EB))
                    write_counts(b + k, k)
            for k in range(2):
                pool.wait_ge(lnc_out[k], ER * 8)

        @block.scalar
        def _(act):
            def normalise(i, k):
                act.wait_ge(aggr_done, i + 1)
                act.activation(std[:, :], mv[:, 1:2], ACT.Sqrt, bias=eps[:, :]).then_inc(std_done, 1)
                act.wait_ge(norm_done, i + 1)
                act.wait_ge(h_used, i + 1)
                act.activation(ht[k][:, :], xt[k][:, :], ACT.Relu, bias=nbias[:, :], scale=rstd[:, :])\
                    .then_inc(h_done, 1)

            def keep_transposed(i, k):
                act.wait_ge(h_used, i + 3)
                act.wait_ge(mm_done, i + 1)
                act.activation(hT[k][:, :, :].rearrange("p k n -> p (k n)"), tp[:, :], ACT.Copy)\
                    .then_inc(hT_done, 1)

            def keep_xp(i, k):
                act.wait_ge(scores_kept, 2 * i + 2)
                act.activation(xp[:, i, :, 0:C], mm[k][:, :].rearrange("p (h c) -> p h c", h=H), ACT.Copy)\
                    .then_inc(xp_copied, 1)

            def clear(i):
                act.dma_start(rows(table2, i).rearrange("p (g w) -> p g w", w=GW),
                              neg[:, :, :].to_broadcast([P, G, GW])).then_inc(table_clear, 16)

            act.sem_inc(h_used, 2)
            act.sem_inc(mm_done, 2)
            act.wait_ge(neg_set, 1)
            for k in range(2):
                act.wait_ge(x_in[k], 16)
            with act.Fori(0, TILES // 2) as i:
                clear(i)
            act.wait_ge(ones_set, 2)
            normalise(0, 0)
            normalise(1, 1)
            with act.Fori(TILES // 2, TILES) as i:
                clear(i)
            keep_transposed(0, 0)

            act.wait_ge(ln_in, 1)
            act.activation(lnc[:, :], lnc[:, :], ACT.Ln).then_inc(ln_done, 1)
            with act.Fori(0, TILES // 2 - 1) as r:
                i = r * 2
                for k in range(2):
                    keep_transposed(i + k + 1, 1 - k)
                    normalise(i + k + 2, k)
                    keep_xp(i + k, k)
            keep_transposed(TILES - 2, 1)
            normalise(TILES - 1, 0)
            keep_xp(TILES - 3, 0)
            keep_transposed(TILES - 1, 0)
            keep_xp(TILES - 2, 1)
            keep_xp(TILES - 1, 0)
            act.wait_ge(a_T_done, 1)
            act.activation(a_rows[:, :], tp[0:H * TILES, 0:P], ACT.Copy).then_inc(a_rows_done, 1)

        @block.vector
        def _(dve):
            dve.memset(e_dst[:, :], -1).then_inc(pads_set, 1)
            dve.memset(e_src[:, :], -1).then_inc(pads_set, 1)
            dve.memset(later[:, :], 0.0).then_inc(tallied, 1)
            dve.memset(before[:, :], 0.0).then_inc(tallied, 1)
            dve.memset(xp[:, :, :, C:CX], 1.0).then_inc(ones_set, 1)
            dve.memset(eps[:, :], LN_EPS).then_inc(ones_set, 1)
            def statistics(i, k, rounds):
                dve.wait_ge(x_in[k], rounds * 16)
                for j in range(2):
                    dve.bn_stats(stats[:, j, :], xt[k][:, j * HALF:(j + 1) * HALF]).then_inc(stats_done, 1)
                hold(dve, passed, stats_done, 2 * i + 2)
                dve.bn_aggr(mv[:, :], stats[:, :, :].rearrange("p a b -> p (a b)")).then_inc(aggr_done, 1)
                dve.wait_ge(std_done, i + 1)
                dve.reciprocal(rstd[:, :], std[:, :]).then_inc(rstd_done, 1)
                dve.wait_ge(rstd_done, i + 1)
                dve.scalar_tensor_tensor(out=nbias[:, :], in0=mv[:, 0:1], scalar=-1.0, in1=rstd[:, :],
                                         op0=ALU.mult, op1=ALU.mult).then_inc(norm_done, 1)
                dve.wait_ge(h_done, i + 3)

            def score(i, k):
                dve.wait_ge(mm_done, i + 3)
                for h in range(H):
                    for j in range(2):
                        dve.tensor_tensor_reduce(out=prod[:, :], in0=mm[k][:, h * C:(h + 1) * C],
                                                 in1=att_bc[:, j, h * C:(h + 1) * C], scale=1.0, scalar=0.0,
                                                 op0=ALU.mult, op1=ALU.add, accum_out=asd[k][:, j, h:h + 1])\
                            .then_inc(scored, 1)
                        dve.wait_ge(scored, i * (2 * H) + 2 * h + j + 1)
                dve.tensor_copy(a_src[:, bass.ds(i * H, H)], asd[k][:, 0, :]).then_inc(scores_kept, 1)
                dve.tensor_copy(a_dst[:, bass.ds(i * H, H)], asd[k][:, 1, :]).then_inc(scores_kept, 1)

            mine = slice(HALO, HALO + ER)

            def compare(k, slot):
                dve.tensor_tensor(equal[slot][:, :], key[:, 0:HALO + ER], key[:, bass.ds(k, HALO + ER)],
                                  ALU.is_equal).then_inc(compared, 1)

            def tally(k, slot):
                dve.wait_ge(compared, k)
                dve.wait_ge(tallied, k * 2)
                dve.tensor_tensor(later[:, :], later[:, :], equal[slot][:, mine], ALU.add).then_inc(tallied, 1)
                dve.tensor_tensor(before[:, :], before[:, :], equal[slot][:, bass.ds(k * -1 + HALO, ER)],
                                  ALU.add).then_inc(tallied, 1)

            def two_comparisons(r):
                k = r * 2 + 1
                for j in range(2):
                    dve.wait_ge(tallied, (k + j) * 2)
                    compare(k + j + 1, 1 - j)
                    tally(k + j, j)

            def index_edges():
                dve.tensor_tensor(back[:, 0, :], e_dst[:, mine], e_dst[:, HALO - 1:HALO + ER - 1],
                                  ALU.subtract).then_inc(edge_math, 1)
                dve.tensor_tensor(back[:, 1, :], e_dst[:, mine], e_dst[:, 0:ER],
                                  ALU.subtract).then_inc(edge_math, 1)
                dve.wait_ge(edge_math, 2)
                dve.tensor_scalar(back[:, 0, :], back[:, 0, :], 0.0, None, ALU.is_lt).then_inc(edge_math, 1)
                dve.tensor_scalar(back[:, 1, :], back[:, 1, :], 1.0, None, ALU.is_lt).then_inc(edge_math, 1)
                dve.wait_ge(edge_math, 4)
                dve.tensor_reduce(bad[0:EP, :], back[0:EP, :, :].rearrange("p a b -> p (a b)"), AX_X, ALU.max)\
                    .then_inc(bad_done, 1)
                dve.wait_ge(bad_done, 1)
                dve.wait_ge(tallied, 2 * HALO)
                dve.tensor_scalar(lnc[:, :], later[:, :], 1.0, None, ALU.add).then_inc(ln_in, 1)
                dve.tensor_scalar(back[:, 0, :], key[:, mine], 0.0, None, ALU.is_lt).then_inc(edge_math, 1)
                dve.wait_ge(edge_math, 5)
                dve.tensor_tensor(back[:, 0, :], back[:, 0, :], before[:, :], ALU.add).then_inc(edge_math, 1)
                dve.wait_ge(bad_summed, 1)
                dve.wait_ge(edge_math, 6)
                dve.tensor_scalar(back[:, 0, :], back[:, 0, :], bad_all[:, :], None, ALU.add)\
                    .then_inc(edge_math, 1)
                dve.tensor_copy(crowded[:, :], bad_all[:, :]).then_inc(edge_math, 1)
                dve.wait_ge(edge_math, 8)
                dve.tensor_scalar(skip[:, :], back[:, 0, :], 0.0, OOB, ALU.is_gt, ALU.mult)\
                    .then_inc(edge_math, 1)
                dve.wait_ge(edge_math, 9)
                dve.tensor_tensor(idx[:, :], skip[:, :], key[:, mine], ALU.add).then_inc(idx_done, 1)
                dve.wait_ge(ln_done, 1)
                dve.scalar_tensor_tensor(out=lnc[:, :], in0=later[:, :], scalar=0.5, in1=lnc[:, :],
                                         op0=ALU.is_gt, op1=ALU.mult).then_inc(ln_done, 1)

            dve.memset(bad[:, :], 0.0).then_inc(bad_set, 1)
            dve.wait_ge(bad_set, 1)
            dve.wait_ge(edges_in, 96)
            dve.scalar_tensor_tensor(out=key[:, :], in0=e_dst[:, :], scalar=float(NP), in1=e_src[:, :],
                                     op0=ALU.mult, op1=ALU.add).then_inc(key_done, 1)
            dve.wait_ge(key_done, 1)
            compare(1, 0)
            with dve.Fori(0, FIRST) as r:
                two_comparisons(r)
            statistics(0, 0, 1)
            statistics(1, 1, 1)
            with dve.Fori(FIRST, HALO // 2) as r:
                two_comparisons(r)
            index_edges()
            dve.wait_ge(weights_in, 48)
            with dve.Fori(0, TILES // 2 - 1) as r:
                for k in range(2):
                    statistics(r * 2 + k + 2, k, r + 2)
                    score(r * 2 + k, k)
            statistics(TILES - 1, 0, TILES // 2 + 1)
            score(TILES - 3, 0)
            score(TILES - 2, 1)
            score(TILES - 1, 0)
            dve.wait_ge(scores_kept, 2 * TILES)
            dve.tensor_copy(a_hm[:, :].rearrange("p (h t) -> p h t", h=H),
                            a_src[:, :].rearrange("p (t h) -> p h t", h=H)).then_inc(a_hm_done, 1)

        @block.tensor
        def _(pe):
            def transpose_h(i, k):
                pe.wait_ge(h_done, i + 3)
                pe.wait_ge(hT_done, i)
                for c in range(KC):
                    last = pe.transpose(tp[:, c * P:(c + 1) * P], ht[k][:, c * P:(c + 1) * P], ident[:, :])
                last.then_inc(h_used, 1)

            def project(i, k):
                pe.wait_ge(hT_done, i + 1)
                pe.wait_ge(xp_copied, i + 1)
                for c in range(KC):
                    for f in range(2):
                        last = pe.matmul(mm[k][:, f * HALF:(f + 1) * HALF], hT[k][:, c, :],
                                         w_sb[:, c, f * HALF:(f + 1) * HALF], start=c == 0, stop=c == KC - 1)
                last.then_inc(mm_done, 1)

            pe.sem_inc(xp_copied, 2)
            pe.wait_ge(consts, 2)
            pe.wait_ge(weights_in, 48)
            transpose_h(0, 0)
            with pe.Fori(0, TILES // 2) as r:
                i = r * 2
                for k in range(2):
                    transpose_h(i + k + 1, 1 - k)
                    project(i + k, k)
            project(TILES - 1, 0)
            pe.wait_ge(a_hm_done, 1)
            pe.wait_ge(hT_done, TILES)
            pe.transpose(tp[0:H * TILES, 0:P], a_hm[:, :], ident[:, :]).then_inc(a_T_done, 1)


def any_edges(nc, table, counts, ident, key, crowded):
    with ExitStack() as ctx:
        flag = nc.values_load(crowded[0:1, 0:1], min_val=0, max_val=P)
        ctx.enter_context(nc.If(flag > 0))
        ctx.enter_context(ExitStack())

        def sb(name, shape, dt=F32):
            return ctx.enter_context(nc.sbuf_tensor(name, shape, dt))

        def sem(name):
            return ctx.enter_context(nc.semaphore(name))

        zeros = sb("zeros", [P, NP])
        below = sb("below", [P, P])
        col = sb("col", [P, 1])
        spread = sb("spread", [P, P])
        same = sb("same", [P, P])
        same_low = sb("same_low", [P, P])
        times = sb("times", [P, 1])
        first = sb("first", [P, 1])
        skip1 = sb("skip1", [P, 1])
        idx1 = sb("idx1", [P, 1], U32)
        seen = sb("seen", [P, 1])
        ln_seen = sb("ln_seen", [P, 1])
        turned = ctx.enter_context(nc.psum_tensor("turned", [P, P], F32))
        set_up = sem("set_up")
        zeroed = sem("zeroed")
        col_math = sem("col_math")
        turned_done = sem("turned_done")
        idx_ready = sem("idx_ready")
        seen_clear = sem("seen_clear")
        seen_in = sem("seen_in")
        seen_done = sem("seen_done")
        ln_seen_done = sem("ln_seen_done")
        written = sem("written")
        col_written = sem("col_written")
        passed = sem("passed_any_edges")
        block = ctx.enter_context(nc.Block())

        @block.sync
        def _(sp):
            sp.wait_ge(set_up, 1)
            with sp.Fori(0, TILES) as i:
                sp.dma_start(rows(counts.rearrange("(d s) o -> d (s o)", s=NP), i), zeros[:, :])\
                    .then_inc(zeroed, 16)

        @block.gpsimd
        def _(pool):
            pool.memset(zeros[:, :], 0.0).then_inc(set_up, 1)
            pool.memset(below[:, :], 1.0).then_inc(set_up, 1)
            pool.wait_ge(set_up, 2)
            pool.affine_select(out=below[:, :], in_=below[:, :], compare_op=ALU.is_gt, fill=0.0,
                               base=0, pattern=[[-1, P]], channel_multiplier=1).then_inc(set_up, 1)
            pool.sem_inc(col_written, 1)
            pool.wait_ge(zeroed, 16 * TILES)

            with pool.Fori(0, ER) as c:
                pool.memset(seen[:, :], 0.0).then_inc(seen_clear, 1)
                hold(pool, passed, seen_clear, c + 1)
                hold(pool, passed, idx_ready, c + 1)
                pool.indirect_dma_start(out=seen[:, :], out_offset=None, in_=counts,
                                        in_offset=bass.IndirectOffsetOnAxis(ap=idx1[:, :], axis=0),
                                        bounds_check=NP * NP - 1, oob_is_err=False).then_inc(seen_in, 16)
                hold(pool, passed, ln_seen_done, c + 1)
                for to, value in ((counts, seen), (table, ln_seen)):
                    pool.indirect_dma_start(out=to, out_offset=bass.IndirectOffsetOnAxis(ap=idx1[:, :], axis=0),
                                            in_=value[:, :], in_offset=None,
                                            bounds_check=NP * NP - 1, oob_is_err=False).then_inc(written, 16)
                hold(pool, passed, written, (c + 1) * 32)
                pool.sem_inc(col_written, 1)

        @block.scalar
        def _(act):
            with act.Fori(0, ER) as c:
                act.wait_ge(seen_done, c + 1)
                act.activation(ln_seen[:, :], seen[:, :], ACT.Ln).then_inc(ln_seen_done, 1)

        @block.tensor
        def _(pe):
            with pe.Fori(0, ER) as c:
                pe.wait_ge(col_math, c * 7 + 2)
                pe.transpose(turned[:, :], spread[:, :], ident[:, :]).then_inc(turned_done, 1)

        @block.vector
        def _(dve):
            dve.wait_ge(set_up, 3)
            with dve.Fori(0, ER) as c:
                def step(n, ins):
                    ins.then_inc(col_math, 1)
                    dve.wait_ge(col_math, c * 7 + n)

                step(1, dve.tensor_copy(col[:, :], key[:, bass.ds(c + HALO, 1)]))
                step(2, dve.tensor_copy(spread[:, :], col[:, :].to_broadcast([P, P])))
                dve.wait_ge(turned_done, c + 1)
                step(3, dve.tensor_scalar(same[:, :], turned[:, :], col[:, :], None, ALU.is_equal))
                step(4, dve.tensor_tensor(same_low[:, :], same[:, :], below[:, :], ALU.mult))
                step(5, dve.tensor_reduce(times[:, :], same[:, :], AX_X, ALU.add))
                step(6, dve.tensor_reduce(first[:, :], same_low[:, :], AX_X, ALU.max))
                dve.wait_ge(col_written, c + 1)
                step(7, dve.scalar_tensor_tensor(out=skip1[:, :], in0=col[:, :], scalar=0.0, in1=first[:, :],
                                                 op0=ALU.is_lt, op1=ALU.max))
                dve.scalar_tensor_tensor(out=idx1[:, :], in0=skip1[:, :], scalar=OOB, in1=col[:, :],
                                         op0=ALU.mult, op1=ALU.add).then_inc(idx_ready, 1)
                dve.wait_ge(seen_in, (c + 1) * 16)
                dve.tensor_tensor(seen[:, :], seen[:, :], times[:, :], ALU.add).then_inc(seen_done, 1)


def phase2(nc, table2, arow_d, trow_d, agg_d, ident, xp, a_src, a_dst):
    CW = 400
    CH = NP // CW
    ITEMS = CH * GT
    STEPS = H * TILES
    VS = 4
    EARLY = 5
    LATE = 6
    first_looks = [c * (H - 1) * TILES // EARLY for c in range(EARLY)]
    first_looks += [(H - 1) * TILES + 1 + (c - EARLY) * LATE for c in range(EARLY, CH)]
    SPAN = first_looks[-1] + GT
    KEEP = 1
    FINISH, TURN, COPY = SPAN, SPAN + 1, SPAN + 2
    TM = 11
    assert CH * CW == NP and ITEMS % 2 == 0 and STEPS % VS == 0 and COPY < STEPS - 1
    due = {}
    for item in range(ITEMS):
        c, dt = divmod(item, GT)
        due.setdefault(first_looks[c] + (dt * 3 if c < EARLY else dt), []).append(item)
    arow_v = arow_d.rearrange("(h t) p -> h (t p)", h=H)
    ctx = ExitStack()
    with ctx:
        def sb(name, shape, dt=F32):
            return ctx.enter_context(nc.sbuf_tensor(name, shape, dt))

        def sem(name):
            return ctx.enter_context(nc.semaphore(name))

        steep = sb("steep", [P, TILES * H])
        flat = sb("flat", [P, TILES * H])
        e_self = sb("e_self", [P, TILES * H])
        L = sb("L", [P, TILES, GW])
        t12 = [sb(f"t12_{k}", [P, 2, GW]) for k in range(2)]
        v = [sb(f"v{k}", [P, GW]) for k in range(VS)]
        blk = [sb(f"blk{k}", [P, GT, P]) for k in range(2)]
        bc = sb("bc", [P, H, CW])
        nat = [sb(f"nat{k}", [P, CW]) for k in range(2)]
        stage = sb("stage", [P, GT, CX])
        mpart = sb("mpart", [P, GT, H, CH])
        mx = sb("mx", [P, GT * H])
        ms = sb("ms", [P, GT * H])
        t1 = sb("t1", [P, GT * H])
        t2 = sb("t2", [P, GT * H])
        le = sb("le", [P, GT * H])
        trow = sb("trow", [P, 2, H, GT])
        trow_t = sb("trow_t", [2 * H * GT, P])
        junk_sb = sb("junk_sb", [P, CW], BF16)
        acc = [ctx.enter_context(nc.psum_tensor(f"acc{k}", [P, HALF], F32)) for k in range(GT)]
        lt = ctx.enter_context(nc.psum_tensor("lt", [P, 2 * HALF], F32))
        spare = ctx.enter_context(nc.psum_tensor("spare", [P, HALF], F32))
        junk = [spare[:, 0:CW], junk_sb[:, :]]

        scaled = sem("scaled")
        bc_in = sem("bc_in")
        nat_in = [sem(f"nat_in{k}") for k in range(2)]
        maxed = sem("maxed")
        t_math = sem("t_math")
        t_turned = sem("t_turned")
        t_copied = sem("t_copied")
        t_out = sem("t_out")
        self_done = sem("self_done")
        t12_in = [sem(f"t12_in{k}") for k in range(2)]
        blk_in = [sem(f"blk_in{k}") for k in range(2)]
        L_turned = sem("L_turned")
        L_filled = sem("L_filled")
        raw_done = sem("raw_done")
        masked = sem("masked")
        w_ready = sem("w_ready")
        v_used = sem("v_used")
        acc_done = sem("acc_done")
        acc_free = sem("acc_free")
        agg_out = sem("agg_out")
        passed = sem("passed_phase2")
        block = ctx.enter_context(nc.Block())

        @block.sync
        def _(sp):
            def load_item(g, item):
                c, dt = divmod(item, GT)
                if dt == 0:
                    hold(sp, passed, maxed, (g * ITEMS + item) * H + H)
                    sp.dma_start(bc[:, :, :], arow_v[:, c * CW:(c + 1) * CW].rearrange("(o h) c -> o h c", o=1)
                                 .to_broadcast([P, H, CW])).then_inc(bc_in, 16)
                hold(sp, passed, maxed, (g * ITEMS + item) * H)
                sp.dma_start(nat[item % 2][:, :], table2[bass.ds(g * GW + dt * P, P), c * CW:(c + 1) * CW])\
                    .then_inc(nat_in[item % 2], 16)

            def store_sums(g, h):
                unit = g * H + h
                hold(sp, passed, acc_free, unit * GT + 2 * GT)
                sp.dma_start(agg_d[h, bass.ds(g * GW, GW), :].rearrange("(t p) c -> p t c", p=P),
                             stage[:, :, :]).then_inc(agg_out, 16)

            def load_terms(g, h, first=False):
                if not first:
                    hold(sp, passed, raw_done, g * STEPS + (h - 1) * TILES + 1)
                rows_g = trow_d[bass.ds(g * (2 * H * GT), 2 * H * GT), :]
                sp.dma_start(t12[h % 2][:, :, :],
                               rows_g.rearrange("(k h t) p -> h k (t p)", k=2, h=H)[h:h + 1, :, :]
                               .to_broadcast([P, 2, GW])).then_inc(t12_in[h % 2], 16)

            def store_terms(g):
                hold(sp, passed, t_copied, g + 1)
                sp.dma_start(trow_d[bass.ds(g * (2 * H * GT), 2 * H * GT), :], trow_t[:, :]).then_inc(t_out, 16)
                hold(sp, passed, t_out, g * 16 + 16)

            def group(g, ahead, first=False):
                for n in range(STEPS):
                    if n % TILES == 4 and n < (H - 1) * TILES:
                        load_terms(g, n // TILES + 1)
                    if ahead and n == COPY:
                        store_terms(g + 1)
                        load_terms(g + 1, 0)
                    if ahead:
                        for item in due.get(n, ()):
                            load_item(g + 1, item)
                    if n == KEEP + 6 and not first:
                        store_sums(g - 1, H - 1)
                    if n % TILES == KEEP + 6 and n > TILES:
                        store_sums(g, n // TILES - 1)

            sp.sem_inc(agg_out, 16)
            sp.sem_inc(maxed, H)
            for item in range(ITEMS):
                load_item(0, item)
            store_terms(0)
            load_terms(0, 0, first=True)
            group(0, True, first=True)
            with sp.Fori(1, G - 1) as g:
                group(g, True)
            group(G - 1, False)
            store_sums(G - 1, H - 1)
            sp.wait_ge(agg_out, 16 * G * H + 16)

        @block.gpsimd
        def _(pool):
            def load_block(g, s):
                hold(pool, passed, L_turned, g * TILES + max(s + 1, 2))
                pool.dma_start(blk[s % 2][:, :, :],
                               table2[bass.ds(g * GW, GW), s * P:(s + 1) * P].rearrange("(t p) c -> p t c", p=P))\
                    .then_inc(blk_in[s % 2], 16)

            pool.sem_inc(L_turned, 2)
            with pool.Fori(0, G) as g:
                for s in range(TILES):
                    load_block(g, s)

        @block.scalar
        def _(act):
            def weigh(g, n):
                h, s = divmod(n, TILES)
                act.wait_ge(masked, g * STEPS + n + 1)
                act.activation(v[n % VS][:, :], v[n % VS][:, :], ACT.Exp,
                               bias=flat[:, s * H + h:s * H + h + 1]).then_inc(w_ready, 1)

            def fill(g, s):
                act.wait_ge(L_turned, g * TILES + s + 3)
                act.activation(L[:, s, :], lt[:, 0:GW], ACT.Copy).then_inc(L_filled, 1)

            def copy_terms(g):
                act.wait_ge(t_turned, g + 1)
                act.wait_ge(t_out, g * 16)
                act.activation(trow_t[:, :], spare[0:2 * H * GT, 0:P], ACT.Copy).then_inc(t_copied, 1)
                act.activation(e_self[:, bass.ds(g * (GT * H), GT * H)], le[:, :], ACT.Exp).then_inc(self_done, 1)

            def group(g, ahead):
                for n in range(STEPS):
                    weigh(g, n)
                    if ahead and n >= STEPS - TILES + 2:
                        fill(g + 1, n - (STEPS - TILES + 2))
                    if ahead and n == COPY:
                        copy_terms(g + 1)
                if ahead:
                    fill(g + 1, TILES - 2)
                    fill(g + 1, TILES - 1)

            for s in range(TILES):
                fill(0, s)
            copy_terms(0)
            act.wait_ge(scaled, 2)
            with act.Fori(0, G - 1) as g:
                group(g, True)
            group(G - 1, False)

        @block.tensor
        def _(pe):
            def turn(g, s):
                ahead = g * 13 + s // 2 if s % 2 == 0 else g * 12 + s // 2
                pe.wait_ge(blk_in[s % 2], ahead * 16 + 16)
                pe.wait_ge(L_filled, g * TILES + s)
                for dt in range(GT):
                    last = pe.transpose(lt[:, dt * P:(dt + 1) * P], blk[s % 2][:, dt, :], ident[:, :])
                last.then_inc(L_turned, 1)

            def turn_terms(g):
                hold(pe, passed, t_math, g * TM + TM)
                pe.transpose(spare[0:2 * H * GT, 0:P], trow[:, :, :, :].rearrange("p k h t -> p (k h t)"),
                             ident[:, :]).then_inc(t_turned, 1)

            def add_up(g, n):
                h, s = divmod(n, TILES)
                pe.wait_ge(w_ready, g * STEPS + n + 1)
                for dt in range(GT):
                    if s == 0:
                        pe.wait_ge(acc_free, (g * H + h) * GT + dt + 1)
                    one = pe.matmul(acc[dt][:, 0:CX], v[n % VS][:, dt * P:(dt + 1) * P], xp[:, s, h, :],
                                    start=s == 0, stop=s == TILES - 1)
                    if dt == GT - 1:
                        one.then_inc(v_used, 1)
                    elif s == TILES - 1:
                        one.then_inc(acc_done, 1)

            def group(g, ahead):
                for n in range(STEPS):
                    add_up(g, n)
                    if ahead and n >= STEPS - TILES:
                        turn(g + 1, n - (STEPS - TILES))
                    if ahead and n == TURN:
                        turn_terms(g + 1)

            pe.sem_inc(acc_free, GT)
            for s in range(TILES):
                turn(0, s)
            turn_terms(0)
            with pe.Fori(0, G - 1) as g:
                group(g, True)
            group(G - 1, False)

        @block.vector
        def _(dve):
            def look(g, item):
                c, dt = divmod(item, GT)
                dve.wait_ge(nat_in[item % 2], (g * (ITEMS // 2) + item // 2 + 1) * 16)
                if dt == 0:
                    dve.wait_ge(bc_in, (g * CH + c + 1) * 16)
                if item == 0:
                    dve.wait_ge(t_copied, g)
                    dve.wait_ge(t_math, g * TM)
                for h in range(H):
                    hold(dve, passed, maxed, (g * ITEMS + item) * H + h + H - 1)
                    dve.tensor_tensor_reduce(out=junk[h % 2], in0=nat[item % 2][:, :], in1=bc[:, h, :],
                                             scale=1.0, scalar=NEG, op0=ALU.add, op1=ALU.max,
                                             accum_out=mpart[:, dt, h, c:c + 1]).then_inc(maxed, 1)

            def finish_terms(g):
                mine = bass.ds(g * (GT * H), GT * H)
                done = [0]

                def then(ins):
                    ins.then_inc(t_math, 1)
                    done[0] += 1
                    dve.wait_ge(t_math, g * TM + done[0])

                dve.wait_ge(maxed, (g + 1) * (ITEMS * H) + H)
                dve.wait_ge(t_turned, g)
                dve.wait_ge(self_done, g)
                then(dve.tensor_reduce(mx[:, :], mpart[:, :, :, :].rearrange("p t h c -> p (t h) c"), AX_X, ALU.max))
                then(dve.tensor_tensor(mx[:, :], mx[:, :], a_src[:, mine], ALU.max))
                then(dve.tensor_tensor(mx[:, :], mx[:, :], a_dst[:, mine], ALU.add))
                then(dve.scalar_tensor_tensor(out=ms[:, :], in0=mx[:, :], scalar=SLOPE0, in1=mx[:, :],
                                              op0=ALU.mult, op1=ALU.max))
                then(dve.tensor_tensor(t1[:, :], a_dst[:, mine], ms[:, :], ALU.subtract))
                then(dve.scalar_tensor_tensor(out=t2[:, :], in0=a_dst[:, mine], scalar=SLOPE0, in1=ms[:, :],
                                              op0=ALU.mult, op1=ALU.subtract))
                then(dve.tensor_tensor(le[:, :], t1[:, :], steep[:, mine], ALU.add))
                then(dve.tensor_tensor(le[:, :], le[:, :], t2[:, :], ALU.max))
                then(dve.tensor_tensor(le[:, :], le[:, :], flat[:, mine], ALU.add))
                for k, t in enumerate((t1, t2)):
                    then(dve.tensor_copy(trow[:, k, :, :], t[:, :].rearrange("p (t h) -> p h t", h=H)))

            def score(g, n):
                h, s = divmod(n, TILES)
                dve.wait_ge(v_used, g * STEPS + n + 1)
                if s == 0:
                    dve.wait_ge(t12_in[h % 2], (g * (H // 2) + h // 2 + 1) * 16)
                dve.scalar_tensor_tensor(out=v[n % VS][:, :], in0=t12[h % 2][:, 0, :],
                                         scalar=steep[:, s * H + h:s * H + h + 1], in1=t12[h % 2][:, 1, :],
                                         op0=ALU.add, op1=ALU.max).then_inc(raw_done, 1)

            def mask(g, n):
                h, s = divmod(n, TILES)
                dve.wait_ge(raw_done, g * STEPS + n + 2)
                if h == 0:
                    dve.wait_ge(L_filled, g * TILES + s + 1)
                dve.tensor_tensor(v[n % VS][:, :], v[n % VS][:, :], L[:, s, :], ALU.add).then_inc(masked, 1)

            def keep_sums(g, h):
                unit = g * H + h
                dve.wait_ge(agg_out, unit * 16 + 16)
                dve.wait_ge(self_done, g + 1)
                for dt in range(GT):
                    if dt < GT - 1:
                        dve.wait_ge(acc_done, unit * (GT - 1) + dt + 1)
                    else:
                        dve.wait_ge(v_used, unit * TILES + TILES + VS)
                    dve.scalar_tensor_tensor(out=stage[:, dt, :], in0=xp[:, g * GT + dt, h, :],
                                             scalar=e_self[:, bass.ds(g * (GT * H) + dt * H + h, 1)],
                                             in1=acc[dt][:, 0:CX], op0=ALU.mult, op1=ALU.add).then_inc(acc_free, 1)

            def group(g, ahead, first=False):
                for n in range(STEPS):
                    if n < STEPS - 1:
                        score(g, n + 1)
                    elif ahead:
                        score(g + 1, 0)
                    mask(g, n)
                    if n == KEEP and not first:
                        keep_sums(g - 1, H - 1)
                    if n % TILES == KEEP and n > TILES:
                        keep_sums(g, n // TILES - 1)
                    if ahead:
                        for item in due.get(n, ()):
                            look(g + 1, item)
                        if n == FINISH:
                            finish_terms(g + 1)

            dve.sem_inc(v_used, VS)
            dve.sem_inc(raw_done, 1)
            dve.tensor_scalar(steep[:, :], a_src[:, :], 1.0 - SLOPE0, None, ALU.mult).then_inc(scaled, 1)
            dve.tensor_scalar(flat[:, :], a_src[:, :], SLOPE0, None, ALU.mult).then_inc(scaled, 1)
            dve.wait_ge(scaled, 2)
            for item in range(ITEMS):
                look(0, item)
            finish_terms(0)
            score(0, 0)
            group(0, True, first=True)
            with dve.Fori(1, G - 1) as g:
                group(g, True)
            group(G - 1, False)
            keep_sums(G - 1, H - 1)


def phase3(nc, x, bias, w1, a1, agg_d, x1_d, alrow_d, low_d, ident, h2, al, ar):
    ctx = ExitStack()
    with ctx:
        def sb(name, shape, dt=F32):
            return ctx.enter_context(nc.sbuf_tensor(name, shape, dt))

        def sem(name):
            return ctx.enter_context(nc.semaphore(name))

        w_sb = sb("w1_sb", [P, KC, D])
        bias_bc = sb("bias_bc", [P, D])
        a_bc = sb("a_bc", [P, 2, D])
        xt = [sb(f"x1t{k}", [P, D]) for k in range(2)]
        sums = [sb(f"sums{k}", [P, H, CX]) for k in range(2)]
        y = sb("y", [P, D])
        ht = [sb(f"h1t{k}", [P, D]) for k in range(2)]
        hT = [sb(f"h1T{k}", [P, KC, P]) for k in range(2)]
        rz = sb("rz", [P, H])
        stats = sb("stats1", [P, 2, 6])
        mv = sb("mv1", [P, 2])
        std = sb("std1", [P, 1])
        rstd = sb("rstd1", [P, 1])
        nbias = sb("nbias1", [P, 1])
        prod = sb("prod1", [P, D])
        alr = [sb(f"alr{k}", [P, 2]) for k in range(2)]
        al_rows = sb("al_rows_sb", [TILES, P])
        eps = sb("eps1", [P, 1])
        low = [sb(f"low{k}", [P, D], F32R) for k in range(2)]
        tp = ctx.enter_context(nc.psum_tensor("tp1", [P, KC * P], F32))
        mm = [ctx.enter_context(nc.psum_tensor(f"mmb{k}", [P, D], F32)) for k in range(2)]

        weights_in = sem("w1_in")
        x_in = [sem(f"xb_in{k}") for k in range(2)]
        x1_done = sem("x1_done")
        x1_out = [sem(f"x1_out{k}") for k in range(2)]
        eps_set = sem("eps_set")
        rz_done = sem("rz_done")
        y_done = sem("y_done")
        stats_done = sem("stats1_done")
        aggr_done = sem("aggr1_done")
        std_done = sem("std1_done")
        rstd_done = sem("rstd1_done")
        norm_done = sem("norm1_done")
        h_done = sem("h1_done")
        h_used = sem("h1_used")
        hT_done = sem("hT1_done")
        mm_done = sem("mm1_done")
        h2_copied = sem("h2_copied")
        scored = sem("scored1")
        low_done = sem("low_done")
        low_out = [sem(f"low_out{k}") for k in range(2)]
        low_free = sem("low_free")
        scores_kept = sem("scores1_kept")
        al_turned = sem("al_turned")
        al_copied = sem("al_copied")
        al_out = sem("al_out")
        passed = sem("passed_phase3")
        block = ctx.enter_context(nc.Block())

        @block.sync
        def _(sp):
            def load(i, k, rounds, size=P):
                hold(sp, passed, h_done, i + 1)
                hold(sp, passed, x1_out[k], rounds * 16)
                sp.dma_start(xt[k][0:size, :], rows(x, i, size)).then_inc(x_in[k], 16)
                sp.dma_start(sums[k][:, :, :], agg_d[:, bass.ds(i * P, P), :].rearrange("h p c -> p h c"))\
                    .then_inc(x_in[k], 16)

            def store(i, k):
                hold(sp, passed, x1_done, i + 1)
                sp.dma_start(rows(x1_d, i), xt[k][:, :]).then_inc(x1_out[k], 16)

            sp.sem_inc(h_done, 2)
            load(0, 0, 0)
            sp.dma_start(bias_bc[:, :], bias.rearrange("(o n) -> o n", o=1).to_broadcast([P, D]))\
                .then_inc(weights_in, 16)
            sp.dma_start(a_bc[:, :, :].rearrange("p k n -> p (k n)"), a1.to_broadcast([P, 2 * D]))\
                .then_inc(weights_in, 16)
            sp.dma_start(w_sb[:, :, :], w1.rearrange("(k p) n -> p k n", p=P)).then_inc(weights_in, 16)
            load(1, 1, 0)
            with sp.Fori(0, TILES // 2 - 1) as r:
                for k in range(2):
                    store(r * 2 + k, k)
                    load(r * 2 + k + 2, k, r + 1)
            store(TILES - 3, 0)
            load(TILES - 1, 0, TILES // 2, TAIL)
            store(TILES - 2, 1)
            store(TILES - 1, 0)
            for k in range(2):
                sp.wait_ge(x1_out[k], 16 * (TILES // 2 + 1 - k))
            sp.wait_ge(al_copied, 1)
            sp.dma_start(alrow_d, al_rows[:, :]).then_inc(al_out, 16)
            sp.wait_ge(al_out, 16)

        @block.gpsimd
        def _(pool):
            def store_low(i, k, rounds):
                hold(pool, passed, low_done, i + 3)
                pool.dma_start(rows(low_d, i), low[k][:, :]).then_inc(low_out[k], 16)
                hold(pool, low_free, low_out[k], rounds * 16)

            pool.sem_inc(low_free, 2)
            with pool.Fori(0, TILES // 2) as r:
                for k in range(2):
                    store_low(r * 2 + k, k, r + 1)
            store_low(TILES - 1, 0, TILES // 2 + 1)

        @block.scalar
        def _(act):
            def normalise(i, k):
                act.wait_ge(aggr_done, i + 1)
                act.activation(std[:, :], mv[:, 1:2], ACT.Sqrt, bias=eps[:, :]).then_inc(std_done, 1)
                act.wait_ge(norm_done, i + 1)
                act.wait_ge(h_used, i + 1)
                act.activation(ht[k][:, :], xt[k][:, :], ACT.Relu, bias=nbias[:, :], scale=rstd[:, :])\
                    .then_inc(h_done, 1)

            def keep_transposed(i, k):
                act.wait_ge(h_used, i + 3)
                act.wait_ge(mm_done, i + 1)
                act.activation(hT[k][:, :, :].rearrange("p k n -> p (k n)"), tp[:, :], ACT.Copy)\
                    .then_inc(hT_done, 1)

            def keep_h2(i, k):
                act.wait_ge(mm_done, i + 3)
                act.activation(h2[:, bass.ds(i * D, D)], mm[k][:, :], ACT.Copy).then_inc(h2_copied, 1)

            act.sem_inc(h_used, 2)
            act.sem_inc(mm_done, 2)
            act.wait_ge(eps_set, 1)
            normalise(0, 0)
            normalise(1, 1)
            keep_transposed(0, 0)
            with act.Fori(0, TILES // 2 - 1) as r:
                i = r * 2
                for k in range(2):
                    keep_transposed(i + k + 1, 1 - k)
                    normalise(i + k + 2, k)
                    keep_h2(i + k, k)
            keep_transposed(TILES - 2, 1)
            normalise(TILES - 1, 0)
            keep_h2(TILES - 3, 0)
            keep_transposed(TILES - 1, 0)
            keep_h2(TILES - 2, 1)
            keep_h2(TILES - 1, 0)
            act.wait_ge(al_turned, 1)
            act.activation(al_rows[:, :], tp[0:TILES, 0:P], ACT.Copy).then_inc(al_copied, 1)

        @block.vector
        def _(dve):
            def finish_layer(i, k, rounds):
                dve.wait_ge(x_in[k], rounds * 32)
                dve.wait_ge(y_done, i * H)
                dve.reciprocal(rz[:, :], sums[k][:, :, C:CX].rearrange("p h c -> p (h c)")).then_inc(rz_done, 1)
                dve.wait_ge(rz_done, i + 1)
                dve.wait_ge(x1_done, i)
                for h in range(H):
                    dve.scalar_tensor_tensor(out=y[:, h * C:(h + 1) * C], in0=sums[k][:, h, 0:C],
                                             scalar=rz[:, h:h + 1], in1=bias_bc[:, h * C:(h + 1) * C],
                                             op0=ALU.mult, op1=ALU.add).then_inc(y_done, 1)
                dve.wait_ge(y_done, i * H + H)
                dve.scalar_tensor_tensor(out=xt[k][:, :], in0=y[:, :], scalar=0.0, in1=xt[k][:, :],
                                         op0=ALU.max, op1=ALU.add).then_inc(x1_done, 1)
                dve.wait_ge(x1_done, i + 1)

            def statistics(i, k):
                for j in range(2):
                    dve.bn_stats(stats[:, j, :], xt[k][:, j * HALF:(j + 1) * HALF]).then_inc(stats_done, 1)
                hold(dve, passed, stats_done, 2 * i + 2)
                dve.bn_aggr(mv[:, :], stats[:, :, :].rearrange("p a b -> p (a b)")).then_inc(aggr_done, 1)
                dve.wait_ge(std_done, i + 1)
                dve.reciprocal(rstd[:, :], std[:, :]).then_inc(rstd_done, 1)
                dve.wait_ge(rstd_done, i + 1)
                dve.scalar_tensor_tensor(out=nbias[:, :], in0=mv[:, 0:1], scalar=-1.0, in1=rstd[:, :],
                                         op0=ALU.mult, op1=ALU.mult).then_inc(norm_done, 1)
                dve.wait_ge(h_done, i + 3)

            def score(i, k):
                dve.wait_ge(h2_copied, i + 1)
                for j in range(2):
                    dve.wait_ge(scored, i * 2 + j)
                    dve.tensor_tensor_reduce(out=prod[:, :], in0=mm[k][:, :], in1=a_bc[:, j, :], scale=1.0,
                                             scalar=0.0, op0=ALU.mult, op1=ALU.add,
                                             accum_out=alr[k][:, j:j + 1]).then_inc(scored, 1)
                dve.wait_ge(scored, i * 2 + 2)
                dve.tensor_copy(al[:, bass.ds(i, 1)], alr[k][:, 0:1]).then_inc(scores_kept, 1)
                dve.tensor_copy(ar[:, bass.ds(i, 1)], alr[k][:, 1:2]).then_inc(scores_kept, 1)
                dve.wait_ge(scores_kept, 2 * i + 2)
                dve.wait_ge(low_free, i + 1)
                dve.tensor_tensor(low[k][:, :], mm[k][:, :], h2[:, bass.ds(i * D, D)].bitcast(F32), ALU.subtract)\
                    .then_inc(low_done, 1)

            dve.memset(eps[:, :], LN_EPS).then_inc(eps_set, 1)
            dve.wait_ge(weights_in, 48)
            for k in range(2):
                finish_layer(k, k, 1)
                statistics(k, k)
            with dve.Fori(0, TILES // 2 - 1) as r:
                for k in range(2):
                    finish_layer(r * 2 + k + 2, k, r + 2)
                    statistics(r * 2 + k + 2, k)
                    score(r * 2 + k, k)
            finish_layer(TILES - 1, 0, TILES // 2 + 1)
            statistics(TILES - 1, 0)
            score(TILES - 3, 0)
            score(TILES - 2, 1)
            score(TILES - 1, 0)

        @block.tensor
        def _(pe):
            def transpose_h(i, k):
                pe.wait_ge(h_done, i + 3)
                pe.wait_ge(hT_done, i)
                for c in range(KC):
                    last = pe.transpose(tp[:, c * P:(c + 1) * P], ht[k][:, c * P:(c + 1) * P], ident[:, :])
                last.then_inc(h_used, 1)

            def project(i, k):
                pe.wait_ge(hT_done, i + 1)
                pe.wait_ge(low_done, i + 1)
                for c in range(KC):
                    for f in range(2):
                        last = pe.matmul(mm[k][:, f * HALF:(f + 1) * HALF], hT[k][:, c, :],
                                         w_sb[:, c, f * HALF:(f + 1) * HALF], start=c == 0, stop=c == KC - 1)
                last.then_inc(mm_done, 1)

            pe.sem_inc(low_done, 2)
            pe.wait_ge(weights_in, 48)
            transpose_h(0, 0)
            with pe.Fori(0, TILES // 2) as r:
                i = r * 2
                for k in range(2):
                    transpose_h(i + k + 1, 1 - k)
                    project(i + k, k)
            project(TILES - 1, 0)
            pe.wait_ge(scores_kept, 2 * TILES)
            pe.wait_ge(hT_done, TILES)
            pe.transpose(tp[0:TILES, 0:P], al[:, :], ident[:, :]).then_inc(al_turned, 1)


def phase4(nc, table2, alrow_d, x1_d, low_d, ident, h2, ar, out):
    STEPS = 2 * TILES
    WS = 5
    LAG = 2
    KEEP, EXP, FINISH = WS, WS + 2, WS + 3
    PAIRS = 2
    RS = 3
    assert STEPS % WS == 0 and STEPS % 2 == 0
    ctx = ExitStack()
    with ctx:
        def sb(name, shape, dt=F32):
            return ctx.enter_context(nc.sbuf_tensor(name, shape, dt))

        def sem(name):
            return ctx.enter_context(nc.semaphore(name))

        neg_al = sb("neg_al", [P, NP])
        neg_flat = sb("neg_flat", [P, NP])
        steep_ar = sb("steep_ar", [P, TILES])
        flat_ar = sb("flat_ar", [P, TILES])
        w = [sb(f"w{k}", [P, GW]) for k in range(WS)]
        w_high = [sb(f"w_high{k}", [P, GW], F32R) for k in range(WS)]
        w_low = [sb(f"w_low{k}", [P, GW], F32R) for k in range(WS)]
        h2_low = [sb(f"h2_low{k}", [P, HALF], F32R) for k in range(WS)]
        raw = [sb(f"raw{k}", [P, GW]) for k in range(2)]
        w_sum = sb("w_sum", [P, GW])
        ones = sb("ones", [P, 1])
        total = sb("total", [P, GT])
        rs = sb("rs", [P, GT])
        neg_rs = sb("neg_rs", [P, GT])
        plus = [sb(f"plus{k}", [P, HALF]) for k in range(2)]
        minus = sb("minus", [P, GT, HALF])
        y = sb("yo", [P, GT, HALF])
        acc = [ctx.enter_context(nc.psum_tensor(f"accb{k}", [P, HALF], F32)) for k in range(GT)]
        acc1 = [ctx.enter_context(nc.psum_tensor(f"accc{k}", [P, HALF], F32)) for k in range(PAIRS)]
        banks = (acc, acc1 + acc[PAIRS:])
        rs_ps = ctx.enter_context(nc.psum_tensor("rs_ps", [P, HALF], F32))

        al_in = sem("al_in")
        consts = sem("consts4")
        L_in = [sem(f"L_in{k}") for k in range(WS)]
        low_in = [sem(f"low_in{k}") for k in range(WS)]
        raw_done = sem("raw4_done")
        masked = sem("masked4")
        w_ready = sem("w4_ready")
        w_summed = sem("w_summed")
        rounded = sem("rounded")
        split = sem("split")
        w_used = sem("w_used")
        acc_done = sem("acc4_done")
        total_done = sem("total_done")
        rs_math = sem("rs_math")
        minus_done = sem("minus_done")
        plus_done = sem("plus_done")
        plus_used = sem("plus_used")
        e_done = sem("e_done")
        x1_in = sem("x1_in")
        y_done = sem("yo_done")
        y_out = sem("y_out")
        passed = sem("passed_phase4")
        block = ctx.enter_context(nc.Block())

        @block.sync
        def _(sp):
            def load_L(g, n):
                dt = n % TILES
                hold(sp, passed, split, g * STEPS + n + 1)
                if WS <= n < TILES + WS:
                    hold(sp, passed, w_summed, g * TILES + n - WS + 1)
                sp.dma_start(w[n % WS][:, :], table2[dt * P:(dt + 1) * P, bass.ds(g * GW, GW)])\
                    .then_inc(L_in[n % WS], 16)

            def load_x1(g, f, last=False):
                hold(sp, passed, y_out, (g * 2 + f) * 16 + (32 if last and f == 1 else 16))
                sp.dma_start(y[:, :, :], x1_d[bass.ds(g * GW, GW), f * HALF:(f + 1) * HALF]
                             .rearrange("(t p) c -> p t c", p=P)).then_inc(x1_in, 16)

            def store(g, f, last=False):
                hold(sp, passed, y_done, g * 2 + f + 1)
                cols = slice(f * HALF, (f + 1) * HALF)
                whole = GT - 1 if last else GT
                sp.dma_start(out[bass.ds(g * GW, whole * P), cols].rearrange("(t p) c -> p t c", p=P),
                             y[:, 0:whole, :]).then_inc(y_out, 16)
                if last:
                    sp.dma_start(out[N - TAIL:N, cols], y[0:TAIL, GT - 1, :]).then_inc(y_out, 16)

            def group(g, first=False, last=False):
                for n in range(STEPS):
                    load_L(g, n)
                    if n == TILES // 2 and not first:
                        store(g - 1, 1)
                    if n == TILES // 2 + 4:
                        load_x1(g, 0)
                    if n == TILES + TILES // 2:
                        store(g, 0, last)
                    if n == TILES + TILES // 2 + 4:
                        load_x1(g, 1, last)

            sp.sem_inc(split, WS)
            sp.sem_inc(y_out, 16)
            sp.dma_start(neg_al[:, :], alrow_d.rearrange("t p -> (t p)").rearrange("(o n) -> o n", o=1)
                         .to_broadcast([P, NP])).then_inc(al_in, 16)
            group(0, first=True)
            with sp.Fori(1, G - 1) as g:
                group(g)
            group(G - 1, last=True)
            store(G - 1, 1, last=True)
            sp.wait_ge(y_out, 16 + 16 * (2 * G + 2))

        @block.gpsimd
        def _(pool):
            with pool.Fori(0, G) as g:
                for n in range(STEPS):
                    f, dt = divmod(n, TILES)
                    hold(pool, passed, w_used, g * STEPS + n + 1)
                    pool.dma_start(h2_low[n % WS][:, :], low_d[dt * P:(dt + 1) * P, f * HALF:(f + 1) * HALF])\
                        .then_inc(low_in[n % WS], 16)

        @block.scalar
        def _(act):
            def weigh(g, n):
                dt = n % TILES
                act.wait_ge(masked, g * STEPS + n + 3)
                act.activation(w[n % WS][:, :], w[n % WS][:, :], ACT.Exp, bias=flat_ar[:, dt:dt + 1])\
                    .then_inc(w_ready, 1)

            def round_weights(g, n):
                act.wait_ge(w_ready, g * STEPS + n + 1)
                act.wait_ge(w_used, g * STEPS + n + 1)
                act.activation(w_high[n % WS][:, :], w[n % WS][:, :], ACT.Copy).then_inc(rounded, 1)

            def keep(g, f):
                unit = g * 2 + f
                act.wait_ge(rs_math, g * RS + RS + 1)
                act.wait_ge(y_done, unit)
                for st in range(GT):
                    if st < GT - 1:
                        act.wait_ge(acc_done, unit * (GT - 1) + st + 1)
                    else:
                        act.wait_ge(w_used, unit * TILES + TILES + WS)
                    bank = banks[f][st]
                    act.activation(minus[:, st, :], bank[:, :], ACT.Relu, scale=neg_rs[:, st:st + 1])\
                        .then_inc(minus_done, 1)
                    act.wait_ge(plus_used, unit * GT + st + 1)
                    act.activation(plus[(f * GT + st) % 2][:, :], bank[:, :], ACT.Relu, scale=rs[:, st:st + 1])\
                        .then_inc(plus_done, 1)

            def exp_minus(unit):
                act.wait_ge(minus_done, unit * GT + GT)
                act.activation(minus[:, :, :], minus[:, :, :], ACT.Exp, scale=-1.0).then_inc(e_done, 1)

            def group(g, first=False):
                for n in range(STEPS):
                    weigh(g, n)
                    if n == TILES + KEEP:
                        keep(g, 0)
                    if n == KEEP and not first:
                        keep(g - 1, 1)
                    if n > 0 or not first:
                        round_weights(g, n - 1)
                    if n == EXP and not first:
                        exp_minus(g * 2 - 1)
                    if n == TILES + EXP:
                        exp_minus(g * 2)

            act.sem_inc(plus_used, 2)
            act.wait_ge(consts, 5)
            group(0, first=True)
            with act.Fori(1, G) as g:
                group(g)
            round_weights(G - 1, STEPS - 1)
            keep(G - 1, 1)
            exp_minus(2 * G - 1)

        @block.vector
        def _(dve):
            def score(g, n):
                dt = n % TILES
                cols = bass.ds(g * GW, GW)
                dve.wait_ge(masked, g * STEPS + n + 1)
                dve.scalar_tensor_tensor(out=raw[n % 2][:, :], in0=neg_al[:, cols], scalar=steep_ar[:, dt:dt + 1],
                                         in1=neg_flat[:, cols], op0=ALU.add, op1=ALU.min).then_inc(raw_done, 1)

            def mask(g, n):
                dve.wait_ge(raw_done, g * STEPS + n + 1)
                dve.wait_ge(L_in[n % WS], (g * (STEPS // WS) + n // WS + 1) * 16)
                dve.tensor_tensor(w[n % WS][:, :], w[n % WS][:, :], raw[n % 2][:, :], ALU.add).then_inc(masked, 1)

            def sum_weights(g, n):
                dve.wait_ge(w_ready, g * STEPS + n + 1)
                if n == 0:
                    dve.wait_ge(total_done, g)
                    dve.tensor_copy(w_sum[:, :], w[0][:, :]).then_inc(w_summed, 1)
                else:
                    dve.wait_ge(w_summed, g * TILES + n)
                    dve.tensor_tensor(w_sum[:, :], w_sum[:, :], w[n % WS][:, :], ALU.add).then_inc(w_summed, 1)

            def split_weights(g, n):
                dve.wait_ge(rounded, g * STEPS + n + 1)
                dve.tensor_tensor(w_low[n % WS][:, :], w[n % WS][:, :], w_high[n % WS][:, :].bitcast(F32),
                                  ALU.subtract).then_inc(split, 1)

            def invert_total(g):
                dve.wait_ge(total_done, g + 1)
                dve.wait_ge(plus_done, g * 2 * GT + 2 * GT)
                dve.tensor_scalar(total[:, :], rs_ps[:, 0:GT], SUM_EPS, None, ALU.add).then_inc(rs_math, 1)
                dve.wait_ge(rs_math, g * RS + 2)
                dve.reciprocal(rs[:, :], total[:, :]).then_inc(rs_math, 1)
                dve.wait_ge(rs_math, g * RS + 3)
                dve.tensor_scalar(neg_rs[:, :], rs[:, :], -1.0, None, ALU.mult).then_inc(rs_math, 1)

            def add_plus(unit, f):
                dve.wait_ge(x1_in, unit * 16 + 16)
                for st in range(GT):
                    dve.wait_ge(plus_done, unit * GT + st + 1 + 2 * GT)
                    dve.tensor_tensor(y[:, st, :], y[:, st, :], plus[(f * GT + st) % 2][:, :], ALU.add)\
                        .then_inc(plus_used, 1)

            def finish(unit):
                dve.wait_ge(e_done, unit + 1)
                dve.wait_ge(plus_used, unit * GT + GT + 2)
                dve.scalar_tensor_tensor(out=y[:, :, :], in0=minus[:, :, :], scalar=-1.0, in1=y[:, :, :],
                                         op0=ALU.add, op1=ALU.add).then_inc(y_done, 1)

            def group(g, first=False):
                score(g, 0)
                for n in range(STEPS):
                    if n < STEPS - 1:
                        score(g, n + 1)
                    mask(g, n)
                    if LAG <= n < TILES + LAG:
                        sum_weights(g, n - LAG)
                    if n >= LAG or not first:
                        split_weights(g, n - LAG)
                    if n == TILES + KEEP:
                        invert_total(g)
                        add_plus(g * 2, 0)
                    if n == TILES + FINISH:
                        finish(g * 2)
                    if n == KEEP and not first:
                        add_plus(g * 2 - 1, 1)
                    if n == FINISH and not first:
                        finish(g * 2 - 1)

            dve.sem_inc(masked, 2)
            dve.sem_inc(rs_math, 1)
            dve.memset(ones[:, :], 1.0).then_inc(consts, 1)
            dve.tensor_scalar(steep_ar[:, :], ar[:, :], SLOPE1 - 1.0, None, ALU.mult).then_inc(consts, 1)
            dve.tensor_scalar(flat_ar[:, :], ar[:, :], -SLOPE1, None, ALU.mult).then_inc(consts, 1)
            dve.wait_ge(al_in, 16)
            dve.tensor_scalar(neg_flat[:, :], neg_al[:, :], -SLOPE1, None, ALU.mult).then_inc(consts, 1)
            dve.wait_ge(consts, 4)
            dve.tensor_scalar(neg_al[:, :], neg_al[:, :], -1.0, None, ALU.mult).then_inc(consts, 1)
            dve.wait_ge(consts, 5)
            group(0, first=True)
            with dve.Fori(1, G) as g:
                group(g)
            for n in range(STEPS - LAG, STEPS):
                split_weights(G - 1, n)
            add_plus(2 * G - 1, 1)
            finish(2 * G - 1)

        @block.tensor
        def _(pe):
            def add_up(g, n):
                f, dt = divmod(n, TILES)
                pe.wait_ge(split, g * STEPS + n + 1 + WS)
                pe.wait_ge(low_in[n % WS], (g * (STEPS // WS) + n // WS + 1) * 16)
                cols = slice(dt * D + f * HALF, dt * D + (f + 1) * HALF)
                for st in range(GT):
                    if dt == 0:
                        pe.wait_ge(plus_done, (g * 2 + f) * GT + st + 1 + (0 if st < PAIRS else GT))
                    bank = banks[f][st]
                    mine = slice(st * P, (st + 1) * P)
                    pe.matmul(bank[:, :], w_high[n % WS][:, mine], h2[:, cols], start=dt == 0, stop=False)
                    pe.matmul(bank[:, :], w_high[n % WS][:, mine], h2_low[n % WS][:, :], start=False, stop=False)
                    one = pe.matmul(bank[:, :], w_low[n % WS][:, mine], h2[:, cols],
                                    start=False, stop=dt == TILES - 1)
                    if st == GT - 1:
                        one.then_inc(w_used, 1)
                    elif dt == TILES - 1:
                        one.then_inc(acc_done, 1)

            def sum_total(g):
                pe.wait_ge(w_summed, g * TILES + TILES)
                pe.wait_ge(rs_math, g * RS + 1)
                for st in range(GT):
                    one = pe.matmul(rs_ps[:, st:st + 1], w_sum[:, st * P:(st + 1) * P], ones[:, :],
                                    start=True, stop=True)
                one.then_inc(total_done, 1)

            def group(g):
                for n in range(STEPS):
                    if n == TILES - 1:
                        sum_total(g)
                    add_up(g, n)

            pe.sem_inc(plus_done, 2 * GT)
            pe.sem_inc(w_used, WS)
            pe.wait_ge(consts, 5)
            with pe.Fori(0, G) as g:
                group(g)


_INS = ["x", "src", "dst", "L0_gnn_W", "L0_gnn_att_src", "L0_gnn_att_dst", "L0_gnn_bias",
        "L1_gnn_W", "L1_gnn_a"]


def kernel(**inputs):
    import numpy as _np
    import concourse.bacc as _bacc
    from concourse import mybir as _mybir
    from concourse.bass_utils import run_bass_kernel_spmd as _run

    nc = _bacc.Bacc("TRN2", target_bir_lowering=False, num_devices=1)
    arrays, args = {}, []
    for name in _INS:
        a = _np.ascontiguousarray(inputs[name])
        arrays[f"in_{name}_dram"] = a
        args.append(nc.dram_tensor(f"in_{name}_dram", a.shape, _mybir.dt.from_np(a.dtype), kind="ExternalInput").ap())
    out = nc.dram_tensor("out_0_dram", (N, D), _mybir.dt.float32, kind="ExternalOutput").ap()
    build(nc, *args, out)
    r = _run(nc, [arrays], core_ids=[0])
    return r.results[0]["out_0_dram"]
```

```python
from contextlib import ExitStack

import concourse.bass as bass
from concourse import mybir

F32 = mybir.dt.float32
F32R = mybir.dt.float32r
BF16 = mybir.dt.bfloat16
U32 = mybir.dt.uint32
I32 = mybir.dt.int32
ALU = mybir.AluOpType
ACT = mybir.ActivationFunctionType
AX_X = mybir.AxisListType.X

P = 128
N = 3125
D = 1024
H = 4
C = D // H
E = 50000
SLOPE0 = 0.2
SLOPE1 = 0.1
LN_EPS = 1e-5
SUM_EPS = 1e-5
NEG = -1.0e30

TILES = -(-N // P)
NP = TILES * P
TAIL = N - (TILES - 1) * P
KC = D // P
HALF = 512
CX = C + 1

GT = 5
G = TILES // GT
GW = GT * P

EP = 125
ER = E // EP
HALO = 49
EX = HALO + ER + HALO
OOB = float(1 << 25)
LOAD_AFTER = 18
EB = 20

assert TILES == G * GT and EP * ER == E and ER % (2 * EB) == 0 and HALO % 2 == 1


def rows(table, tile, size=P):
    return table[bass.ds(tile * P, size), :]


def hold(eng, passed, sem, value):
    eng.wait_ge(sem, value)
    eng.sem_inc(passed, 1)


def build(nc, x, src, dst, w0, att_src, att_dst, bias, w1, a1, out):
    counts = nc.dram_tensor("counts", [NP * NP, 1], F32, kind="Internal").ap()
    table = nc.dram_tensor("edge_table", [NP * NP, 1], F32, kind="Internal").ap()
    table2 = table.rearrange("(d s) o -> d (s o)", s=NP)
    arow_d = nc.dram_tensor("a_src_rows", [H * TILES, P], F32, kind="Internal").ap()
    trow_d = nc.dram_tensor("dst_term_rows", [G * 2 * H * GT, P], F32, kind="Internal").ap()
    agg_d = nc.dram_tensor("attention_sums", [H, NP, CX], F32, kind="Internal").ap()
    x1_d = nc.dram_tensor("x1", [NP, D], F32, kind="Internal").ap()
    alrow_d = nc.dram_tensor("al_rows", [TILES, P], F32, kind="Internal").ap()
    low_d = nc.dram_tensor("h2_low", [NP, D], F32R, kind="Internal").ap()
    ctx = ExitStack()
    with ctx:
        ident = ctx.enter_context(nc.sbuf_tensor("ident", [P, P], F32))
        crowded = ctx.enter_context(nc.sbuf_tensor("crowded", [P, 1], I32))
        with ExitStack() as both:
            xp = both.enter_context(nc.sbuf_tensor("xp", [P, TILES, H, CX], F32))
            a_src = both.enter_context(nc.sbuf_tensor("a_src", [P, TILES * H], F32))
            a_dst = both.enter_context(nc.sbuf_tensor("a_dst", [P, TILES * H], F32))
            with ExitStack() as edges:
                key = edges.enter_context(nc.sbuf_tensor("key", [P, EX], F32))
                phase1(nc, x, src, dst, w0, att_src, att_dst, table, table2, arow_d,
                       ident, xp, a_src, a_dst, key, crowded)
                any_edges(nc, table, counts, ident, key, crowded)
            phase2(nc, table2, arow_d, trow_d, agg_d, ident, xp, a_src, a_dst)
        with ExitStack() as both:
            h2 = both.enter_context(nc.sbuf_tensor("h2", [P, TILES * D], F32R))
            al = both.enter_context(nc.sbuf_tensor("al", [P, TILES], F32))
            ar = both.enter_context(nc.sbuf_tensor("ar", [P, TILES], F32))
            phase3(nc, x, bias, w1, a1, agg_d, x1_d, alrow_d, low_d, ident, h2, al, ar)
            phase4(nc, table2, alrow_d, x1_d, low_d, ident, h2, ar, out)


def phase1(nc, x, src, dst, w0, att_src, att_dst, table, table2, arow_d,
           ident, xp, a_src, a_dst, key, crowded):
    ctx = ExitStack()
    with ctx:
        def sb(name, shape, dt=F32):
            return ctx.enter_context(nc.sbuf_tensor(name, shape, dt))

        def sem(name):
            return ctx.enter_context(nc.semaphore(name))

        w_sb = sb("w0_sb", [P, KC, D])
        att_bc = sb("att_bc", [P, 2, D])
        xt = [sb(f"xt{k}", [P, D]) for k in range(2)]
        ht = [sb(f"ht{k}", [P, D]) for k in range(2)]
        hT = [sb(f"hT{k}", [P, KC, P]) for k in range(2)]
        stats = sb("stats", [P, 2, 6])
        mv = sb("mv", [P, 2])
        std = sb("std", [P, 1])
        rstd = sb("rstd", [P, 1])
        nbias = sb("nbias", [P, 1])
        prod = sb("prod", [P, C])
        asd = [sb(f"asd{k}", [P, 2, H]) for k in range(2)]
        a_hm = sb("a_hm", [P, H * TILES])
        a_rows = sb("a_rows", [H * TILES, P])
        neg = sb("neg", [P, 1, GW])
        e_src = sb("e_src", [P, EX], I32)
        e_dst = sb("e_dst", [P, EX], I32)
        equal = [sb(f"equal{k}", [P, HALO + ER], BF16) for k in range(2)]
        later = sb("later", [P, ER], BF16)
        before = sb("before", [P, ER], BF16)
        back = sb("back", [P, 2, ER])
        bad = sb("bad", [P, 1])
        bad_all = sb("bad_all", [P, 1])
        lnc = sb("lnc", [P, ER])
        skip = sb("skip", [P, ER])
        idx = sb("idx", [P, ER], U32)
        idx_st = [sb(f"idx_st{k}", [P, EB], U32) for k in range(2)]
        lnc_st = [sb(f"lnc_st{k}", [P, EB]) for k in range(2)]
        eps = sb("eps", [P, 1])

        tp = ctx.enter_context(nc.psum_tensor("tp", [P, KC * P], F32))
        mm = [ctx.enter_context(nc.psum_tensor(f"mm{k}", [P, D], F32)) for k in range(2)]

        edges_in = sem("edges_in")
        weights_in = sem("weights_in")
        x_in = [sem(f"x_in{k}") for k in range(2)]
        neg_set = sem("neg_set")
        ones_set = sem("ones_set")
        table_clear = [sem(f"table_clear{k}") for k in range(2)]
        consts = sem("consts")
        stats_done = sem("stats_done")
        aggr_done = sem("aggr_done")
        std_done = sem("std_done")
        rstd_done = sem("rstd_done")
        norm_done = sem("norm_done")
        h_done = sem("h_done")
        h_used = sem("h_used")
        hT_done = sem("hT_done")
        mm_done = sem("mm_done")
        xp_copied = sem("xp_copied")
        scored = sem("scored")
        scores_kept = sem("scores_kept")
        a_hm_done = sem("a_hm_done")
        a_T_done = sem("a_T_done")
        a_rows_done = sem("a_rows_done")
        a_rows_out = sem("a_rows_out")
        pads_set = sem("pads_set")
        key_done = sem("key_done")
        compared = sem("compared")
        tallied = sem("tallied")
        edge_math = sem("edge_math")
        bad_set = sem("bad_set")
        bad_done = sem("bad_done")
        bad_summed = sem("bad_summed")
        ln_in = sem("ln_in")
        ln_done = sem("ln_done")
        idx_done = sem("idx_done")
        staged = sem("staged")
        lnc_out = [sem(f"lnc_out{k}") for k in range(2)]
        passed = sem("passed_phase1")
        block = ctx.enter_context(nc.Block())

        @block.sync
        def _(sp):
            sp.sem_inc(h_done, 2)
            sp.wait_ge(pads_set, 2)
            for e_sb, e_in in ((e_dst, dst), (e_src, src)):
                near = e_in.rearrange("(p t) -> p t", t=ER)
                sp.dma_start(e_sb[0:EP, HALO:HALO + ER], near).then_inc(edges_in, 16)
                sp.dma_start(e_sb[1:EP, 0:HALO], near[0:EP - 1, ER - HALO:ER]).then_inc(edges_in, 16)
                sp.dma_start(e_sb[0:EP - 1, HALO + ER:EX], near[1:EP, 0:HALO]).then_inc(edges_in, 16)
            def load(i, k, size=P):
                hold(sp, passed, h_done, i + 1)
                sp.dma_start(xt[k][0:size, :], rows(x, i, size)).then_inc(x_in[k], 16)

            sp.wait_ge(table_clear[0], 16 * LOAD_AFTER)
            for k in range(2):
                load(k, k)
            sp.dma_start(w_sb[:, :, :], w0.rearrange("(k p) n -> p k n", p=P)).then_inc(weights_in, 16)
            for k, att in enumerate((att_src, att_dst)):
                sp.dma_start(att_bc[:, k, :],
                             att.rearrange("h c -> (h c)").rearrange("(o n) -> o n", o=1).to_broadcast([P, D]))\
                    .then_inc(weights_in, 16)
            with sp.Fori(1, TILES // 2) as r:
                i = r * 2
                for k in range(2):
                    load(i + k, k)
            load(TILES - 1, 0, TAIL)
            sp.wait_ge(a_rows_done, 1)
            sp.dma_start(arow_d, a_rows[:, :]).then_inc(a_rows_out, 16)
            sp.wait_ge(a_rows_out, 16)

        @block.gpsimd
        def _(pool):
            pool.memset(neg[:, :, :], NEG).then_inc(neg_set, 1)
            pool.memset(ident[:, :], 0.0).then_inc(consts, 1)
            pool.wait_ge(consts, 1)
            pool.affine_select(out=ident[:, :], in_=ident[:, :], compare_op=ALU.not_equal, fill=1.0,
                               base=0, pattern=[[-1, P]], channel_multiplier=1).then_inc(consts, 1)
            pool.wait_ge(bad_done, 1)
            pool.partition_all_reduce(bad_all[:, :], bad[:, :], P, bass.bass_isa.ReduceOp.add)\
                .then_inc(bad_summed, 1)

            pool.wait_ge(table_clear[0], 16 * LOAD_AFTER)
            pool.wait_ge(table_clear[1], 16 * (TILES - LOAD_AFTER))
            pool.wait_ge(idx_done, 1)
            pool.wait_ge(ln_done, 2)

            def write_counts(b, k):
                cols = bass.ds(b * EB, EB)
                pool.tensor_copy(idx_st[k][:, :], idx[:, cols]).then_inc(staged, 1)
                pool.tensor_copy(lnc_st[k][:, :], lnc[:, cols]).then_inc(staged, 1)
                hold(pool, passed, staged, 2 * b + 2)
                for j in range(EB):
                    pool.indirect_dma_start(
                        out=table, out_offset=bass.IndirectOffsetOnAxis(ap=idx_st[k][:, j:j + 1], axis=0),
                        in_=lnc_st[k][:, j:j + 1], in_offset=None,
                        bounds_check=NP * NP - 1, oob_is_err=False).then_inc(lnc_out[k], 16)

            blocks = ER // EB
            for k in range(2):
                write_counts(k, k)
            with pool.Fori(1, blocks // 2) as r:
                b = r * 2
                for k in range(2):
                    hold(pool, passed, lnc_out[k], b * (8 * EB))
                    write_counts(b + k, k)
            for k in range(2):
                pool.wait_ge(lnc_out[k], ER * 8)

        @block.scalar
        def _(act):
            def normalise(i, k):
                act.wait_ge(aggr_done, i + 1)
                act.activation(std[:, :], mv[:, 1:2], ACT.Sqrt, bias=eps[:, :]).then_inc(std_done, 1)
                act.wait_ge(norm_done, i + 1)
                act.wait_ge(h_used, i + 1)
                act.activation(ht[k][:, :], xt[k][:, :], ACT.Relu, bias=nbias[:, :], scale=rstd[:, :])\
                    .then_inc(h_done, 1)

            def keep_transposed(i, k):
                act.wait_ge(h_used, i + 3)
                act.wait_ge(mm_done, i + 1)
                act.activation(hT[k][:, :, :].rearrange("p k n -> p (k n)"), tp[:, :], ACT.Copy)\
                    .then_inc(hT_done, 1)

            def keep_xp(i, k):
                act.wait_ge(scores_kept, 2 * i + 2)
                act.activation(xp[:, i, :, 0:C], mm[k][:, :].rearrange("p (h c) -> p h c", h=H), ACT.Copy)\
                    .then_inc(xp_copied, 1)

            act.sem_inc(h_used, 2)
            act.sem_inc(mm_done, 2)
            act.wait_ge(neg_set, 1)
            for start, end, part in ((0, LOAD_AFTER, 0), (LOAD_AFTER, TILES, 1)):
                with act.Fori(start, end) as i:
                    act.dma_start(rows(table2, i).rearrange("p (g w) -> p g w", w=GW),
                                  neg[:, :, :].to_broadcast([P, G, GW])).then_inc(table_clear[part], 16)
            act.wait_ge(ln_in, 1)
            act.activation(lnc[:, :], lnc[:, :], ACT.Ln).then_inc(ln_done, 1)
            act.wait_ge(ones_set, 2)
            normalise(0, 0)
            normalise(1, 1)
            keep_transposed(0, 0)
            with act.Fori(0, TILES // 2 - 1) as r:
                i = r * 2
                for k in range(2):
                    keep_transposed(i + k + 1, 1 - k)
                    normalise(i + k + 2, k)
                    keep_xp(i + k, k)
            keep_transposed(TILES - 2, 1)
            normalise(TILES - 1, 0)
            keep_xp(TILES - 3, 0)
            keep_transposed(TILES - 1, 0)
            keep_xp(TILES - 2, 1)
            keep_xp(TILES - 1, 0)
            act.wait_ge(a_T_done, 1)
            act.activation(a_rows[:, :], tp[0:H * TILES, 0:P], ACT.Copy).then_inc(a_rows_done, 1)

        @block.vector
        def _(dve):
            dve.memset(e_dst[:, :], -1).then_inc(pads_set, 1)
            dve.memset(e_src[:, :], -1).then_inc(pads_set, 1)
            dve.memset(later[:, :], 0.0).then_inc(tallied, 1)
            dve.memset(before[:, :], 0.0).then_inc(tallied, 1)
            dve.memset(xp[:, :, :, C:CX], 1.0).then_inc(ones_set, 1)
            dve.memset(eps[:, :], LN_EPS).then_inc(ones_set, 1)
            def statistics(i, k, rounds):
                dve.wait_ge(x_in[k], rounds * 16)
                for j in range(2):
                    dve.bn_stats(stats[:, j, :], xt[k][:, j * HALF:(j + 1) * HALF]).then_inc(stats_done, 1)
                hold(dve, passed, stats_done, 2 * i + 2)
                dve.bn_aggr(mv[:, :], stats[:, :, :].rearrange("p a b -> p (a b)")).then_inc(aggr_done, 1)
                dve.wait_ge(std_done, i + 1)
                dve.reciprocal(rstd[:, :], std[:, :]).then_inc(rstd_done, 1)
                dve.wait_ge(rstd_done, i + 1)
                dve.scalar_tensor_tensor(out=nbias[:, :], in0=mv[:, 0:1], scalar=-1.0, in1=rstd[:, :],
                                         op0=ALU.mult, op1=ALU.mult).then_inc(norm_done, 1)
                dve.wait_ge(h_done, i + 3)

            def score(i, k):
                dve.wait_ge(mm_done, i + 3)
                for h in range(H):
                    for j in range(2):
                        dve.tensor_tensor_reduce(out=prod[:, :], in0=mm[k][:, h * C:(h + 1) * C],
                                                 in1=att_bc[:, j, h * C:(h + 1) * C], scale=1.0, scalar=0.0,
                                                 op0=ALU.mult, op1=ALU.add, accum_out=asd[k][:, j, h:h + 1])\
                            .then_inc(scored, 1)
                        dve.wait_ge(scored, i * (2 * H) + 2 * h + j + 1)
                dve.tensor_copy(a_src[:, bass.ds(i * H, H)], asd[k][:, 0, :]).then_inc(scores_kept, 1)
                dve.tensor_copy(a_dst[:, bass.ds(i * H, H)], asd[k][:, 1, :]).then_inc(scores_kept, 1)

            mine = slice(HALO, HALO + ER)

            def compare(k, slot):
                dve.tensor_tensor(equal[slot][:, :], key[:, 0:HALO + ER], key[:, bass.ds(k, HALO + ER)],
                                  ALU.is_equal).then_inc(compared, 1)

            def tally(k, slot):
                dve.wait_ge(compared, k)
                dve.wait_ge(tallied, k * 2)
                dve.tensor_tensor(later[:, :], later[:, :], equal[slot][:, mine], ALU.add).then_inc(tallied, 1)
                dve.tensor_tensor(before[:, :], before[:, :], equal[slot][:, bass.ds(k * -1 + HALO, ER)],
                                  ALU.add).then_inc(tallied, 1)

            def two_comparisons(r):
                k = r * 2 + 1
                for j in range(2):
                    dve.wait_ge(tallied, (k + j) * 2)
                    compare(k + j + 1, 1 - j)
                    tally(k + j, j)

            def index_edges():
                dve.tensor_tensor(back[:, 0, :], e_dst[:, mine], e_dst[:, HALO - 1:HALO + ER - 1],
                                  ALU.subtract).then_inc(edge_math, 1)
                dve.tensor_tensor(back[:, 1, :], e_dst[:, mine], e_dst[:, 0:ER],
                                  ALU.subtract).then_inc(edge_math, 1)
                dve.wait_ge(edge_math, 2)
                dve.tensor_scalar(back[:, 0, :], back[:, 0, :], 0.0, None, ALU.is_lt).then_inc(edge_math, 1)
                dve.tensor_scalar(back[:, 1, :], back[:, 1, :], 1.0, None, ALU.is_lt).then_inc(edge_math, 1)
                dve.wait_ge(edge_math, 4)
                dve.tensor_reduce(bad[0:EP, :], back[0:EP, :, :].rearrange("p a b -> p (a b)"), AX_X, ALU.max)\
                    .then_inc(bad_done, 1)
                dve.wait_ge(bad_done, 1)
                dve.wait_ge(tallied, 2 * HALO)
                dve.tensor_scalar(lnc[:, :], later[:, :], 1.0, None, ALU.add).then_inc(ln_in, 1)
                dve.tensor_scalar(back[:, 0, :], key[:, mine], 0.0, None, ALU.is_lt).then_inc(edge_math, 1)
                dve.wait_ge(edge_math, 5)
                dve.tensor_tensor(back[:, 0, :], back[:, 0, :], before[:, :], ALU.add).then_inc(edge_math, 1)
                dve.wait_ge(bad_summed, 1)
                dve.wait_ge(edge_math, 6)
                dve.tensor_scalar(back[:, 0, :], back[:, 0, :], bad_all[:, :], None, ALU.add)\
                    .then_inc(edge_math, 1)
                dve.tensor_copy(crowded[:, :], bad_all[:, :]).then_inc(edge_math, 1)
                dve.wait_ge(edge_math, 8)
                dve.tensor_scalar(skip[:, :], back[:, 0, :], 0.0, OOB, ALU.is_gt, ALU.mult)\
                    .then_inc(edge_math, 1)
                dve.wait_ge(edge_math, 9)
                dve.tensor_tensor(idx[:, :], skip[:, :], key[:, mine], ALU.add).then_inc(idx_done, 1)
                dve.wait_ge(ln_done, 1)
                dve.scalar_tensor_tensor(out=lnc[:, :], in0=later[:, :], scalar=0.5, in1=lnc[:, :],
                                         op0=ALU.is_gt, op1=ALU.mult).then_inc(ln_done, 1)

            dve.memset(bad[:, :], 0.0).then_inc(bad_set, 1)
            dve.wait_ge(bad_set, 1)
            dve.wait_ge(edges_in, 96)
            dve.scalar_tensor_tensor(out=key[:, :], in0=e_dst[:, :], scalar=float(NP), in1=e_src[:, :],
                                     op0=ALU.mult, op1=ALU.add).then_inc(key_done, 1)
            dve.wait_ge(key_done, 1)
            compare(1, 0)
            with dve.Fori(0, HALO // 2) as r:
                two_comparisons(r)
            index_edges()
            statistics(0, 0, 1)
            statistics(1, 1, 1)
            dve.wait_ge(weights_in, 48)
            with dve.Fori(0, TILES // 2 - 1) as r:
                for k in range(2):
                    statistics(r * 2 + k + 2, k, r + 2)
                    score(r * 2 + k, k)
            statistics(TILES - 1, 0, TILES // 2 + 1)
            score(TILES - 3, 0)
            score(TILES - 2, 1)
            score(TILES - 1, 0)
            dve.wait_ge(scores_kept, 2 * TILES)
            dve.tensor_copy(a_hm[:, :].rearrange("p (h t) -> p h t", h=H),
                            a_src[:, :].rearrange("p (t h) -> p h t", h=H)).then_inc(a_hm_done, 1)

        @block.tensor
        def _(pe):
            def transpose_h(i, k):
                pe.wait_ge(h_done, i + 3)
                pe.wait_ge(hT_done, i)
                for c in range(KC):
                    last = pe.transpose(tp[:, c * P:(c + 1) * P], ht[k][:, c * P:(c + 1) * P], ident[:, :])
                last.then_inc(h_used, 1)

            def project(i, k):
                pe.wait_ge(hT_done, i + 1)
                pe.wait_ge(xp_copied, i + 1)
                for c in range(KC):
                    for f in range(2):
                        last = pe.matmul(mm[k][:, f * HALF:(f + 1) * HALF], hT[k][:, c, :],
                                         w_sb[:, c, f * HALF:(f + 1) * HALF], start=c == 0, stop=c == KC - 1)
                last.then_inc(mm_done, 1)

            pe.sem_inc(xp_copied, 2)
            pe.wait_ge(consts, 2)
            pe.wait_ge(weights_in, 48)
            transpose_h(0, 0)
            with pe.Fori(0, TILES // 2) as r:
                i = r * 2
                for k in range(2):
                    transpose_h(i + k + 1, 1 - k)
                    project(i + k, k)
            project(TILES - 1, 0)
            pe.wait_ge(a_hm_done, 1)
            pe.wait_ge(hT_done, TILES)
            pe.transpose(tp[0:H * TILES, 0:P], a_hm[:, :], ident[:, :]).then_inc(a_T_done, 1)


def any_edges(nc, table, counts, ident, key, crowded):
    with ExitStack() as ctx:
        flag = nc.values_load(crowded[0:1, 0:1], min_val=0, max_val=P)
        ctx.enter_context(nc.If(flag > 0))
        ctx.enter_context(ExitStack())

        def sb(name, shape, dt=F32):
            return ctx.enter_context(nc.sbuf_tensor(name, shape, dt))

        def sem(name):
            return ctx.enter_context(nc.semaphore(name))

        zeros = sb("zeros", [P, NP])
        below = sb("below", [P, P])
        col = sb("col", [P, 1])
        spread = sb("spread", [P, P])
        same = sb("same", [P, P])
        same_low = sb("same_low", [P, P])
        times = sb("times", [P, 1])
        first = sb("first", [P, 1])
        skip1 = sb("skip1", [P, 1])
        idx1 = sb("idx1", [P, 1], U32)
        seen = sb("seen", [P, 1])
        ln_seen = sb("ln_seen", [P, 1])
        turned = ctx.enter_context(nc.psum_tensor("turned", [P, P], F32))
        set_up = sem("set_up")
        zeroed = sem("zeroed")
        col_math = sem("col_math")
        turned_done = sem("turned_done")
        idx_ready = sem("idx_ready")
        seen_clear = sem("seen_clear")
        seen_in = sem("seen_in")
        seen_done = sem("seen_done")
        ln_seen_done = sem("ln_seen_done")
        written = sem("written")
        col_written = sem("col_written")
        passed = sem("passed_any_edges")
        block = ctx.enter_context(nc.Block())

        @block.sync
        def _(sp):
            sp.wait_ge(set_up, 1)
            with sp.Fori(0, TILES) as i:
                sp.dma_start(rows(counts.rearrange("(d s) o -> d (s o)", s=NP), i), zeros[:, :])\
                    .then_inc(zeroed, 16)

        @block.gpsimd
        def _(pool):
            pool.memset(zeros[:, :], 0.0).then_inc(set_up, 1)
            pool.memset(below[:, :], 1.0).then_inc(set_up, 1)
            pool.wait_ge(set_up, 2)
            pool.affine_select(out=below[:, :], in_=below[:, :], compare_op=ALU.is_gt, fill=0.0,
                               base=0, pattern=[[-1, P]], channel_multiplier=1).then_inc(set_up, 1)
            pool.sem_inc(col_written, 1)
            pool.wait_ge(zeroed, 16 * TILES)

            with pool.Fori(0, ER) as c:
                pool.memset(seen[:, :], 0.0).then_inc(seen_clear, 1)
                hold(pool, passed, seen_clear, c + 1)
                hold(pool, passed, idx_ready, c + 1)
                pool.indirect_dma_start(out=seen[:, :], out_offset=None, in_=counts,
                                        in_offset=bass.IndirectOffsetOnAxis(ap=idx1[:, :], axis=0),
                                        bounds_check=NP * NP - 1, oob_is_err=False).then_inc(seen_in, 16)
                hold(pool, passed, ln_seen_done, c + 1)
                for to, value in ((counts, seen), (table, ln_seen)):
                    pool.indirect_dma_start(out=to, out_offset=bass.IndirectOffsetOnAxis(ap=idx1[:, :], axis=0),
                                            in_=value[:, :], in_offset=None,
                                            bounds_check=NP * NP - 1, oob_is_err=False).then_inc(written, 16)
                hold(pool, passed, written, (c + 1) * 32)
                pool.sem_inc(col_written, 1)

        @block.scalar
        def _(act):
            with act.Fori(0, ER) as c:
                act.wait_ge(seen_done, c + 1)
                act.activation(ln_seen[:, :], seen[:, :], ACT.Ln).then_inc(ln_seen_done, 1)

        @block.tensor
        def _(pe):
            with pe.Fori(0, ER) as c:
                pe.wait_ge(col_math, c * 7 + 2)
                pe.transpose(turned[:, :], spread[:, :], ident[:, :]).then_inc(turned_done, 1)

        @block.vector
        def _(dve):
            dve.wait_ge(set_up, 3)
            with dve.Fori(0, ER) as c:
                def step(n, ins):
                    ins.then_inc(col_math, 1)
                    dve.wait_ge(col_math, c * 7 + n)

                step(1, dve.tensor_copy(col[:, :], key[:, bass.ds(c + HALO, 1)]))
                step(2, dve.tensor_copy(spread[:, :], col[:, :].to_broadcast([P, P])))
                dve.wait_ge(turned_done, c + 1)
                step(3, dve.tensor_scalar(same[:, :], turned[:, :], col[:, :], None, ALU.is_equal))
                step(4, dve.tensor_tensor(same_low[:, :], same[:, :], below[:, :], ALU.mult))
                step(5, dve.tensor_reduce(times[:, :], same[:, :], AX_X, ALU.add))
                step(6, dve.tensor_reduce(first[:, :], same_low[:, :], AX_X, ALU.max))
                dve.wait_ge(col_written, c + 1)
                step(7, dve.scalar_tensor_tensor(out=skip1[:, :], in0=col[:, :], scalar=0.0, in1=first[:, :],
                                                 op0=ALU.is_lt, op1=ALU.max))
                dve.scalar_tensor_tensor(out=idx1[:, :], in0=skip1[:, :], scalar=OOB, in1=col[:, :],
                                         op0=ALU.mult, op1=ALU.add).then_inc(idx_ready, 1)
                dve.wait_ge(seen_in, (c + 1) * 16)
                dve.tensor_tensor(seen[:, :], seen[:, :], times[:, :], ALU.add).then_inc(seen_done, 1)


def phase2(nc, table2, arow_d, trow_d, agg_d, ident, xp, a_src, a_dst):
    CW = 400
    CH = NP // CW
    ITEMS = CH * GT
    STEPS = H * TILES
    VS = 4
    EARLY = 5
    first_looks = [c * (H - 1) * TILES // EARLY for c in range(EARLY)]
    first_looks += [(H - 1) * TILES + 1 + (c - EARLY) * (GT + 1) for c in range(EARLY, CH)]
    SPAN = first_looks[-1] + GT
    KEEP = 1
    FINISH, TURN, COPY = SPAN, SPAN + 1, SPAN + 2
    TM = 11
    assert VS >= H and CW <= GW and CH * CW == NP and ITEMS % 2 == 0 and STEPS % VS == 0 and COPY < STEPS - 1
    due = {}
    for item in range(ITEMS):
        c, dt = divmod(item, GT)
        due.setdefault(first_looks[c] + (dt * 3 if c < EARLY else dt), []).append(item)
    arow_v = arow_d.rearrange("(h t) p -> h (t p)", h=H)
    ctx = ExitStack()
    with ctx:
        def sb(name, shape, dt=F32):
            return ctx.enter_context(nc.sbuf_tensor(name, shape, dt))

        def sem(name):
            return ctx.enter_context(nc.semaphore(name))

        steep = sb("steep", [P, TILES * H])
        flat = sb("flat", [P, TILES * H])
        e_self = sb("e_self", [P, TILES * H])
        L = sb("L", [P, TILES, GW])
        t12 = [sb(f"t12_{k}", [P, 2, GW]) for k in range(2)]
        v = [sb(f"v{k}", [P, GW]) for k in range(VS)]
        blk = [sb(f"blk{k}", [P, GT, P]) for k in range(2)]
        bc = sb("bc", [P, H, CW])
        nat = [sb(f"nat{k}", [P, CW]) for k in range(2)]
        stage = sb("stage", [P, GT, CX])
        mpart = sb("mpart", [P, GT, H, CH])
        mx = sb("mx", [P, GT * H])
        ms = sb("ms", [P, GT * H])
        t1 = sb("t1", [P, GT * H])
        t2 = sb("t2", [P, GT * H])
        le = sb("le", [P, GT * H])
        trow = sb("trow", [P, 2, H, GT])
        trow_t = sb("trow_t", [2 * H * GT, P])
        junk_sb = sb("junk_sb", [P, CW], BF16)
        acc = [ctx.enter_context(nc.psum_tensor(f"acc{k}", [P, HALF], F32)) for k in range(GT)]
        lt = ctx.enter_context(nc.psum_tensor("lt", [P, 2 * HALF], F32))
        spare = ctx.enter_context(nc.psum_tensor("spare", [P, HALF], F32))
        junk = [spare[:, 0:CW], junk_sb[:, :]]

        scaled = sem("scaled")
        bc_in = sem("bc_in")
        bc2_in = [sem(f"bc2_in{k}") for k in range(2)]
        nat_in = [sem(f"nat_in{k}") for k in range(2)]
        maxed = sem("maxed")
        t_math = sem("t_math")
        t_turned = sem("t_turned")
        t_copied = sem("t_copied")
        t_out = sem("t_out")
        self_done = sem("self_done")
        t12_in = [sem(f"t12_in{k}") for k in range(2)]
        blk_in = [sem(f"blk_in{k}") for k in range(2)]
        L_turned = sem("L_turned")
        L_filled = sem("L_filled")
        raw_done = sem("raw_done")
        masked = sem("masked")
        w_ready = sem("w_ready")
        v_used = sem("v_used")
        acc_done = sem("acc_done")
        acc_free = sem("acc_free")
        agg_out = sem("agg_out")
        passed = sem("passed_phase2")
        block = ctx.enter_context(nc.Block())

        def a_src_chunk(c, h, first):
            return v[h][:, 0:CW] if first and c % 2 else bc[:, h, :]

        @block.sync
        def _(sp):
            def load_item(g, item, first=False):
                c, dt = divmod(item, GT)
                if dt == 0 and first:
                    if c >= 2:
                        hold(sp, passed, maxed, (item - GT) * H + H)
                    for h in range(H):
                        sp.dma_start(a_src_chunk(c, h, first),
                                     arow_v[h:h + 1, c * CW:(c + 1) * CW].to_broadcast([P, CW])).then_inc(bc2_in[c % 2], 16)
                elif dt == 0:
                    hold(sp, passed, maxed, (g * ITEMS + item) * H + H)
                    sp.dma_start(bc[:, :, :], arow_v[:, c * CW:(c + 1) * CW].rearrange("(o h) c -> o h c", o=1)
                                 .to_broadcast([P, H, CW])).then_inc(bc_in, 16)
                hold(sp, passed, maxed, (g * ITEMS + item) * H)
                sp.dma_start(nat[item % 2][:, :], table2[bass.ds(g * GW + dt * P, P), c * CW:(c + 1) * CW])\
                    .then_inc(nat_in[item % 2], 16)

            def store_sums(g, h):
                unit = g * H + h
                hold(sp, passed, acc_free, unit * GT + 2 * GT)
                sp.dma_start(agg_d[h, bass.ds(g * GW, GW), :].rearrange("(t p) c -> p t c", p=P),
                             stage[:, :, :]).then_inc(agg_out, 16)

            def load_terms(g, h, first=False):
                if not first:
                    hold(sp, passed, raw_done, g * STEPS + (h - 1) * TILES + 1)
                rows_g = trow_d[bass.ds(g * (2 * H * GT), 2 * H * GT), :]
                sp.dma_start(t12[h % 2][:, :, :],
                               rows_g.rearrange("(k h t) p -> h k (t p)", k=2, h=H)[h:h + 1, :, :]
                               .to_broadcast([P, 2, GW])).then_inc(t12_in[h % 2], 16)

            def store_terms(g):
                hold(sp, passed, t_copied, g + 1)
                sp.dma_start(trow_d[bass.ds(g * (2 * H * GT), 2 * H * GT), :], trow_t[:, :]).then_inc(t_out, 16)
                hold(sp, passed, t_out, g * 16 + 16)

            def group(g, ahead, first=False):
                for n in range(STEPS):
                    if n % TILES == 4 and n < (H - 1) * TILES:
                        load_terms(g, n // TILES + 1)
                    if ahead and n == COPY:
                        store_terms(g + 1)
                        load_terms(g + 1, 0)
                    if ahead:
                        for item in due.get(n, ()):
                            load_item(g + 1, item)
                    if n == KEEP + 6 and not first:
                        store_sums(g - 1, H - 1)
                    if n % TILES == KEEP + 6 and n > TILES:
                        store_sums(g, n // TILES - 1)

            sp.sem_inc(agg_out, 16)
            sp.sem_inc(maxed, H)
            for item in range(ITEMS):
                load_item(0, item, first=True)
            store_terms(0)
            load_terms(0, 0, first=True)
            group(0, True, first=True)
            with sp.Fori(1, G - 1) as g:
                group(g, True)
            group(G - 1, False)
            store_sums(G - 1, H - 1)
            sp.wait_ge(agg_out, 16 * G * H + 16)

        @block.gpsimd
        def _(pool):
            def load_block(g, s):
                hold(pool, passed, L_turned, g * TILES + max(s + 1, 2))
                pool.dma_start(blk[s % 2][:, :, :],
                               table2[bass.ds(g * GW, GW), s * P:(s + 1) * P].rearrange("(t p) c -> p t c", p=P))\
                    .then_inc(blk_in[s % 2], 16)

            pool.sem_inc(L_turned, 2)
            with pool.Fori(0, G) as g:
                for s in range(TILES):
                    load_block(g, s)

        @block.scalar
        def _(act):
            def weigh(g, n):
                h, s = divmod(n, TILES)
                act.wait_ge(masked, g * STEPS + n + 1)
                act.activation(v[n % VS][:, :], v[n % VS][:, :], ACT.Exp,
                               bias=flat[:, s * H + h:s * H + h + 1]).then_inc(w_ready, 1)

            def fill(g, s):
                act.wait_ge(L_turned, g * TILES + s + 3)
                act.activation(L[:, s, :], lt[:, 0:GW], ACT.Copy).then_inc(L_filled, 1)

            def copy_terms(g):
                act.wait_ge(t_turned, g + 1)
                act.wait_ge(t_out, g * 16)
                act.activation(trow_t[:, :], spare[0:2 * H * GT, 0:P], ACT.Copy).then_inc(t_copied, 1)
                act.activation(e_self[:, bass.ds(g * (GT * H), GT * H)], le[:, :], ACT.Exp).then_inc(self_done, 1)

            def group(g, ahead):
                for n in range(STEPS):
                    weigh(g, n)
                    if ahead and n >= STEPS - TILES + 2:
                        fill(g + 1, n - (STEPS - TILES + 2))
                    if ahead and n == COPY:
                        copy_terms(g + 1)
                if ahead:
                    fill(g + 1, TILES - 2)
                    fill(g + 1, TILES - 1)

            for s in range(TILES):
                fill(0, s)
            copy_terms(0)
            act.wait_ge(scaled, 2)
            with act.Fori(0, G - 1) as g:
                group(g, True)
            group(G - 1, False)

        @block.tensor
        def _(pe):
            def turn(g, s):
                ahead = g * 13 + s // 2 if s % 2 == 0 else g * 12 + s // 2
                pe.wait_ge(blk_in[s % 2], ahead * 16 + 16)
                pe.wait_ge(L_filled, g * TILES + s)
                for dt in range(GT):
                    last = pe.transpose(lt[:, dt * P:(dt + 1) * P], blk[s % 2][:, dt, :], ident[:, :])
                last.then_inc(L_turned, 1)

            def turn_terms(g):
                hold(pe, passed, t_math, g * TM + TM)
                pe.transpose(spare[0:2 * H * GT, 0:P], trow[:, :, :, :].rearrange("p k h t -> p (k h t)"),
                             ident[:, :]).then_inc(t_turned, 1)

            def add_up(g, n):
                h, s = divmod(n, TILES)
                pe.wait_ge(w_ready, g * STEPS + n + 1)
                for dt in range(GT):
                    if s == 0:
                        pe.wait_ge(acc_free, (g * H + h) * GT + dt + 1)
                    one = pe.matmul(acc[dt][:, 0:CX], v[n % VS][:, dt * P:(dt + 1) * P], xp[:, s, h, :],
                                    start=s == 0, stop=s == TILES - 1)
                    if dt == GT - 1:
                        one.then_inc(v_used, 1)
                    elif s == TILES - 1:
                        one.then_inc(acc_done, 1)

            def group(g, ahead):
                for n in range(STEPS):
                    add_up(g, n)
                    if ahead and n >= STEPS - TILES:
                        turn(g + 1, n - (STEPS - TILES))
                    if ahead and n == TURN:
                        turn_terms(g + 1)

            pe.sem_inc(acc_free, GT)
            for s in range(TILES):
                turn(0, s)
            turn_terms(0)
            with pe.Fori(0, G - 1) as g:
                group(g, True)
            group(G - 1, False)

        @block.vector
        def _(dve):
            def look(g, item, first=False):
                c, dt = divmod(item, GT)
                dve.wait_ge(nat_in[item % 2], (g * (ITEMS // 2) + item // 2 + 1) * 16)
                if dt == 0 and first:
                    dve.wait_ge(bc2_in[c % 2], (c // 2 + 1) * H * 16)
                elif dt == 0:
                    dve.wait_ge(bc_in, ((g - 1) * CH + c + 1) * 16)
                if item == 0:
                    dve.wait_ge(t_copied, g)
                    dve.wait_ge(t_math, g * TM)
                for h in range(H):
                    hold(dve, passed, maxed, (g * ITEMS + item) * H + h + H - 1)
                    dve.tensor_tensor_reduce(out=junk[h % 2], in0=nat[item % 2][:, :], in1=a_src_chunk(c, h, first),
                                             scale=1.0, scalar=NEG, op0=ALU.add, op1=ALU.max,
                                             accum_out=mpart[:, dt, h, c:c + 1]).then_inc(maxed, 1)

            def finish_terms(g):
                mine = bass.ds(g * (GT * H), GT * H)
                done = [0]

                def then(ins):
                    ins.then_inc(t_math, 1)
                    done[0] += 1
                    dve.wait_ge(t_math, g * TM + done[0])

                dve.wait_ge(maxed, (g + 1) * (ITEMS * H) + H)
                dve.wait_ge(t_turned, g)
                dve.wait_ge(self_done, g)
                then(dve.tensor_reduce(mx[:, :], mpart[:, :, :, :].rearrange("p t h c -> p (t h) c"), AX_X, ALU.max))
                then(dve.tensor_tensor(mx[:, :], mx[:, :], a_src[:, mine], ALU.max))
                then(dve.tensor_tensor(mx[:, :], mx[:, :], a_dst[:, mine], ALU.add))
                then(dve.scalar_tensor_tensor(out=ms[:, :], in0=mx[:, :], scalar=SLOPE0, in1=mx[:, :],
                                              op0=ALU.mult, op1=ALU.max))
                then(dve.tensor_tensor(t1[:, :], a_dst[:, mine], ms[:, :], ALU.subtract))
                then(dve.scalar_tensor_tensor(out=t2[:, :], in0=a_dst[:, mine], scalar=SLOPE0, in1=ms[:, :],
                                              op0=ALU.mult, op1=ALU.subtract))
                then(dve.tensor_tensor(le[:, :], t1[:, :], steep[:, mine], ALU.add))
                then(dve.tensor_tensor(le[:, :], le[:, :], t2[:, :], ALU.max))
                then(dve.tensor_tensor(le[:, :], le[:, :], flat[:, mine], ALU.add))
                for k, t in enumerate((t1, t2)):
                    then(dve.tensor_copy(trow[:, k, :, :], t[:, :].rearrange("p (t h) -> p h t", h=H)))

            def score(g, n):
                h, s = divmod(n, TILES)
                dve.wait_ge(v_used, g * STEPS + n + 1)
                if s == 0:
                    dve.wait_ge(t12_in[h % 2], (g * (H // 2) + h // 2 + 1) * 16)
                dve.scalar_tensor_tensor(out=v[n % VS][:, :], in0=t12[h % 2][:, 0, :],
                                         scalar=steep[:, s * H + h:s * H + h + 1], in1=t12[h % 2][:, 1, :],
                                         op0=ALU.add, op1=ALU.max).then_inc(raw_done, 1)

            def mask(g, n):
                h, s = divmod(n, TILES)
                dve.wait_ge(raw_done, g * STEPS + n + 2)
                if h == 0:
                    dve.wait_ge(L_filled, g * TILES + s + 1)
                dve.tensor_tensor(v[n % VS][:, :], v[n % VS][:, :], L[:, s, :], ALU.add).then_inc(masked, 1)

            def keep_sums(g, h):
                unit = g * H + h
                dve.wait_ge(agg_out, unit * 16 + 16)
                dve.wait_ge(self_done, g + 1)
                for dt in range(GT):
                    if dt < GT - 1:
                        dve.wait_ge(acc_done, unit * (GT - 1) + dt + 1)
                    else:
                        dve.wait_ge(v_used, unit * TILES + TILES + VS)
                    dve.scalar_tensor_tensor(out=stage[:, dt, :], in0=xp[:, g * GT + dt, h, :],
                                             scalar=e_self[:, bass.ds(g * (GT * H) + dt * H + h, 1)],
                                             in1=acc[dt][:, 0:CX], op0=ALU.mult, op1=ALU.add).then_inc(acc_free, 1)

            def group(g, ahead, first=False):
                for n in range(STEPS):
                    if n < STEPS - 1:
                        score(g, n + 1)
                    elif ahead:
                        score(g + 1, 0)
                    mask(g, n)
                    if n == KEEP and not first:
                        keep_sums(g - 1, H - 1)
                    if n % TILES == KEEP and n > TILES:
                        keep_sums(g, n // TILES - 1)
                    if ahead:
                        for item in due.get(n, ()):
                            look(g + 1, item)
                        if n == FINISH:
                            finish_terms(g + 1)

            dve.sem_inc(v_used, VS)
            dve.sem_inc(raw_done, 1)
            dve.tensor_scalar(steep[:, :], a_src[:, :], 1.0 - SLOPE0, None, ALU.mult).then_inc(scaled, 1)
            dve.tensor_scalar(flat[:, :], a_src[:, :], SLOPE0, None, ALU.mult).then_inc(scaled, 1)
            dve.wait_ge(scaled, 2)
            for item in range(ITEMS):
                look(0, item, first=True)
            finish_terms(0)
            score(0, 0)
            group(0, True, first=True)
            with dve.Fori(1, G - 1) as g:
                group(g, True)
            group(G - 1, False)
            keep_sums(G - 1, H - 1)


def phase3(nc, x, bias, w1, a1, agg_d, x1_d, alrow_d, low_d, ident, h2, al, ar):
    HC = KC // 2
    ctx = ExitStack()
    with ctx:
        def sb(name, shape, dt=F32):
            return ctx.enter_context(nc.sbuf_tensor(name, shape, dt))

        def sem(name):
            return ctx.enter_context(nc.semaphore(name))

        w_high = sb("w1_high", [P, KC, D], F32R)
        w_low = sb("w1_low", [P, KC, D], F32R)
        bias_bc = sb("bias_bc", [P, D])
        a_bc = sb("a_bc", [P, 2, D])
        xt = [sb(f"x1t{k}", [P, D]) for k in range(2)]
        sums = sb("sums", [P, H, CX])
        ht = sb("h1t", [P, D])
        hT_high = sb("h1T_high", [P, KC, P], F32R)
        hT_low = sb("h1T_low", [P, KC, P], F32R)
        low = sb("low", [P, D])
        rz = sb("rz", [P, H])
        stats = sb("stats1", [P, 2, 6])
        mv = sb("mv1", [P, 2])
        std = sb("std1", [P, 1])
        rstd = sb("rstd1", [P, 1])
        nbias = sb("nbias1", [P, 1])
        alr = [sb(f"alr{k}", [P, 2]) for k in range(2)]
        al_rows = sb("al_rows_sb", [TILES, P])
        eps = sb("eps1", [P, 1])
        tp = [ctx.enter_context(nc.psum_tensor(f"tp1_{k}", [P, KC * P], F32)) for k in range(2)]
        mm = [ctx.enter_context(nc.psum_tensor(f"mmb{k}", [P, D], F32)) for k in range(2)]
        landing = [a_bc[:, 0, :], a_bc[:, 1, :], low[:, :]]

        bias_in = sem("bias_in")
        w_in = [sem(f"w1_in{k}") for k in range(len(landing))]
        w_rounded = sem("w1_rounded")
        w_split = sem("w1_split")
        a_in = sem("a_in")
        x_in = [sem(f"xb_in{k}") for k in range(2)]
        sums_in = sem("sums_in")
        x1_done = sem("x1_done")
        x1_out = [sem(f"x1_out{k}") for k in range(2)]
        eps_set = sem("eps_set")
        rz_done = sem("rz_done")
        y_done = sem("y_done")
        stats_done = sem("stats1_done")
        aggr_done = sem("aggr1_done")
        std_done = sem("std1_done")
        rstd_done = sem("rstd1_done")
        norm_done = sem("norm1_done")
        h_done = sem("h1_done")
        transposed = sem("transposed1")
        hT_rounded = sem("hT1_rounded")
        hT_split = sem("hT1_split")
        half_done = sem("half_done")
        h2_copied = sem("h2_copied")
        scored = sem("scored1")
        scores_kept = sem("scores1_kept")
        low_done = sem("low_done")
        low_out = sem("low_out")
        al_turned = sem("al_turned")
        al_copied = sem("al_copied")
        al_out = sem("al_out")
        passed = sem("passed_phase3")
        block = ctx.enter_context(nc.Block())

        @block.sync
        def _(sp):
            def load_x(i, k, rounds, size=P):
                hold(sp, passed, h_done, i + 1)
                hold(sp, passed, x1_out[k], rounds * 16)
                sp.dma_start(xt[k][0:size, :], rows(x, i, size)).then_inc(x_in[k], 16)

            def load_sums(i):
                hold(sp, passed, x1_done, i)
                sp.dma_start(sums[:, :, :], agg_d[:, bass.ds(i * P, P), :].rearrange("h p c -> p h c"))\
                    .then_inc(sums_in, 16)

            def store(i, k):
                hold(sp, passed, x1_done, i + 1)
                sp.dma_start(rows(x1_d, i), xt[k][:, :]).then_inc(x1_out[k], 16)

            def load_w(c):
                if c >= len(landing):
                    hold(sp, passed, w_split, c - len(landing) + 1)
                sp.dma_start(landing[c % len(landing)], w1[c * P:(c + 1) * P, :]).then_inc(w_in[c % len(landing)], 16)

            sp.sem_inc(h_done, 2)
            load_sums(0)
            load_x(0, 0, 0)
            sp.dma_start(bias_bc[:, :], bias.rearrange("(o n) -> o n", o=1).to_broadcast([P, D]))\
                .then_inc(bias_in, 16)
            for c in range(len(landing)):
                load_w(c)
            load_x(1, 1, 0)
            load_sums(1)
            for c in range(len(landing), KC):
                load_w(c)
            hold(sp, passed, w_split, KC)
            sp.dma_start(a_bc[:, :, :].rearrange("p k n -> p (k n)"), a1.to_broadcast([P, 2 * D])).then_inc(a_in, 16)
            with sp.Fori(0, TILES // 2 - 1) as r:
                for k in range(2):
                    store(r * 2 + k, k)
                    load_x(r * 2 + k + 2, k, r + 1)
                    load_sums(r * 2 + k + 2)
            store(TILES - 3, 0)
            load_x(TILES - 1, 0, TILES // 2, TAIL)
            load_sums(TILES - 1)
            store(TILES - 2, 1)
            store(TILES - 1, 0)
            for k in range(2):
                sp.wait_ge(x1_out[k], 16 * (TILES // 2 + 1 - k))
            sp.wait_ge(al_copied, 1)
            sp.dma_start(alrow_d, al_rows[:, :]).then_inc(al_out, 16)
            sp.wait_ge(al_out, 16)

        @block.gpsimd
        def _(pool):
            with pool.Fori(0, TILES) as i:
                hold(pool, passed, low_done, i + 3)
                pool.dma_start(rows(low_d, i), low[:, :]).then_inc(low_out, 16)
            pool.wait_ge(low_out, 16 * TILES)

        @block.scalar
        def _(act):
            def normalise(i, k):
                act.wait_ge(aggr_done, i + 1)
                act.activation(std[:, :], mv[:, 1:2], ACT.Sqrt, bias=eps[:, :]).then_inc(std_done, 1)
                act.wait_ge(norm_done, i + 1)
                act.wait_ge(transposed, i)
                act.activation(ht[:, :], xt[k][:, :], ACT.Relu, bias=nbias[:, :], scale=rstd[:, :])\
                    .then_inc(h_done, 1)

            def round_half(i, k, a, first=False):
                act.wait_ge(transposed, i + 1)
                if not first:
                    act.wait_ge(half_done, 2 * i + a - 1)
                act.activation(hT_high[:, a * HC:(a + 1) * HC, :].rearrange("p k n -> p (k n)"),
                               tp[k][:, a * HALF:(a + 1) * HALF], ACT.Copy).then_inc(hT_rounded, 1)

            def keep_h2(i, k):
                act.wait_ge(half_done, 2 * i + 2)
                act.activation(h2[:, bass.ds(i * D, D)], mm[k][:, :], ACT.Copy).then_inc(h2_copied, 1)

            act.wait_ge(eps_set, 1)
            normalise(0, 0)
            for c in range(KC):
                act.wait_ge(w_in[c % len(landing)], 16 * (c // len(landing) + 1))
                act.activation(w_high[:, c, :], landing[c % len(landing)], ACT.Copy).then_inc(w_rounded, 1)
            round_half(0, 0, 0, first=True)
            round_half(0, 0, 1, first=True)
            normalise(1, 1)
            with act.Fori(0, TILES // 2 - 1) as r:
                i = r * 2
                for k in range(2):
                    round_half(i + k + 1, 1 - k, 0)
                    normalise(i + k + 2, k)
                    round_half(i + k + 1, 1 - k, 1)
                    keep_h2(i + k, k)
            round_half(TILES - 2, 1, 0)
            normalise(TILES - 1, 0)
            round_half(TILES - 2, 1, 1)
            keep_h2(TILES - 3, 0)
            round_half(TILES - 1, 0, 0)
            round_half(TILES - 1, 0, 1)
            keep_h2(TILES - 2, 1)
            keep_h2(TILES - 1, 0)
            act.wait_ge(al_turned, 1)
            act.activation(al_rows[:, :], tp[0][0:TILES, 0:P], ACT.Copy).then_inc(al_copied, 1)

        @block.vector
        def _(dve):
            def finish_layer(i, k, rounds):
                dve.wait_ge(sums_in, i * 16 + 16)
                dve.wait_ge(y_done, i * H)
                dve.reciprocal(rz[:, :], sums[:, :, C:CX].rearrange("p h c -> p (h c)")).then_inc(rz_done, 1)
                dve.wait_ge(rz_done, i + 1)
                for h in range(H):
                    dve.scalar_tensor_tensor(out=sums[:, h, 0:C], in0=sums[:, h, 0:C],
                                             scalar=rz[:, h:h + 1], in1=bias_bc[:, h * C:(h + 1) * C],
                                             op0=ALU.mult, op1=ALU.add).then_inc(y_done, 1)
                dve.wait_ge(x_in[k], rounds * 16)
                dve.wait_ge(y_done, i * H + H)
                x_heads = xt[k][:, :].rearrange("p (h c) -> p h c", h=H)
                dve.scalar_tensor_tensor(out=x_heads, in0=sums[:, :, 0:C], scalar=0.0, in1=x_heads,
                                         op0=ALU.max, op1=ALU.add).then_inc(x1_done, 1)
                dve.wait_ge(x1_done, i + 1)

            def statistics(i, k):
                for j in range(2):
                    dve.bn_stats(stats[:, j, :], xt[k][:, j * HALF:(j + 1) * HALF]).then_inc(stats_done, 1)
                hold(dve, passed, stats_done, 2 * i + 2)
                dve.bn_aggr(mv[:, :], stats[:, :, :].rearrange("p a b -> p (a b)")).then_inc(aggr_done, 1)
                dve.wait_ge(std_done, i + 1)
                dve.reciprocal(rstd[:, :], std[:, :]).then_inc(rstd_done, 1)
                dve.wait_ge(rstd_done, i + 1)
                dve.scalar_tensor_tensor(out=nbias[:, :], in0=mv[:, 0:1], scalar=-1.0, in1=rstd[:, :],
                                         op0=ALU.mult, op1=ALU.mult).then_inc(norm_done, 1)

            def split_half(i, k, a):
                dve.wait_ge(hT_rounded, 2 * i + a + 1)
                cols = slice(a * HC, (a + 1) * HC)
                dve.tensor_tensor(hT_low[:, cols, :].rearrange("p k n -> p (k n)"),
                                  tp[k][:, a * HALF:(a + 1) * HALF],
                                  hT_high[:, cols, :].bitcast(F32).rearrange("p k n -> p (k n)"),
                                  ALU.subtract).then_inc(hT_split, 1)

            def score(i, k, first=False):
                dve.wait_ge(h2_copied, i + 1)
                if not first:
                    dve.wait_ge(low_out, i * 16)
                for j in range(2):
                    if j == 1:
                        dve.wait_ge(scored, i * 2 + j)
                    dve.tensor_tensor_reduce(out=low[:, :], in0=mm[k][:, :], in1=a_bc[:, j, :], scale=1.0,
                                             scalar=0.0, op0=ALU.mult, op1=ALU.add,
                                             accum_out=alr[k][:, j:j + 1]).then_inc(scored, 1)
                dve.wait_ge(scored, i * 2 + 2)
                dve.tensor_tensor(low[:, :], mm[k][:, :], h2[:, bass.ds(i * D, D)].bitcast(F32), ALU.subtract)\
                    .then_inc(low_done, 1)
                dve.tensor_copy(al[:, bass.ds(i, 1)], alr[k][:, 0:1]).then_inc(scores_kept, 1)
                dve.tensor_copy(ar[:, bass.ds(i, 1)], alr[k][:, 1:2]).then_inc(scores_kept, 1)
                dve.wait_ge(scores_kept, 2 * i + 2)

            dve.memset(eps[:, :], LN_EPS).then_inc(eps_set, 1)
            dve.wait_ge(bias_in, 16)
            finish_layer(0, 0, 1)
            statistics(0, 0)
            for c in range(KC):
                dve.wait_ge(w_rounded, c + 1)
                dve.tensor_tensor(w_low[:, c, :], landing[c % len(landing)], w_high[:, c, :].bitcast(F32),
                                  ALU.subtract).then_inc(w_split, 1)
            split_half(0, 0, 0)
            split_half(0, 0, 1)
            dve.wait_ge(h_done, 3)
            finish_layer(1, 1, 1)
            statistics(1, 1)
            dve.wait_ge(h_done, 4)
            dve.wait_ge(w_split, KC)
            dve.wait_ge(a_in, 16)

            def tile(i, k, rounds, first=False):
                split_half(i + 1, 1 - k, 0)
                finish_layer(i + 2, k, rounds)
                statistics(i + 2, k)
                split_half(i + 1, 1 - k, 1)
                dve.wait_ge(h_done, i + 5)
                score(i, k, first)

            tile(0, 0, 2, first=True)
            tile(1, 1, 2)
            with dve.Fori(1, TILES // 2 - 1) as r:
                for k in range(2):
                    tile(r * 2 + k, k, r + 2)
            tile(TILES - 3, 0, TILES // 2 + 1)
            split_half(TILES - 1, 0, 0)
            split_half(TILES - 1, 0, 1)
            score(TILES - 2, 1)
            score(TILES - 1, 0)

        @block.tensor
        def _(pe):
            def transpose_h(i, k):
                pe.wait_ge(h_done, i + 3)
                pe.wait_ge(hT_split, 2 * i)
                for c in range(KC):
                    last = pe.transpose(tp[k][:, c * P:(c + 1) * P], ht[:, c * P:(c + 1) * P], ident[:, :])
                last.then_inc(transposed, 1)

            def project_half(i, k, a):
                pe.wait_ge(hT_split, 2 * i + a + 3)
                if a == 0:
                    pe.wait_ge(low_done, i + 1)
                for c in range(a * HC, (a + 1) * HC):
                    for f in range(2):
                        cols = slice(f * HALF, (f + 1) * HALF)
                        pe.matmul(mm[k][:, cols], hT_high[:, c, :], w_high[:, c, cols], start=c == 0, stop=False)
                        pe.matmul(mm[k][:, cols], hT_high[:, c, :], w_low[:, c, cols], start=False, stop=False)
                        last = pe.matmul(mm[k][:, cols], hT_low[:, c, :], w_high[:, c, cols],
                                         start=False, stop=c == KC - 1)
                last.then_inc(half_done, 1)

            pe.sem_inc(low_done, 2)
            pe.sem_inc(hT_split, 2)
            transpose_h(0, 0)
            pe.wait_ge(w_split, KC)
            with pe.Fori(0, TILES // 2) as r:
                i = r * 2
                for k in range(2):
                    project_half(i + k, k, 0)
                    transpose_h(i + k + 1, 1 - k)
                    project_half(i + k, k, 1)
            project_half(TILES - 1, 0, 0)
            project_half(TILES - 1, 0, 1)
            pe.wait_ge(scores_kept, 2 * TILES)
            pe.transpose(tp[0][0:TILES, 0:P], al[:, :], ident[:, :]).then_inc(al_turned, 1)


def phase4(nc, table2, alrow_d, x1_d, low_d, ident, h2, ar, out):
    STEPS = 2 * TILES
    WS = 5
    LAG = 2
    KEEP, EXP, FINISH = WS, WS + 2, WS + 3
    PAIRS = 2
    RS = 3
    assert STEPS % WS == 0 and STEPS % 2 == 0
    ctx = ExitStack()
    with ctx:
        def sb(name, shape, dt=F32):
            return ctx.enter_context(nc.sbuf_tensor(name, shape, dt))

        def sem(name):
            return ctx.enter_context(nc.semaphore(name))

        neg_al = sb("neg_al", [P, NP])
        neg_flat = sb("neg_flat", [P, NP])
        steep_ar = sb("steep_ar", [P, TILES])
        flat_ar = sb("flat_ar", [P, TILES])
        w = [sb(f"w{k}", [P, GW]) for k in range(WS)]
        w_high = [sb(f"w_high{k}", [P, GW], F32R) for k in range(WS)]
        w_low = [sb(f"w_low{k}", [P, GW], F32R) for k in range(WS)]
        h2_low = [sb(f"h2_low{k}", [P, HALF], F32R) for k in range(WS)]
        raw = [sb(f"raw{k}", [P, GW]) for k in range(2)]
        w_sum = sb("w_sum", [P, GW])
        ones = sb("ones", [P, 1])
        total = sb("total", [P, GT])
        rs = sb("rs", [P, GT])
        neg_rs = sb("neg_rs", [P, GT])
        plus = [sb(f"plus{k}", [P, HALF]) for k in range(2)]
        minus = sb("minus", [P, GT, HALF])
        y = sb("yo", [P, GT, HALF])
        acc = [ctx.enter_context(nc.psum_tensor(f"accb{k}", [P, HALF], F32)) for k in range(GT)]
        acc1 = [ctx.enter_context(nc.psum_tensor(f"accc{k}", [P, HALF], F32)) for k in range(PAIRS)]
        banks = (acc, acc1 + acc[PAIRS:])
        rs_ps = ctx.enter_context(nc.psum_tensor("rs_ps", [P, HALF], F32))

        al_in = sem("al_in")
        consts = sem("consts4")
        L_in = [sem(f"L_in{k}") for k in range(WS)]
        low_in = [sem(f"low_in{k}") for k in range(WS)]
        raw_done = sem("raw4_done")
        masked = sem("masked4")
        w_ready = sem("w4_ready")
        w_summed = sem("w_summed")
        rounded = sem("rounded")
        split = sem("split")
        w_used = sem("w_used")
        acc_done = sem("acc4_done")
        total_done = sem("total_done")
        rs_math = sem("rs_math")
        minus_done = sem("minus_done")
        plus_done = sem("plus_done")
        plus_used = sem("plus_used")
        e_done = sem("e_done")
        x1_in = sem("x1_in")
        y_done = sem("yo_done")
        y_out = sem("y_out")
        passed = sem("passed_phase4")
        block = ctx.enter_context(nc.Block())

        @block.sync
        def _(sp):
            def load_L(g, n):
                dt = n % TILES
                hold(sp, passed, split, g * STEPS + n + 1)
                if WS <= n < TILES + WS:
                    hold(sp, passed, w_summed, g * TILES + n - WS + 1)
                sp.dma_start(w[n % WS][:, :], table2[dt * P:(dt + 1) * P, bass.ds(g * GW, GW)])\
                    .then_inc(L_in[n % WS], 16)

            def load_x1(g, f, last=False):
                hold(sp, passed, y_out, (g * 2 + f) * 16 + (32 if last and f == 1 else 16))
                sp.dma_start(y[:, :, :], x1_d[bass.ds(g * GW, GW), f * HALF:(f + 1) * HALF]
                             .rearrange("(t p) c -> p t c", p=P)).then_inc(x1_in, 16)

            def store(g, f, last=False):
                hold(sp, passed, y_done, g * 2 + f + 1)
                cols = slice(f * HALF, (f + 1) * HALF)
                whole = GT - 1 if last else GT
                sp.dma_start(out[bass.ds(g * GW, whole * P), cols].rearrange("(t p) c -> p t c", p=P),
                             y[:, 0:whole, :]).then_inc(y_out, 16)
                if last:
                    sp.dma_start(out[N - TAIL:N, cols], y[0:TAIL, GT - 1, :]).then_inc(y_out, 16)

            def group(g, first=False, last=False):
                for n in range(STEPS):
                    load_L(g, n)
                    if n == TILES // 2 and not first:
                        store(g - 1, 1)
                    if n == TILES // 2 + 4:
                        load_x1(g, 0)
                    if n == TILES + TILES // 2:
                        store(g, 0, last)
                    if n == TILES + TILES // 2 + 4:
                        load_x1(g, 1, last)

            sp.sem_inc(split, WS)
            sp.sem_inc(y_out, 16)
            sp.dma_start(neg_al[:, :], alrow_d.rearrange("t p -> (t p)").rearrange("(o n) -> o n", o=1)
                         .to_broadcast([P, NP])).then_inc(al_in, 16)
            group(0, first=True)
            with sp.Fori(1, G - 1) as g:
                group(g)
            group(G - 1, last=True)
            store(G - 1, 1, last=True)
            sp.wait_ge(y_out, 16 + 16 * (2 * G + 2))

        @block.gpsimd
        def _(pool):
            with pool.Fori(0, G) as g:
                for n in range(STEPS):
                    f, dt = divmod(n, TILES)
                    hold(pool, passed, w_used, g * STEPS + n + 1)
                    pool.dma_start(h2_low[n % WS][:, :], low_d[dt * P:(dt + 1) * P, f * HALF:(f + 1) * HALF])\
                        .then_inc(low_in[n % WS], 16)

        @block.scalar
        def _(act):
            def weigh(g, n):
                dt = n % TILES
                act.wait_ge(masked, g * STEPS + n + 3)
                act.activation(w[n % WS][:, :], w[n % WS][:, :], ACT.Exp, bias=flat_ar[:, dt:dt + 1])\
                    .then_inc(w_ready, 1)

            def round_weights(g, n):
                act.wait_ge(w_ready, g * STEPS + n + 1)
                act.wait_ge(w_used, g * STEPS + n + 1)
                act.activation(w_high[n % WS][:, :], w[n % WS][:, :], ACT.Copy).then_inc(rounded, 1)

            def keep(g, f):
                unit = g * 2 + f
                act.wait_ge(rs_math, g * RS + RS + 1)
                act.wait_ge(y_done, unit)
                for st in range(GT):
                    if st < GT - 1:
                        act.wait_ge(acc_done, unit * (GT - 1) + st + 1)
                    else:
                        act.wait_ge(w_used, unit * TILES + TILES + WS)
                    bank = banks[f][st]
                    act.activation(minus[:, st, :], bank[:, :], ACT.Relu, scale=neg_rs[:, st:st + 1])\
                        .then_inc(minus_done, 1)
                    act.wait_ge(plus_used, unit * GT + st + 1)
                    act.activation(plus[(f * GT + st) % 2][:, :], bank[:, :], ACT.Relu, scale=rs[:, st:st + 1])\
                        .then_inc(plus_done, 1)

            def exp_minus(unit):
                act.wait_ge(minus_done, unit * GT + GT)
                act.activation(minus[:, :, :], minus[:, :, :], ACT.Exp, scale=-1.0).then_inc(e_done, 1)

            def group(g, first=False):
                for n in range(STEPS):
                    weigh(g, n)
                    if n == TILES + KEEP:
                        keep(g, 0)
                    if n == KEEP and not first:
                        keep(g - 1, 1)
                    if n > 0 or not first:
                        round_weights(g, n - 1)
                    if n == EXP and not first:
                        exp_minus(g * 2 - 1)
                    if n == TILES + EXP:
                        exp_minus(g * 2)

            act.sem_inc(plus_used, 2)
            act.wait_ge(consts, 5)
            group(0, first=True)
            with act.Fori(1, G) as g:
                group(g)
            round_weights(G - 1, STEPS - 1)
            keep(G - 1, 1)
            exp_minus(2 * G - 1)

        @block.vector
        def _(dve):
            def score(g, n):
                dt = n % TILES
                cols = bass.ds(g * GW, GW)
                dve.wait_ge(masked, g * STEPS + n + 1)
                dve.scalar_tensor_tensor(out=raw[n % 2][:, :], in0=neg_al[:, cols], scalar=steep_ar[:, dt:dt + 1],
                                         in1=neg_flat[:, cols], op0=ALU.add, op1=ALU.min).then_inc(raw_done, 1)

            def mask(g, n):
                dve.wait_ge(raw_done, g * STEPS + n + 1)
                dve.wait_ge(L_in[n % WS], (g * (STEPS // WS) + n // WS + 1) * 16)
                dve.tensor_tensor(w[n % WS][:, :], w[n % WS][:, :], raw[n % 2][:, :], ALU.add).then_inc(masked, 1)

            def sum_weights(g, n):
                dve.wait_ge(w_ready, g * STEPS + n + 1)
                if n == 0:
                    dve.wait_ge(total_done, g)
                    dve.tensor_copy(w_sum[:, :], w[0][:, :]).then_inc(w_summed, 1)
                else:
                    dve.wait_ge(w_summed, g * TILES + n)
                    dve.tensor_tensor(w_sum[:, :], w_sum[:, :], w[n % WS][:, :], ALU.add).then_inc(w_summed, 1)

            def split_weights(g, n):
                dve.wait_ge(rounded, g * STEPS + n + 1)
                dve.tensor_tensor(w_low[n % WS][:, :], w[n % WS][:, :], w_high[n % WS][:, :].bitcast(F32),
                                  ALU.subtract).then_inc(split, 1)

            def invert_total(g):
                dve.wait_ge(total_done, g + 1)
                dve.wait_ge(plus_done, g * 2 * GT + 2 * GT)
                dve.tensor_scalar(total[:, :], rs_ps[:, 0:GT], SUM_EPS, None, ALU.add).then_inc(rs_math, 1)
                dve.wait_ge(rs_math, g * RS + 2)
                dve.reciprocal(rs[:, :], total[:, :]).then_inc(rs_math, 1)
                dve.wait_ge(rs_math, g * RS + 3)
                dve.tensor_scalar(neg_rs[:, :], rs[:, :], -1.0, None, ALU.mult).then_inc(rs_math, 1)

            def add_plus(unit, f):
                dve.wait_ge(x1_in, unit * 16 + 16)
                for st in range(GT):
                    dve.wait_ge(plus_done, unit * GT + st + 1 + 2 * GT)
                    dve.tensor_tensor(y[:, st, :], y[:, st, :], plus[(f * GT + st) % 2][:, :], ALU.add)\
                        .then_inc(plus_used, 1)

            def finish(unit):
                dve.wait_ge(e_done, unit + 1)
                dve.wait_ge(plus_used, unit * GT + GT + 2)
                dve.scalar_tensor_tensor(out=y[:, :, :], in0=minus[:, :, :], scalar=-1.0, in1=y[:, :, :],
                                         op0=ALU.add, op1=ALU.add).then_inc(y_done, 1)

            def group(g, first=False):
                score(g, 0)
                for n in range(STEPS):
                    if n < STEPS - 1:
                        score(g, n + 1)
                    mask(g, n)
                    if LAG <= n < TILES + LAG:
                        sum_weights(g, n - LAG)
                    if n >= LAG or not first:
                        split_weights(g, n - LAG)
                    if n == TILES + KEEP:
                        invert_total(g)
                        add_plus(g * 2, 0)
                    if n == TILES + FINISH:
                        finish(g * 2)
                    if n == KEEP and not first:
                        add_plus(g * 2 - 1, 1)
                    if n == FINISH and not first:
                        finish(g * 2 - 1)

            dve.sem_inc(masked, 2)
            dve.sem_inc(rs_math, 1)
            dve.memset(ones[:, :], 1.0).then_inc(consts, 1)
            dve.tensor_scalar(steep_ar[:, :], ar[:, :], SLOPE1 - 1.0, None, ALU.mult).then_inc(consts, 1)
            dve.tensor_scalar(flat_ar[:, :], ar[:, :], -SLOPE1, None, ALU.mult).then_inc(consts, 1)
            dve.wait_ge(al_in, 16)
            dve.tensor_scalar(neg_flat[:, :], neg_al[:, :], -SLOPE1, None, ALU.mult).then_inc(consts, 1)
            dve.wait_ge(consts, 4)
            dve.tensor_scalar(neg_al[:, :], neg_al[:, :], -1.0, None, ALU.mult).then_inc(consts, 1)
            dve.wait_ge(consts, 5)
            group(0, first=True)
            with dve.Fori(1, G) as g:
                group(g)
            for n in range(STEPS - LAG, STEPS):
                split_weights(G - 1, n)
            add_plus(2 * G - 1, 1)
            finish(2 * G - 1)

        @block.tensor
        def _(pe):
            def add_up(g, n):
                f, dt = divmod(n, TILES)
                pe.wait_ge(split, g * STEPS + n + 1 + WS)
                pe.wait_ge(low_in[n % WS], (g * (STEPS // WS) + n // WS + 1) * 16)
                cols = slice(dt * D + f * HALF, dt * D + (f + 1) * HALF)
                for st in range(GT):
                    if dt == 0:
                        pe.wait_ge(plus_done, (g * 2 + f) * GT + st + 1 + (0 if st < PAIRS else GT))
                    bank = banks[f][st]
                    mine = slice(st * P, (st + 1) * P)
                    pe.matmul(bank[:, :], w_high[n % WS][:, mine], h2[:, cols], start=dt == 0, stop=False)
                    pe.matmul(bank[:, :], w_high[n % WS][:, mine], h2_low[n % WS][:, :], start=False, stop=False)
                    one = pe.matmul(bank[:, :], w_low[n % WS][:, mine], h2[:, cols],
                                    start=False, stop=dt == TILES - 1)
                    if st == GT - 1:
                        one.then_inc(w_used, 1)
                    elif dt == TILES - 1:
                        one.then_inc(acc_done, 1)

            def sum_total(g):
                pe.wait_ge(w_summed, g * TILES + TILES)
                pe.wait_ge(rs_math, g * RS + 1)
                for st in range(GT):
                    one = pe.matmul(rs_ps[:, st:st + 1], w_sum[:, st * P:(st + 1) * P], ones[:, :],
                                    start=True, stop=True)
                one.then_inc(total_done, 1)

            def group(g):
                for n in range(STEPS):
                    if n == TILES - 1:
                        sum_total(g)
                    add_up(g, n)

            pe.sem_inc(plus_done, 2 * GT)
            pe.sem_inc(w_used, WS)
            pe.wait_ge(consts, 5)
            with pe.Fori(0, G) as g:
                group(g)


_INS = ["x", "src", "dst", "L0_gnn_W", "L0_gnn_att_src", "L0_gnn_att_dst", "L0_gnn_bias",
        "L1_gnn_W", "L1_gnn_a"]


def kernel(**inputs):
    import numpy as _np
    import concourse.bacc as _bacc
    from concourse import mybir as _mybir
    from concourse.bass_utils import run_bass_kernel_spmd as _run

    nc = _bacc.Bacc("TRN2", target_bir_lowering=False, num_devices=1)
    arrays, args = {}, []
    for name in _INS:
        a = _np.ascontiguousarray(inputs[name])
        arrays[f"in_{name}_dram"] = a
        args.append(nc.dram_tensor(f"in_{name}_dram", a.shape, _mybir.dt.from_np(a.dtype), kind="ExternalInput").ap())
    out = nc.dram_tensor("out_0_dram", (N, D), _mybir.dt.float32, kind="ExternalOutput").ap()
    build(nc, *args, out)
    r = _run(nc, [arrays], core_ids=[0])
    return r.results[0]["out_0_dram"]
```
